# Optimizing a Trainium2 kernel written in Bass

```python
import numpy as np
import jax
import jax.numpy as jnp

def _softmax(x, axis=-1):
    return jax.nn.softmax(x, axis=axis)

def _gelu(x):
    return jax.nn.gelu(x, approximate=True)

def _silu(x):
    return jax.nn.silu(x)

def _sigmoid(x):
    return jax.nn.sigmoid(x)

def _layernorm(x, axis=-1, eps=1e-05):
    m = jnp.mean(x, axis=axis, keepdims=True)
    v = jnp.var(x, axis=axis, keepdims=True)
    return (x - m) / jnp.sqrt(v + eps)

def _scatter_add(tgt, idx, src, axis=0):
    return tgt.at[idx].add(src)

def _segment_sum(src, seg, n):
    return jax.ops.segment_sum(src, seg, n)
kernel_name = 'mk_gnn_resnorm_d4_gnn_r32_f951f2'

def setup_inputs(seed: int=0):
    np.random.seed(seed)
    _w = jnp.asarray

    def _rec_inputs():
        import jax
        import jax.numpy as jnp
        _gk = jax.random.key(seed)
        x = -0.000202 + 1 * jax.random.normal(jax.random.fold_in(_gk, 1), (50000, 128), jnp.float32)
        src = jax.random.randint(jax.random.fold_in(_gk, 2), (50000,), 0, 50000, jnp.int32)
        dst = jnp.minimum((50000 * jax.random.uniform(jax.random.fold_in(_gk, 3), (50000,)) ** 2.0).astype(jnp.int32), 49999)
        _o = jnp.argsort(dst, stable=True)
        src = src[_o]
        dst = dst[_o]
        edge_attr_2 = 0.000126197 + 0.999763 * jax.random.normal(jax.random.fold_in(_gk, 12), (50000, 2), jnp.float32)
        edge_attr_64 = 0.000189758 + 1.00013 * jax.random.normal(jax.random.fold_in(_gk, 13), (50000, 64), jnp.float32)
        return (x, src, dst, edge_attr_2, edge_attr_64)
    x, src, dst, edge_attr_2, edge_attr_64 = _rec_inputs()

    def _L0_gnn_setup():
        import jax, jax.numpy as jnp
        import numpy as np
        N_NODES = 50000
        N_EDGES = 25000
        D = 128
        key = jax.random.key(seed)
        k1, k2, k3, k4, k5 = jax.random.split(key, 5)
        h = jax.random.normal(k1, (N_NODES, D), dtype=jnp.float32)
        W = jax.random.normal(k2, (D, D), dtype=jnp.float32) * 0.05
        b = jax.random.normal(k3, (D,), dtype=jnp.float32) * 0.05
        src = jax.random.randint(k4, (N_EDGES,), 0, N_NODES, dtype=jnp.int64)
        dst = jax.random.randint(k5, (N_EDGES,), 0, N_NODES, dtype=jnp.int64)
        return {'h': h, 'W': W, 'b': b, 'src': src, 'dst': dst}
    _L0_gnn_all = _L0_gnn_setup()
    _L0_gnn_in = {k: v for k, v in _L0_gnn_all.items() if k in ('W', 'b')}
    del _L0_gnn_all

    def _L1_gnn_setup():
        import jax, jax.numpy as jnp
        import numpy as np
        N = 1250
        E = 20000
        CIN = 128
        COUT = 128
        EDGE_DIM = 2
        BN_EPS = 1e-05
        key = jax.random.key(seed)
        ks = jax.random.split(key, 9)
        din = 2 * CIN + EDGE_DIM
        x = jax.random.normal(ks[0], (N, CIN), dtype=jnp.float32)
        edge_index = jax.random.randint(ks[1], (2, E), 0, N, dtype=jnp.int64)
        edge_attr = jax.random.normal(ks[2], (E, EDGE_DIM), dtype=jnp.float32)
        W1 = jax.random.normal(ks[3], (din, COUT), dtype=jnp.float32) / np.sqrt(din)
        b1 = jax.random.normal(ks[4], (COUT,), dtype=jnp.float32) * 0.01
        gamma = jnp.ones((COUT,), dtype=jnp.float32)
        beta = jnp.zeros((COUT,), dtype=jnp.float32)
        W2 = jax.random.normal(ks[5], (COUT, COUT), dtype=jnp.float32) / np.sqrt(COUT)
        b2 = jax.random.normal(ks[6], (COUT,), dtype=jnp.float32) * 0.01
        return {'x': x, 'edge_index': edge_index, 'edge_attr': edge_attr, 'W1': W1, 'b1': b1, 'gamma': gamma, 'beta': beta, 'W2': W2, 'b2': b2}
    _L1_gnn_all = _L1_gnn_setup()
    _L1_gnn_in = {k: v for k, v in _L1_gnn_all.items() if k in ('W1', 'b1', 'gamma', 'beta', 'W2', 'b2')}
    del _L1_gnn_all

    def _L2_gnn_setup():
        import jax, jax.numpy as jnp
        import numpy as np
        N, E, D, H, ED = (50000, 25000, 128, 8, 64)
        C = D // H

        def _ln(x, g, b, eps=1e-05):
            m = jnp.mean(x, axis=-1, keepdims=True)
            v = jnp.var(x, axis=-1, keepdims=True)
            return (x - m) * jax.lax.rsqrt(v + eps) * g + b
        key = jax.random.key(seed)
        ks = jax.random.split(key, 16)
        p = lambda k, shape: jax.random.normal(k, shape, dtype=jnp.float32) * 0.05
        return {'x': jax.random.normal(ks[0], (N, D), dtype=jnp.float32), 'edge_index': jax.random.randint(ks[1], (2, E), 0, N, dtype=jnp.int64), 'edge_attr': jax.random.normal(ks[2], (E, ED), dtype=jnp.float32), 'Wq': p(ks[3], (D, D)), 'bq': jnp.zeros((D,), jnp.float32), 'Wk': p(ks[4], (D, D)), 'bk': jnp.zeros((D,), jnp.float32), 'Wv': p(ks[5], (D, D)), 'bv': jnp.zeros((D,), jnp.float32), 'We': p(ks[6], (ED, D)), 'Wskip': p(ks[7], (D, D)), 'bskip': jnp.zeros((D,), jnp.float32), 'g1': jnp.ones((D,), jnp.float32), 'b1': jnp.zeros((D,), jnp.float32), 'g2': jnp.ones((D,), jnp.float32), 'b2': jnp.zeros((D,), jnp.float32), 'Wf1': p(ks[8], (D, 4 * D)), 'bf1': jnp.zeros((4 * D,), jnp.float32), 'Wf2': p(ks[9], (4 * D, D)), 'bf2': jnp.zeros((D,), jnp.float32)}
    _L2_gnn_all = _L2_gnn_setup()
    _L2_gnn_in = {k: v for k, v in _L2_gnn_all.items() if k in ('Wq', 'bq', 'Wk', 'bk', 'Wv', 'bv', 'We', 'Wskip', 'bskip', 'g1', 'b1', 'g2', 'b2', 'Wf1', 'bf1', 'Wf2', 'bf2')}
    del _L2_gnn_all

    def _L3_gnn_setup():
        import jax, jax.numpy as jnp
        import numpy as np
        N_NODES = 50000
        N_EDGES = 25000
        D_IN = 128
        N_HEAD = 4
        D_OUT = D_IN // N_HEAD
        key = jax.random.key(seed)
        k1, k2, k3, k4, k5 = jax.random.split(key, 5)
        in_feat = jax.random.normal(k1, (N_NODES, D_IN), dtype=jnp.float32)
        edge_ind = jax.random.randint(k2, (2, N_EDGES), 0, N_NODES, dtype=jnp.int64)
        W_proj = jax.random.normal(k3, (D_IN, N_HEAD * D_OUT), dtype=jnp.float32) * (1.0 / np.sqrt(D_IN))
        a_src = jax.random.normal(k4, (1, N_HEAD, D_OUT), dtype=jnp.float32) * (1.0 / np.sqrt(D_OUT))
        a_tgt = jax.random.normal(k5, (1, N_HEAD, D_OUT), dtype=jnp.float32) * (1.0 / np.sqrt(D_OUT))
        bias = jnp.zeros((N_HEAD * D_OUT,), dtype=jnp.float32)
        return {'in_feat': in_feat, 'edge_ind': edge_ind, 'edge_len': N_EDGES, 'W_proj': W_proj, 'a_src': a_src, 'a_tgt': a_tgt, 'bias': bias}
    _L3_gnn_all = _L3_gnn_setup()
    _L3_gnn_in = {k: v for k, v in _L3_gnn_all.items() if k in ('W_proj', 'a_src', 'a_tgt', 'bias')}
    del _L3_gnn_all
    return {'x': x, 'src': src, 'dst': dst, 'edge_attr_2': edge_attr_2, 'edge_attr_64': edge_attr_64, 'L0_gnn_W': _L0_gnn_in['W'], 'L0_gnn_b': _L0_gnn_in['b'], 'L1_gnn_W1': _L1_gnn_in['W1'], 'L1_gnn_b1': _L1_gnn_in['b1'], 'L1_gnn_gamma': _L1_gnn_in['gamma'], 'L1_gnn_beta': _L1_gnn_in['beta'], 'L1_gnn_W2': _L1_gnn_in['W2'], 'L1_gnn_b2': _L1_gnn_in['b2'], 'L2_gnn_Wq': _L2_gnn_in['Wq'], 'L2_gnn_bq': _L2_gnn_in['bq'], 'L2_gnn_Wk': _L2_gnn_in['Wk'], 'L2_gnn_bk': _L2_gnn_in['bk'], 'L2_gnn_Wv': _L2_gnn_in['Wv'], 'L2_gnn_bv': _L2_gnn_in['bv'], 'L2_gnn_We': _L2_gnn_in['We'], 'L2_gnn_Wskip': _L2_gnn_in['Wskip'], 'L2_gnn_bskip': _L2_gnn_in['bskip'], 'L2_gnn_g1': _L2_gnn_in['g1'], 'L2_gnn_b1': _L2_gnn_in['b1'], 'L2_gnn_g2': _L2_gnn_in['g2'], 'L2_gnn_b2': _L2_gnn_in['b2'], 'L2_gnn_Wf1': _L2_gnn_in['Wf1'], 'L2_gnn_bf1': _L2_gnn_in['bf1'], 'L2_gnn_Wf2': _L2_gnn_in['Wf2'], 'L2_gnn_bf2': _L2_gnn_in['bf2'], 'L3_gnn_W_proj': _L3_gnn_in['W_proj'], 'L3_gnn_a_src': _L3_gnn_in['a_src'], 'L3_gnn_a_tgt': _L3_gnn_in['a_tgt'], 'L3_gnn_bias': _L3_gnn_in['bias']}

def reference(x, src, dst, edge_attr_2, edge_attr_64, L0_gnn_W, L0_gnn_b, L1_gnn_W1, L1_gnn_b1, L1_gnn_gamma, L1_gnn_beta, L1_gnn_W2, L1_gnn_b2, L2_gnn_Wq, L2_gnn_bq, L2_gnn_Wk, L2_gnn_bk, L2_gnn_Wv, L2_gnn_bv, L2_gnn_We, L2_gnn_Wskip, L2_gnn_bskip, L2_gnn_g1, L2_gnn_b1, L2_gnn_g2, L2_gnn_b2, L2_gnn_Wf1, L2_gnn_bf1, L2_gnn_Wf2, L2_gnn_bf2, L3_gnn_W_proj, L3_gnn_a_src, L3_gnn_a_tgt, L3_gnn_bias):
    import jax
    import jax.numpy as jnp

    def _L0_gnn_ref(h, W, b, src, dst):
        import jax, jax.numpy as jnp
        import numpy as np
        N_NODES = 50000
        N_EDGES = 25000
        D = 128
        m = h[src]
        agg = jax.ops.segment_sum(m, dst, num_segments=h.shape[0])
        out = jax.nn.relu(agg @ W.T + b)
        return out

    def _L1_gnn_ref(x, edge_index, edge_attr, W1, b1, gamma, beta, W2, b2):
        import jax, jax.numpy as jnp
        import numpy as np
        N = 1250
        E = 20000
        CIN = 128
        COUT = 128
        EDGE_DIM = 2
        BN_EPS = 1e-05
        n_nodes = x.shape[0]
        row, col = (edge_index[0], edge_index[1])
        ef = jnp.concatenate([x[row], x[col], edge_attr], axis=-1)
        h = ef @ W1 + b1
        mu = jnp.mean(h, axis=0)
        var = jnp.mean((h - mu) ** 2, axis=0)
        h = (h - mu) * jax.lax.rsqrt(var + BN_EPS) * gamma + beta
        h = jax.nn.relu(h)
        msgs = h @ W2 + b2
        sums = jax.ops.segment_sum(msgs, row, num_segments=n_nodes)
        counts = jax.ops.segment_sum(jnp.ones((msgs.shape[0],), dtype=msgs.dtype), row, num_segments=n_nodes)
        out = sums / (counts + 1.0)[:, None]
        return out + x

    def _L2_gnn_ref(x, edge_index, edge_attr, Wq, bq, Wk, bk, Wv, bv, We, Wskip, bskip, g1, b1, g2, b2, Wf1, bf1, Wf2, bf2):
        import jax, jax.numpy as jnp
        import numpy as np
        N, E, D, H, ED = (50000, 25000, 128, 8, 64)
        C = D // H

        def _ln(x, g, b, eps=1e-05):
            m = jnp.mean(x, axis=-1, keepdims=True)
            v = jnp.var(x, axis=-1, keepdims=True)
            return (x - m) * jax.lax.rsqrt(v + eps) * g + b
        n = x.shape[0]
        src, dst = (edge_index[0], edge_index[1])
        q = (x @ Wq + bq).reshape(n, H, C)
        k = (x @ Wk + bk).reshape(n, H, C)
        v = (x @ Wv + bv).reshape(n, H, C)
        e = (edge_attr @ We).reshape(-1, H, C)
        k_j = k[src] + e
        v_j = v[src] + e
        logits = jnp.sum(q[dst] * k_j, axis=-1) / np.sqrt(C)
        m = jax.ops.segment_max(logits, dst, num_segments=n)
        ex = jnp.exp(logits - m[dst])
        denom = jax.ops.segment_sum(ex, dst, num_segments=n)
        alpha = ex / denom[dst]
        agg = jax.ops.segment_sum(alpha[..., None] * v_j, dst, num_segments=n)
        conv = agg.reshape(n, D) + x @ Wskip + bskip
        h = _ln(conv + x, g1, b1)
        ffn = jax.nn.gelu(h @ Wf1 + bf1, approximate=False) @ Wf2 + bf2
        return _ln(ffn + h, g2, b2)

    def _L3_gnn_ref(in_feat, edge_ind, edge_len, W_proj, a_src, a_tgt, bias):
        import jax, jax.numpy as jnp
        import numpy as np
        N_NODES = 50000
        N_EDGES = 25000
        D_IN = 128
        N_HEAD = 4
        D_OUT = D_IN // N_HEAD
        n_nodes = in_feat.shape[0]
        n_head, d_out = (a_src.shape[1], a_src.shape[2])
        proj_feat = (in_feat @ W_proj).reshape(n_nodes, n_head, d_out)
        src_score = jnp.sum(proj_feat * a_src, axis=-1)
        tgt_score = jnp.sum(proj_feat * a_tgt, axis=-1)
        src_ind, tgt_ind = (edge_ind[0], edge_ind[1])
        edge_score = jax.nn.leaky_relu(src_score[src_ind] + tgt_score[tgt_ind], negative_slope=0.2)
        edge_score = jnp.exp(edge_score - jnp.max(edge_score))
        neigh_sums = jax.ops.segment_sum(edge_score, tgt_ind, num_segments=n_nodes)
        att_per_edge = edge_score / (neigh_sums[tgt_ind] + 1e-16)
        src_feat_weighted = proj_feat[src_ind] * att_per_edge[..., None]
        out_feat = jax.ops.segment_sum(src_feat_weighted, tgt_ind, num_segments=n_nodes)
        return out_feat.reshape(n_nodes, -1) + bias
    edge_index = jnp.stack([src, dst])
    x = _layernorm(x + _L0_gnn_ref(x, L0_gnn_W, L0_gnn_b, src, dst), axis=-1)
    x = _layernorm(x + _L1_gnn_ref(x, edge_index, edge_attr_2, L1_gnn_W1, L1_gnn_b1, L1_gnn_gamma, L1_gnn_beta, L1_gnn_W2, L1_gnn_b2), axis=-1)
    x = _layernorm(x + _L2_gnn_ref(x, edge_index, edge_attr_64, L2_gnn_Wq, L2_gnn_bq, L2_gnn_Wk, L2_gnn_bk, L2_gnn_Wv, L2_gnn_bv, L2_gnn_We, L2_gnn_Wskip, L2_gnn_bskip, L2_gnn_g1, L2_gnn_b1, L2_gnn_g2, L2_gnn_b2, L2_gnn_Wf1, L2_gnn_bf1, L2_gnn_Wf2, L2_gnn_bf2), axis=-1)
    x = _layernorm(x + _L3_gnn_ref(x, edge_index, 50000, L3_gnn_W_proj, L3_gnn_a_src, L3_gnn_a_tgt, L3_gnn_bias), axis=-1)
    return x

_drawn_inputs = setup_inputs


def setup_inputs(seed=0):
    import zlib

    import numpy as np

    out = dict(_drawn_inputs(seed))
    spreads = {'L1_gnn_gamma': (1.0, 0.2),
     'L1_gnn_beta': (0.0, 0.431),
     'L2_gnn_bq': (0.0, 0.8),
     'L2_gnn_bk': (0.0, 0.8),
     'L2_gnn_bv': (0.0, 0.1),
     'L2_gnn_bskip': (0.0, 0.1),
     'L2_gnn_g1': (1.0, 0.2),
     'L2_gnn_b1': (0.0, 0.1),
     'L2_gnn_g2': (1.0, 0.2),
     'L2_gnn_b2': (0.0, 0.1),
     'L2_gnn_bf1': (0.0, 0.1),
     'L2_gnn_bf2': (0.0, 0.1),
     'L3_gnn_bias': (0.0, 0.1)}
    factors = {'edge_attr_2': 4.376, 'L1_gnn_b1': 8.0, 'L1_gnn_b2': 8.0, 'L2_gnn_Wk': 2.754}
    for name, (base, spread) in spreads.items():
        noise = np.random.default_rng([zlib.crc32(name.encode()), seed]).standard_normal(out[name].shape)
        drawn = base * np.exp(spread * noise) if base else spread * noise
        out[name] = jnp.asarray(drawn.astype(out[name].dtype))
    for name, factor in factors.items():
        out[name] = (out[name] * factor).astype(out[name].dtype)
    return out
```

```python
from contextlib import ExitStack

import concourse.bass as bass
from concourse import mybir

F32 = mybir.dt.float32
BF16 = mybir.dt.bfloat16
I32 = mybir.dt.int32
U32 = mybir.dt.uint32
ALU = mybir.AluOpType
ACT = mybir.ActivationFunctionType
AX = mybir.AxisListType

P = 128
G = 4
GE = G * P
D = 128
H2, C2 = 8, 16
H3, C3 = 4, 32
ED = 64
BINS = 256
SKIP = 1 << 17
EPS = 1e-5
LOW = -3e38


def pipeline(eng, pairs, *stages):
    most = max(lag for lag, _ in stages)
    start = 1 + (most + 1) // 2
    for n in range(2 * start):
        for lag, step in stages:
            if n >= lag:
                step(*divmod(n - lag, 2))
    with eng.Fori(start, pairs) as i:
        for k in range(2):
            for lag, step in stages:
                step(i + (k - lag) // 2, (k - lag) % 2)
    for n in range(2 * pairs, 2 * pairs + most):
        for lag, step in stages:
            if n - lag < 2 * pairs:
                step(*divmod(n - lag, 2))


def before(i, k):
    return (i, 0) if k else (i - 1, 1)


def is_first(i, k):
    return isinstance(i, int) and i == 0 and k == 0


def reuses(i):
    return not (isinstance(i, int) and i == 0)


def group(i, k):
    return i * 2 + k


def workspace(nc, ctx, name):
    sems = []

    def sb(n, shape, dt=F32):
        return ctx.enter_context(nc.sbuf_tensor(f"{name}_{n}", shape, dt))

    def ps(n, shape):
        return ctx.enter_context(nc.psum_tensor(f"{name}_{n}", shape, F32))

    def sem(n):
        made = nc.alloc_semaphore(name=f"{name}_{n}")
        sems.append(made)
        return made

    def free():
        nc.clear_and_free_semaphores(sems)
        nc.all_engine_barrier()
    return sb, ps, sem, free


def segment_steps(space, key, prev, widx, table, width, ident, nodes):
    sb, ps, sem, _ = space

    keys = [sb(f"keys{k}", [P, G]) for k in range(2)]
    same = [sb(f"same{k}", [P, G, P]) for k in range(2)]
    carry = [sb(f"carry{k}", [P, G, P]) for k in range(2)]
    rows = [sb(f"rows{k}", [P, G, width]) for k in range(2)]
    at = [sb(f"at{k}", [P, G], I32) for k in range(2)]
    keys_t = [ps(f"keys_t{k}", [P, G, P]) for k in range(2)]
    sums = [ps(f"sums{j}", [P, 512]) for j in range(G)]
    keys_staged = sem("keys_staged")
    keys_turned = sem("keys_turned")
    compared = sem("compared")
    summed = sem("summed")
    evacuated = sem("evacuated")
    at_staged = sem("at_staged")
    pool_turn = sem("scatter_turn")
    scattered = [[sem(f"scattered{k}{j}") for j in range(G)] for k in range(2)]

    def stage_keys(dve, i, k):
        n = group(i, k)
        if reuses(i):
            dve.wait_ge(compared, n * 2 - 2)
        dve.tensor_copy(keys[k][:], key[:, bass.ds(n * G, G)]).then_inc(keys_staged, 1)

    def turn_keys(pe, i, k):
        n = group(i, k)
        pe.wait_ge(keys_staged, n + 1)
        for j in range(G):
            last = pe.transpose(keys_t[k][:, j, :], keys[k][:, j:j + 1].to_broadcast([P, P]),
                                ident[:])
        last.then_inc(keys_turned, 1)

    def compare(dve, i, k):
        n = group(i, k)
        dve.wait_ge(keys_turned, n + 1)
        if reuses(i):
            dve.wait_ge(summed, n * G - G)
        own = key[:, bass.ds(n * G, G)].unsqueeze(2).to_broadcast([P, G, P])
        closing = prev[:, bass.ds(n * G, G)].unsqueeze(2).to_broadcast([P, G, P])
        dve.tensor_tensor(same[k][:], keys_t[k][:], own, ALU.is_equal).then_inc(compared, 1)
        dve.tensor_tensor(carry[k][:], keys_t[k][:], closing, ALU.is_equal).then_inc(compared, 1)

    def total(pe, i, k, messages):
        n = group(i, k)
        pe.wait_ge(compared, n * 2 + 2)
        for j in range(G):
            out = sums[j][:, 0:width]
            first = is_first(i, k) and j == 0
            ins = pe.matmul(out, same[k][:, j, :], messages[:, j, :], start=True, stop=first)
            if not first:
                pe.wait_ge(evacuated, n * G + j)
                pi, pk = (i, k) if j else before(i, k)
                ins = pe.matmul(out, carry[k][:, j, :], rows[pk][:, (j - 1) % G, :],
                                start=False, stop=True)
            ins.then_inc(summed, 1)

    def empty(act, i, k):
        n = group(i, k)
        if reuses(i):
            for j in range(G):
                act.wait_ge(scattered[k][j], i * 16)
        act.copy(at[k][:], widx[:, bass.ds(n * G, G)]).then_inc(at_staged, 1)
        for j in range(G):
            act.wait_ge(summed, n * G + j + 1)
            act.copy(rows[k][:, j, :], sums[j][:, 0:width]).then_inc(evacuated, 1)

    def scatter(pool, i, k):
        n = group(i, k)
        pool.wait_ge(at_staged, n + 1)
        pool.sem_inc(pool_turn, 1)
        pool.wait_ge(evacuated, n * G + G)
        pool.sem_inc(pool_turn, 1)
        for j in range(G):
            pool.indirect_dma_start(
                table, bass.IndirectOffsetOnAxis(at[k][:, j:j + 1].bitcast(U32), 0),
                rows[k][:, j, :], None, bounds_check=nodes - 1, oob_is_err=False,
            ).then_inc(scattered[k][j], 16)

    def settle(pool, pairs):
        for k in range(2):
            for j in range(G):
                pool.wait_ge(scattered[k][j], 16 * pairs)

    return stage_keys, turn_keys, compare, total, empty, scatter, settle, summed


def norm_steps(space, name, half):
    def sb(n, s):
        return [space[0](f"{name}_{n}{k}", s) for k in range(2)]

    def sem(n):
        return space[2](f"{name}_{n}")

    stats, moments = sb("stats", [P, G, 6]), sb("moments", [P, G, 2])
    spread, rstd, shift = sb("spread", [P, G, 1]), sb("rstd", [P, G, 1]), sb("shift", [P, G, 1])
    s_stats, s_moments, s_spread = sem("s_stats"), sem("s_moments"), sem("s_spread")
    s_rstd, s_shift, normed, turn = sem("s_rstd"), sem("s_shift"), sem("normed"), sem("turn")

    def measure(dve, i, k, u):
        n = group(i, k)
        if reuses(i):
            dve.wait_ge(normed, n * G - G)
        for j in range(G):
            dve.bn_stats(stats[k][:, j, :], u[:, j, :]).then_inc(s_stats, 1)
        for j in range(G):
            dve.wait_ge(s_stats, n * G + j + 1)
            dve.sem_inc(turn, 1)
            dve.bn_aggr(moments[k][:, j, :], stats[k][:, j, :]).then_inc(s_moments, 1)
        dve.wait_ge(s_moments, n * G + G)
        dve.tensor_scalar(spread[k][:], moments[k][:, :, 1:2], EPS, None, ALU.add).then_inc(s_spread, 1)

    def root(pool, i, k):
        n = group(i, k)
        pool.wait_ge(s_spread, n + 1)
        pool.tensor_tensor(rstd[k][:], spread[k][:], half[:].unsqueeze(2), ALU.pow).then_inc(s_rstd, 1)

    def balance(dve, i, k):
        n = group(i, k)
        dve.wait_ge(s_rstd, n + 1)
        dve.scalar_tensor_tensor(shift[k][:], moments[k][:, :, 0:1], -1.0, rstd[k][:],
                                 ALU.mult, ALU.mult).then_inc(s_shift, 1)

    def apply(act, i, k, out, u):
        n = group(i, k)
        act.wait_ge(s_shift, n + 1)
        for j in range(G):
            act.activation(out[:, j, :], u[:, j, :], ACT.Identity, bias=shift[k][:, j, :],
                           scale=rstd[k][:, j, :]).then_inc(normed, 1)

    return measure, root, balance, apply, normed


def gnn(nc, x, src, dst, dst_line, ea2, ea64, w, out, n_edges):
    nodes = x.shape[0]
    tiles = src.shape[1]
    edges = tiles * P
    groups = tiles // G
    pairs = groups // 2
    pad_node = nodes - 1
    assert nodes == groups * GE and groups % 2 == 0 and pairs > 3

    top = ExitStack()
    with top:
        def dram(name, shape, dt=F32):
            return nc.dram_tensor(name, shape, dt).ap()

        def sb0(name, shape, dt=F32):
            return top.enter_context(nc.sbuf_tensor(name, shape, dt))

        agg0, agg1 = dram("agg0", [nodes, D]), dram("agg1", [nodes, D + 1])
        agg2, agg3 = dram("agg2", [nodes, D + H2]), dram("agg3", [nodes, D + H3])
        x1, x2b, x3b = dram("x1", [nodes, D]), dram("x2b", [nodes, D]), dram("x3b", [nodes, D])
        to_row, to_col = dram("to_row", [nodes, D]), dram("to_col", [nodes, D])
        q_tab, kv_tab, skip_tab = dram("q_tab", [nodes, D]), dram("kv_tab", [nodes, 2 * D]), dram("skip_tab", [nodes, D])
        proj_tab, tgt_tab = dram("proj_tab", [nodes, D + H3]), dram("tgt_tab", [nodes, H3])
        h_t = dram("h_t", [groups, P, GE])
        v_edge, p_edge = dram("v_edge", [groups, P, GE]), dram("p_edge", [groups, P, GE])
        logit_t, max_t = dram("logit_t", [tiles, H2, P]), dram("max_t", [tiles, H2, P])
        sorted_a, sorted_b = dram("sorted_a", [edges, 4]), dram("sorted_b", [edges, 4])
        chunks = max(c for c in range(1, P // H2 + 1) if tiles % c == 0)
        ends, starts = dram("ends", [2, 2, chunks * H2]), dram("starts", [2, chunks * H2])

        def by_group(t, width):
            return t.rearrange("(g p j) d -> g p j d", p=P, j=G)

        ident, ones = sb0("ident", [P, P]), sb0("ones", [P, P])
        half = sb0("half", [P, G])
        is_last = sb0("is_last", [P, 1])
        dst_i, src_i = sb0("dst_i", [P, tiles], I32), sb0("src_i", [P, tiles], I32)
        dkey, dprev, dwidx = sb0("dkey", [P, tiles]), sb0("dprev", [P, tiles]), sb0("dwidx", [P, tiles], I32)
        rec = sb0("rec", [P, tiles, 4])
        skey, sprev, swidx = sb0("skey", [P, tiles]), sb0("sprev", [P, tiles]), sb0("swidx", [P, tiles], I32)
        scores = sb0("scores", [P, tiles * H2])
        gmax = sb0("gmax", [P, 1])

        def load_consts():
            with ExitStack() as ctx:
                space = workspace(nc, ctx, "consts")
                sb, _, sem, free = space
                zeros = sb("zeros", [P, 8 * (D + H2)])
                made, loaded, zeroed = sem("made"), [sem(f"loaded{m}") for m in range(3)], sem("zeroed")
                zero_made = sem("zero_made")
                with nc.Block() as block:
                    @block.gpsimd
                    def _(pool):
                        pool.memset(ident[:], 0.0).then_inc(made, 1)
                        pool.memset(is_last[:], 0.0).then_inc(made, 1)
                        pool.memset(ones[:], 1.0).then_inc(made, 1)
                        pool.memset(half[:], -0.5).then_inc(made, 1)
                        pool.wait_ge(made, 4)
                        pool.affine_select(out=ident[:], in_=ident[:], compare_op=ALU.not_equal, fill=1.0, base=0,
                                           pattern=[[-1, P]], channel_multiplier=1).then_inc(made, 1)
                        pool.affine_select(out=is_last[:], in_=is_last[:], compare_op=ALU.not_equal, fill=1.0,
                                           base=1 - P, pattern=[[0, 1]], channel_multiplier=1).then_inc(made, 1)
                        pool.wait_ge(made, 6)

                    @block.vector
                    def _(dve):
                        dve.memset(zeros[:], 0.0).then_inc(zero_made, 1)

                    @block.sync
                    def _(sp):
                        sp.dma_start(dst_i[:], dst).then_inc(loaded[0], 16)
                        sp.dma_start(src_i[:], src).then_inc(loaded[1], 16)
                        with nc.allow_non_contiguous_dma(reason="pairs of edge attributes beside the edge's ends"):
                            sp.dma_start(rec[:, :, 0:2], ea2).then_inc(loaded[2], 16)
                        for s in loaded:
                            sp.wait_ge(s, 16)

                    @block.scalar
                    def _(act):
                        act.wait_ge(zero_made, 1)
                        total = 0
                        for table in (agg0, agg1, agg2, agg3):
                            width = table.shape[1]
                            view = table.rearrange("(g p j) d -> g p (j d)", p=P, j=8)
                            for g in range(nodes // (P * 8)):
                                act.dma_start(view[g], zeros[:, 0:8 * width]).then_inc(zeroed, 16)
                                total += 16
                        act.wait_ge(zeroed, total)
                free()

        def order_consts(name, keys_i, key, prev, widx):
            with ExitStack() as ctx:
                space = workspace(nc, ctx, name)
                sb, _, sem, free = space
                nxt = sb("nxt", [P, tiles])
                drop = sb("drop", [P, tiles])
                off = sb("off", [P, 1])
                step, moved, key_ready = sem("step"), [sem("moved0"), sem("moved1")], sem("key_ready")
                with nc.Block() as block:
                    @block.vector
                    def _(dve):
                        dve.memset(nxt[:], -1.0).then_inc(key_ready, 1)
                        dve.tensor_copy(key[:], keys_i).then_inc(key_ready, 1)
                        dve.memset(prev[:], -1.0).then_inc(step, 1)
                        dve.tensor_scalar(off[:], is_last[:], 1.0, None, ALU.subtract).then_inc(step, 1)
                        dve.wait_ge(step, 2)
                        dve.wait_ge(key_ready, 2)
                        dve.tensor_scalar(prev[:, 1:], key[:, :tiles - 1], is_last[:], off[:], ALU.mult,
                                          ALU.add).then_inc(step, 1)
                        for s in moved:
                            dve.wait_ge(s, 16)
                        dve.tensor_tensor(drop[:], key[:], nxt[:], ALU.is_equal).then_inc(step, 1)
                        dve.wait_ge(step, 4)
                        dve.scalar_tensor_tensor(nxt[:], drop[:], float(SKIP), key[:], ALU.mult,
                                                 ALU.add).then_inc(step, 1)
                        dve.wait_ge(step, 5)
                        dve.tensor_copy(widx[:], nxt[:]).then_inc(step, 1)
                        dve.wait_ge(step, 6)

                    @block.sync
                    def _(sp):
                        sp.wait_ge(key_ready, 2)
                        sp.dma_start(nxt[0:P - 1, :], key[1:P, :]).then_inc(moved[0], 16)
                        sp.dma_start(nxt[P - 1:P, 0:tiles - 1], key[0:1, 1:tiles]).then_inc(moved[1], 16)
                        for s in moved:
                            sp.wait_ge(s, 16)
                free()

        def sort_pass(shift, target):
            with ExitStack() as ctx:
                space = workspace(nc, ctx, f"sort{shift}")
                sb, ps, sem, free = space
                bins = sb("bins", [P, BINS], BF16)
                ones_b, before_b, after_b = (sb(n, [P, P], BF16) for n in ("ones_b", "before_b", "after_b"))
                digit_i, digit = sb("digit_i", [P, tiles], I32), sb("digit", [P, tiles])
                base, total = sb("base", [P, BINS + 1]), sb("total", [P, BINS])
                hot = [[sb(f"hot{k}{j}", [P, BINS], BF16) for j in range(G)] for k in range(2)]
                junk = sb("junk", [P, BINS])
                rank = [sb(f"rank{k}", [P, G]) for k in range(2)]
                rank_i, low, high = ([sb(f"{n}{k}", [P, G], I32) for k in range(2)] for n in ("rank_i", "low", "high"))
                low_f, high_f = ([sb(f"{n}{k}", [P, G]) for k in range(2)] for n in ("low_f", "high_f"))
                at = [sb(f"at{k}", [P, G], I32) for k in range(2)]
                row = [sb(f"row{k}", [P, G, 4]) for k in range(2)]
                hist, run = ps("hist", [P, 512]), ps("run", [P, 512])
                made, step = sem("made"), sem("step")
                counted_hot, counted, hot_made, ranked, taken = (
                    sem(n) for n in ("counted_hot", "counted", "hot_made", "ranked", "taken"))
                placed, at_made, pool_turn, base_set, reloaded = (
                    sem(n) for n in ("placed", "at_made", "pool_turn", "base_set", "reloaded"))
                sent = [[sem(f"sent{k}{j}") for j in range(G)] for k in range(2)]
                with nc.Block() as block:
                    @block.gpsimd
                    def _(pool):
                        pool.iota(bins[:], [[1, BINS]], base=0, channel_multiplier=0,
                                  allow_small_or_imprecise_dtypes=True).then_inc(made, 1)
                        for m in (ones_b, before_b, after_b):
                            pool.memset(m[:], 1.0).then_inc(made, 1)
                        pool.wait_ge(made, 4)
                        pool.affine_select(out=before_b[:], in_=before_b[:], compare_op=ALU.is_gt, fill=0.0, base=0,
                                           pattern=[[1, P]], channel_multiplier=-1).then_inc(made, 1)
                        pool.affine_select(out=after_b[:], in_=after_b[:], compare_op=ALU.is_ge, fill=0.0, base=0,
                                           pattern=[[-1, P]], channel_multiplier=1).then_inc(made, 1)

                        def place(i, k):
                            pool.wait_ge(at_made, group(i, k) * 2 + 2)
                            pool.sem_inc(pool_turn, 1)
                            for j in range(G):
                                pool.indirect_dma_start(
                                    target, bass.IndirectOffsetOnAxis(at[k][:, j:j + 1].bitcast(U32), 0),
                                    row[k][:, j, :], None, bounds_check=edges - 1, oob_is_err=False,
                                ).then_inc(sent[k][j], 16)
                        pipeline(pool, pairs, (0, place))
                        for k in range(2):
                            for j in range(G):
                                pool.wait_ge(sent[k][j], 16 * pairs)
                        pool.dma_start(rec[:], target.rearrange("(p t) w -> p t w", p=P)).then_inc(reloaded, 16)
                        pool.wait_ge(reloaded, 16)

                    @block.vector
                    def _(dve):
                        src_word = rec[:].bitcast(I32)[:, :, 2]
                        dve.tensor_scalar(digit_i[:], src_word, shift, BINS - 1, ALU.logical_shift_right,
                                          ALU.bitwise_and).then_inc(step, 1)
                        dve.wait_ge(step, 1)
                        dve.tensor_copy(digit[:], digit_i[:]).then_inc(step, 1)
                        dve.memset(base[:], 0.0).then_inc(step, 1)
                        dve.wait_ge(step, 3)
                        dve.wait_ge(made, 6)

                        def make_hot(i, k, sem_made):
                            for j in range(G):
                                dve.tensor_scalar(hot[k][j][:], bins[:], digit[:, bass.ds(group(i, k) * G + j, 1)],
                                                  None, ALU.is_equal).then_inc(sem_made, 1)

                        def count(i, k):
                            if reuses(i):
                                dve.wait_ge(counted, group(i, k) - 1)
                            make_hot(i, k, counted_hot)
                        pipeline(dve, pairs, (0, count))
                        dve.wait_ge(counted, groups)
                        dve.tensor_copy(total[:], hist[:, 0:BINS]).then_inc(step, 1)
                        dve.wait_ge(step, 4)
                        dve.tensor_tensor_scan(base[:, 1:], total[:], total[:], 0.0, ALU.add,
                                               ALU.bypass).then_inc(step, 1)
                        dve.wait_ge(step, 5)
                        dve.sem_inc(base_set, 1)

                        def rank_group(i, k):
                            n = group(i, k)
                            if reuses(i):
                                dve.wait_ge(taken, n * G - G)
                            make_hot(i, k, hot_made)
                            if reuses(i):
                                dve.wait_ge(at_made, n * 2 - 2)
                            for j in range(G):
                                dve.wait_ge(ranked, n * G + j + 1)
                                dve.tensor_tensor_reduce(out=junk[:], in0=hot[k][j][:], in1=run[:, 0:BINS], scale=1.0,
                                                         scalar=0.0, op0=ALU.mult, op1=ALU.add,
                                                         accum_out=rank[k][:, j:j + 1]).then_inc(placed, 1)
                                dve.wait_ge(placed, n * (G + 5) + j + 1)
                            dve.tensor_copy(rank_i[k][:], rank[k][:]).then_inc(placed, 1)
                            dve.wait_ge(placed, n * (G + 5) + G + 1)
                            dve.tensor_scalar(low[k][:], rank_i[k][:], P - 1, None, ALU.bitwise_and).then_inc(placed, 1)
                            dve.tensor_scalar(high[k][:], rank_i[k][:], 7, None,
                                              ALU.logical_shift_right).then_inc(placed, 1)
                            dve.wait_ge(placed, n * (G + 5) + G + 3)
                            dve.tensor_scalar(low_f[k][:], low[k][:], float(tiles), None, ALU.mult).then_inc(placed, 1)
                            dve.tensor_copy(high_f[k][:], high[k][:]).then_inc(placed, 1)
                            dve.wait_ge(placed, n * (G + 5) + G + 5)
                            if reuses(i):
                                for j in range(G):
                                    dve.wait_ge(sent[k][j], i * 16)
                            dve.tensor_tensor(at[k][:], low_f[k][:], high_f[k][:], ALU.add).then_inc(at_made, 1)
                            dve.tensor_copy(row[k][:].bitcast(I32), rec[:, bass.ds(n * G, G), :].bitcast(I32)).then_inc(at_made, 1)
                        pipeline(dve, pairs, (0, rank_group))

                    @block.tensor
                    def _(pe):
                        pe.wait_ge(made, 6)

                        def count(i, k):
                            n = group(i, k)
                            for j in range(G):
                                pe.wait_ge(counted_hot, n * G + j + 1)
                                last = pe.matmul(hist[:, 0:BINS], ones_b[:], hot[k][j][:], start=is_first(i, k) and j == 0,
                                                 stop=True, skip_group_check=True)
                            last.then_inc(counted, 1)
                        pipeline(pe, pairs, (0, count))
                        pe.wait_ge(base_set, 1)
                        pe.matmul(run[:, 0:BINS], ones[0:1, :], base[0:1, 0:BINS], start=True, stop=True,
                                  skip_group_check=True)

                        def rank_group(i, k):
                            n = group(i, k)
                            for j in range(G):
                                pe.wait_ge(hot_made, n * G + j + 1)
                                pe.matmul(run[:, 0:BINS], before_b[:], hot[k][j][:], start=False, stop=True,
                                          skip_group_check=True).then_inc(ranked, 1)
                                pe.wait_ge(placed, n * (G + 5) + j + 1)
                                pe.matmul(run[:, 0:BINS], after_b[:], hot[k][j][:], start=False, stop=True,
                                          skip_group_check=True).then_inc(taken, 1)
                        pipeline(pe, pairs, (0, rank_group))
                free()

        def fill_records():
            with ExitStack() as ctx:
                space = workspace(nc, ctx, "records")
                sb, _, sem, free = space
                done = sem("filled")
                with nc.Block() as block:
                    @block.vector
                    def _(dve):
                        words = rec[:].bitcast(I32)
                        dve.tensor_copy(words[:, :, 2], src_i[:]).then_inc(done, 1)
                        dve.tensor_copy(words[:, :, 3], dst_i[:]).then_inc(done, 1)
                        dve.wait_ge(done, 2)
                free()

        def gather_sum_edges():
            with ExitStack() as ctx:
                space = workspace(nc, ctx, "l0_edges")
                sb, ps, sem, free = space
                stage_keys, turn_keys, compare, total, empty, scatter, settle, summed = segment_steps(
                    space, dkey, dprev, dwidx, agg0, D, ident, nodes)
                fetched = [sb(f"fetched{k}", [P, G, D]) for k in range(2)]
                index = [sb(f"index{k}", [P, G], I32) for k in range(2)]
                index_staged = sem("index_staged")
                pool_turn = sem("pool_turn")
                gathered = [[sem(f"gathered{k}{j}") for j in range(G)] for k in range(2)]
                with nc.Block() as block:
                    @block.vector
                    def _(dve):
                        def step(i, k):
                            n = group(i, k)
                            if reuses(i):
                                dve.wait_ge(summed, n * G - G)
                            dve.tensor_copy(index[k][:], src_i[:, bass.ds(n * G, G)]).then_inc(index_staged, 1)
                            stage_keys(dve, i, k)
                            compare(dve, i, k)
                        pipeline(dve, pairs, (0, step))

                    @block.gpsimd
                    def _(pool):
                        def step(i, k):
                            pool.wait_ge(index_staged, group(i, k) + 1)
                            pool.sem_inc(pool_turn, 1)
                            for j in range(G):
                                pool.indirect_dma_start(
                                    fetched[k][:, j, :], None, x,
                                    bass.IndirectOffsetOnAxis(index[k][:, j:j + 1].bitcast(U32), 0),
                                ).then_inc(gathered[k][j], 16)
                        pipeline(pool, pairs, (0, step), (1, lambda i, k: scatter(pool, i, k)))
                        settle(pool, pairs)

                    @block.tensor
                    def _(pe):
                        def step(i, k):
                            turn_keys(pe, i, k)
                            for j in range(G):
                                pe.wait_ge(gathered[k][j], i * 16 + 16)
                            total(pe, i, k, fetched[k])
                        pipeline(pe, pairs, (0, step))

                    @block.scalar
                    def _(act):
                        pipeline(act, pairs, (0, lambda i, k: empty(act, i, k)))
                free()

        w0_t = sb0("w0_t", [P, D])
        w1_ab, w1_c, w1_2 = sb0("w1_ab", [P, 2 * D]), sb0("w1_c", [2, D]), sb0("w1_2", [P, D])
        w_qkvs, w_e = sb0("w_qkvs", [P, 4 * D]), sb0("w_e", [ED, D])
        w_f1, w_f2 = sb0("w_f1", [P, 4 * D]), sb0("w_f2", [P, 4, D])
        w_proj = sb0("w_proj", [P, D + 2 * H3])
        b_0, b_11, b_12 = sb0("b_0", [P, D]), sb0("b_11", [P, D]), sb0("b_12", [P, D])
        b_qkvs, b_f2, g_2, b_2, b_3 = (sb0(n, [P, m * D]) for n, m in (
            ("b_qkvs", 4), ("b_f2", 1), ("g_2", 1), ("b_2", 1), ("b_3", 1)))
        gamma, beta, g_1, b_1, b_f1 = (sb0(n, [P, m]) for n, m in (
            ("gamma", 1), ("beta", 1), ("g_1", 1), ("b_1", 1), ("b_f1", 4)))
        bn_scale, bn_shift = sb0("bn_scale", [P, 1]), sb0("bn_shift", [P, 1])

        def load_weights():
            with ExitStack() as ctx:
                space = workspace(nc, ctx, "weights")
                sb, ps, sem, free = space
                w0, proj_t, attend = sb("w0", [P, D]), sb("proj_t", [P, D]), sb("attend", [P, 2 * H3])
                turned, mixed = ps("turned", [P, 2, P]), ps("mixed", [P, 2 * H3])
                loaded, cleared, attend_loaded = sem("loaded"), sem("cleared"), sem("attend_loaded")
                s_turned, s_copied, s_mixed, s_done = sem("s_turned"), sem("s_copied"), sem("s_mixed"), sem("s_done")

                def row(name):
                    return w[name].rearrange("(a n) -> a n", a=1).to_broadcast([P, D])

                def column(name, m=1):
                    return w[name].rearrange("(m p) -> p m", p=P)
                plain = [(w0[:], w["L0_gnn_W"]), (w1_ab[:, 0:D], w["L1_gnn_W1"][0:D, :]),
                         (w1_ab[:, D:2 * D], w["L1_gnn_W1"][D:2 * D, :]), (w1_c[:], w["L1_gnn_W1"][2 * D:2 * D + 2, :]),
                         (w1_2[:], w["L1_gnn_W2"]), (w_e[:], w["L2_gnn_We"]), (w_f1[:], w["L2_gnn_Wf1"]),
                         (w_f2[:], w["L2_gnn_Wf2"].rearrange("(c p) n -> p c n", p=P)),
                         (w_proj[:, 0:D], w["L3_gnn_W_proj"]),
                         (b_0[:], row("L0_gnn_b")), (b_11[:], row("L1_gnn_b1")), (b_12[:], row("L1_gnn_b2")),
                         (b_f2[:], row("L2_gnn_bf2")), (g_2[:], row("L2_gnn_g2")), (b_2[:], row("L2_gnn_b2")),
                         (b_3[:], row("L3_gnn_bias"))]
                for m, n in enumerate(("q", "k", "v", "skip")):
                    plain.append((w_qkvs[:, m * D:(m + 1) * D], w[f"L2_gnn_W{n}"]))
                    plain.append((b_qkvs[:, m * D:(m + 1) * D], row(f"L2_gnn_b{n}")))
                columns = [(gamma, "L1_gnn_gamma"), (beta, "L1_gnn_beta"), (g_1, "L2_gnn_g1"), (b_1, "L2_gnn_b1"),
                           (b_f1, "L2_gnn_bf1")]
                total = 16 * (len(plain) + len(columns))
                with nc.Block() as block:
                    @block.sync
                    def _(sp):
                        for to, frm in plain:
                            sp.dma_start(to, frm).then_inc(loaded, 16)
                        with nc.allow_non_contiguous_dma(reason="short columns, once"):
                            for to, name in columns:
                                sp.dma_start(to[:], column(name)).then_inc(loaded, 16)
                            sp.wait_ge(cleared, 1)
                            for m, name in enumerate(("L3_gnn_a_src", "L3_gnn_a_tgt")):
                                for h in range(H3):
                                    sp.dma_start(attend[h * C3:(h + 1) * C3, m * H3 + h:m * H3 + h + 1],
                                                 w[name][0, h, :].rearrange("(c a) -> c a", a=1)).then_inc(attend_loaded, 16)
                        sp.wait_ge(loaded, total)
                        sp.wait_ge(attend_loaded, 16 * 2 * H3)

                    @block.vector
                    def _(dve):
                        dve.memset(attend[:], 0.0).then_inc(cleared, 1)
                        dve.wait_ge(loaded, total)
                        dve.tensor_tensor(w_qkvs[:, 3 * D:4 * D], w_qkvs[:, 3 * D:4 * D], ident[:], ALU.add).then_inc(s_done, 1)
                        dve.wait_ge(s_turned, 2)
                        dve.tensor_copy(w0_t[:], turned[:, 0, :]).then_inc(s_copied, 1)
                        dve.tensor_copy(proj_t[:], turned[:, 1, :]).then_inc(s_copied, 1)
                        dve.wait_ge(s_mixed, 1)
                        dve.tensor_copy(w_proj[:, D:D + 2 * H3], mixed[:]).then_inc(s_done, 1)
                        dve.wait_ge(s_done, 2)

                    @block.tensor
                    def _(pe):
                        pe.wait_ge(loaded, total)
                        pe.transpose(turned[:, 0, :], w0[:], ident[:]).then_inc(s_turned, 1)
                        pe.transpose(turned[:, 1, :], w_proj[:, 0:D], ident[:]).then_inc(s_turned, 1)
                        pe.wait_ge(s_copied, 2)
                        pe.wait_ge(attend_loaded, 16 * 2 * H3)
                        pe.matmul(mixed[:], proj_t[:], attend[:], start=True, stop=True).then_inc(s_mixed, 1)
                free()

        def nodes_0():
            with ExitStack() as ctx:
                space = workspace(nc, ctx, "l0_nodes")
                sb, ps, sem, free = space
                measure, root, balance, apply_norm, normed = norm_steps(space, "ln", half)
                xg, ag, ag_t, u, x1s, x1_t, row_s, col_s = (
                    [sb(f"{n}{k}", [P, G, D]) for k in range(2)]
                    for n in ("xg", "ag", "ag_t", "u", "x1s", "x1_t", "row_s", "col_s"))
                turn_a, turn_b = ps("turn_a", [P, G, P]), ps("turn_b", [P, G, P])
                y = [ps(f"y{k}", [P, G, D]) for k in range(2)]
                row_p, col_p = ([ps(f"{n}{k}", [P, G, D]) for k in range(2)] for n in ("row_p", "col_p"))
                x_in, a_in = [sem("x_in0"), sem("x_in1")], [sem("a_in0"), sem("a_in1")]
                a_turned, a_copied, y_done, biased, mixed = (
                    sem(n) for n in ("a_turned", "a_copied", "y_done", "biased", "mixed"))
                x_turned, x_copied, ab_done, row_done, col_done = (
                    sem(n) for n in ("x_turned", "x_copied", "ab_done", "row_done", "col_done"))
                x1_out, row_out, col_out = ([sem(f"{n}{k}") for k in range(2)] for n in ("x1_out", "row_out", "col_out"))
                with nc.Block() as block:
                    @block.sync
                    def _(sp):
                        def load(i, k):
                            n = group(i, k)
                            if reuses(i):
                                sp.wait_ge(a_turned, n - 1)
                                sp.wait_ge(mixed, n - 1)
                            sp.dma_start(ag[k][:], by_group(agg0, D)[bass.ds(n, 1)].squeeze(0)).then_inc(a_in[k], 16)
                            sp.dma_start(xg[k][:], by_group(x, D)[bass.ds(n, 1)].squeeze(0)).then_inc(x_in[k], 16)

                        def store(i, k):
                            n = group(i, k)
                            sp.wait_ge(normed, n * G + G)
                            sp.dma_start(by_group(x1, D)[bass.ds(n, 1)].squeeze(0), x1s[k][:]).then_inc(x1_out[k], 16)
                            sp.wait_ge(row_done, n + 1)
                            sp.dma_start(by_group(to_row, D)[bass.ds(n, 1)].squeeze(0), row_s[k][:]).then_inc(row_out[k], 16)
                            sp.wait_ge(col_done, n + 1)
                            sp.dma_start(by_group(to_col, D)[bass.ds(n, 1)].squeeze(0), col_s[k][:]).then_inc(col_out[k], 16)
                        pipeline(sp, pairs, (0, load), (2, store))
                        for s in x1_out + row_out + col_out:
                            sp.wait_ge(s, 16 * pairs)

                    @block.tensor
                    def _(pe):
                        def turn(i, k):
                            n = group(i, k)
                            pe.wait_ge(a_in[k], i * 16 + 16)
                            if not is_first(i, k):
                                pe.wait_ge(a_copied, n)
                            for j in range(G):
                                last = pe.transpose(turn_a[:, j, :], ag[k][:, j, :], ident[:])
                            last.then_inc(a_turned, 1)

                        def project(i, k):
                            n = group(i, k)
                            pe.wait_ge(a_copied, n + 1)
                            if reuses(i):
                                pe.wait_ge(biased, n - 1)
                            for j in range(G):
                                last = pe.matmul(y[k][:, j, :], ag_t[k][:, j, :], w0_t[:], start=True, stop=True)
                            last.then_inc(y_done, 1)

                        def turn_x1(i, k):
                            n = group(i, k)
                            pe.wait_ge(normed, n * G + G)
                            if not is_first(i, k):
                                pe.wait_ge(x_copied, n)
                            for j in range(G):
                                last = pe.transpose(turn_b[:, j, :], x1s[k][:, j, :], ident[:])
                            last.then_inc(x_turned, 1)

                        def project_x1(i, k):
                            n = group(i, k)
                            pe.wait_ge(x_copied, n + 1)
                            if reuses(i):
                                pe.wait_ge(row_done, n - 1)
                                pe.wait_ge(col_done, n - 1)
                            for j in range(G):
                                pe.matmul(row_p[k][:, j, :], x1_t[k][:, j, :], w1_ab[:, 0:D], start=True, stop=True)
                                last = pe.matmul(col_p[k][:, j, :], x1_t[k][:, j, :], w1_ab[:, D:2 * D], start=True, stop=True)
                            last.then_inc(ab_done, 1)
                        pipeline(pe, pairs, (0, turn), (0, project), (1, turn_x1), (1, project_x1))

                    @block.vector
                    def _(dve):
                        def mix(i, k):
                            n = group(i, k)
                            dve.wait_ge(y_done, n + 1)
                            if reuses(i):
                                dve.wait_ge(normed, n * G - G)
                            dve.tensor_tensor(u[k][:], y[k][:], b_0[:].unsqueeze(1).to_broadcast([P, G, D]),
                                              ALU.add).then_inc(biased, 1)
                            dve.wait_ge(x_in[k], i * 16 + 16)
                            dve.wait_ge(biased, n + 1)
                            dve.scalar_tensor_tensor(u[k][:], u[k][:], 0.0, xg[k][:], ALU.max, ALU.add).then_inc(mixed, 1)
                            dve.wait_ge(mixed, n + 1)
                            measure(dve, i, k, u[k])

                        def row(i, k):
                            n = group(i, k)
                            dve.wait_ge(ab_done, n + 1)
                            if reuses(i):
                                dve.wait_ge(row_out[k], i * 16)
                            dve.tensor_tensor(row_s[k][:], row_p[k][:], b_11[:].unsqueeze(1).to_broadcast([P, G, D]),
                                              ALU.add).then_inc(row_done, 1)
                        pipeline(dve, pairs, (0, mix), (1, row), (0, lambda i, k: balance(dve, i, k)))

                    @block.gpsimd
                    def _(pool):
                        pipeline(pool, pairs, (0, lambda i, k: root(pool, i, k)))

                    @block.scalar
                    def _(act):
                        def copy_a(i, k):
                            n = group(i, k)
                            act.wait_ge(a_turned, n + 1)
                            if reuses(i):
                                act.wait_ge(y_done, n - 1)
                            act.copy(ag_t[k][:], turn_a[:]).then_inc(a_copied, 1)

                        def copy_x1(i, k):
                            n = group(i, k)
                            act.wait_ge(x_turned, n + 1)
                            if reuses(i):
                                act.wait_ge(ab_done, n - 1)
                            act.copy(x1_t[k][:], turn_b[:]).then_inc(x_copied, 1)

                        def col(i, k):
                            n = group(i, k)
                            act.wait_ge(ab_done, n + 1)
                            if reuses(i):
                                act.wait_ge(col_out[k], i * 16)
                            act.copy(col_s[k][:], col_p[k][:]).then_inc(col_done, 1)

                        def apply(i, k):
                            n = group(i, k)
                            if reuses(i):
                                act.wait_ge(x1_out[k], i * 16)
                                act.wait_ge(x_turned, n - 1)
                            apply_norm(act, i, k, x1s[k], u[k])
                        pipeline(act, pairs, (0, copy_a), (1, copy_x1), (1, col), (0, apply))
                free()

        def edges_1a():
            valid = n_edges - (groups - 1) * GE
            with ExitStack() as ctx:
                space = workspace(nc, ctx, "l1_edges_a")
                sb, ps, sem, free = space
                row_i, col_i = ([sb(f"{n}{k}", [P, G], I32) for k in range(2)] for n in ("row_i", "col_i"))
                ea = [sb(f"ea{k}", [P, G, 2]) for k in range(2)]
                ea_t = [sb(f"ea_t{k}", [2, G, P]) for k in range(2)]
                at_row, at_col, both, h_s = ([sb(f"{n}{k}", [P, G, D]) for k in range(2)]
                                             for n in ("at_row", "at_col", "both", "h_s"))
                stats, moments, spread, rstd = sb("stats", [P, groups, 6]), sb("moments", [P, 2]), sb("spread", [P, 1]), sb("rstd", [P, 1])
                ea_turn = [ps(f"ea_turn{k}", [2, G, P]) for k in range(2)]
                h = [ps(f"h{k}", [P, G, P]) for k in range(2)]
                index_staged, ea_staged, added, ea_turned, ea_copied = (
                    sem(n) for n in ("index_staged", "ea_staged", "added", "ea_turned", "ea_copied"))
                h_done, h_copied, measured, pool_turn, final = (
                    sem(n) for n in ("h_done", "h_copied", "measured", "pool_turn", "final"))
                row_in = [[sem(f"row_in{k}{j}") for j in range(G)] for k in range(2)]
                col_in = [[sem(f"col_in{k}{j}") for j in range(G)] for k in range(2)]
                h_out = [sem("h_out0"), sem("h_out1")]
                with nc.Block() as block:
                    @block.vector
                    def _(dve):
                        words = rec[:].bitcast(I32)

                        def stage(i, k):
                            n = group(i, k)
                            if reuses(i):
                                dve.wait_ge(added, n - 1)
                            dve.tensor_copy(row_i[k][:], words[:, bass.ds(n * G, G), 2]).then_inc(index_staged, 1)
                            dve.tensor_copy(col_i[k][:], words[:, bass.ds(n * G, G), 3]).then_inc(index_staged, 1)
                            if reuses(i):
                                dve.wait_ge(ea_turned, n - 1)
                            dve.tensor_copy(ea[k][:], rec[:, bass.ds(n * G, G), 0:2]).then_inc(ea_staged, 1)

                        def add(i, k):
                            n = group(i, k)
                            if reuses(i):
                                dve.wait_ge(h_done, n - 1)
                            for j in range(G):
                                dve.wait_ge(row_in[k][j], i * 16 + 16)
                                dve.wait_ge(col_in[k][j], i * 16 + 16)
                            dve.tensor_tensor(both[k][:], at_row[k][:], at_col[k][:], ALU.add).then_inc(added, 1)

                        def measure(i, k):
                            n = group(i, k)
                            dve.wait_ge(h_copied, n + 1)
                            dve.bn_stats(stats[:, bass.ds(n, 1), :].squeeze(1), h_s[k][:].rearrange("p j e -> p (j e)")
                                         ).then_inc(measured, 1)
                        pipeline(dve, pairs, (0, stage), (1, add), (1, measure))
                        dve.wait_ge(measured, groups)
                        dve.wait_ge(h_copied, groups)
                        dve.bn_stats(stats[:, groups - 1, :], h_s[1][:].rearrange("p j e -> p (j e)")[:, 0:valid]).then_inc(final, 1)
                        dve.wait_ge(final, 1)
                        dve.bn_aggr(moments[:], stats[:].rearrange("p g s -> p (g s)")).then_inc(final, 1)
                        dve.wait_ge(final, 2)
                        dve.tensor_scalar(spread[:], moments[:, 1:2], EPS, None, ALU.add).then_inc(final, 1)
                        dve.wait_ge(final, 4)
                        dve.tensor_tensor(bn_scale[:], gamma[:], rstd[:], ALU.mult).then_inc(final, 1)
                        dve.wait_ge(final, 5)
                        dve.tensor_tensor(spread[:], moments[:, 0:1], bn_scale[:], ALU.mult).then_inc(final, 1)
                        dve.wait_ge(final, 6)
                        dve.tensor_tensor(bn_shift[:], beta[:], spread[:], ALU.subtract).then_inc(final, 1)
                        dve.wait_ge(final, 7)

                    @block.gpsimd
                    def _(pool):
                        def fetch(i, k):
                            pool.wait_ge(index_staged, group(i, k) * 2 + 2)
                            pool.sem_inc(pool_turn, 1)
                            for j in range(G):
                                for to, table, index, done in ((at_row, to_row, row_i, row_in), (at_col, to_col, col_i, col_in)):
                                    pool.indirect_dma_start(
                                        to[k][:, j, :], None, table,
                                        bass.IndirectOffsetOnAxis(index[k][:, j:j + 1].bitcast(U32), 0),
                                    ).then_inc(done[k][j], 16)
                        pipeline(pool, pairs, (0, fetch))
                        pool.wait_ge(final, 3)
                        pool.tensor_tensor(rstd[:], spread[:], half[:, 0:1], ALU.pow).then_inc(final, 1)

                    @block.tensor
                    def _(pe):
                        def turn(i, k):
                            n = group(i, k)
                            pe.wait_ge(ea_staged, n + 1)
                            if reuses(i):
                                pe.wait_ge(ea_copied, n - 1)
                            for j in range(G):
                                last = pe.transpose(ea_turn[k][:, j, :], ea[k][:, j, :], ident[:])
                            last.then_inc(ea_turned, 1)

                        def mix(i, k):
                            n = group(i, k)
                            pe.wait_ge(ea_copied, n + 1)
                            pe.wait_ge(added, n + 1)
                            if reuses(i):
                                pe.wait_ge(h_copied, n - 1)
                            pe.matmul(h[k][:], w1_c[:], ea_t[k][:], start=True, stop=False, skip_group_check=True)
                            for j in range(G):
                                last = pe.matmul(h[k][:, j, :], both[k][:, j, :], ident[:], start=False, stop=True,
                                                 skip_group_check=True)
                            last.then_inc(h_done, 1)
                        pipeline(pe, pairs, (0, turn), (1, mix))

                    @block.scalar
                    def _(act):
                        def copy_ea(i, k):
                            n = group(i, k)
                            act.wait_ge(ea_turned, n + 1)
                            if reuses(i):
                                act.wait_ge(h_done, n - 1)
                            act.copy(ea_t[k][:], ea_turn[k][:]).then_inc(ea_copied, 1)

                        def copy_h(i, k):
                            n = group(i, k)
                            act.wait_ge(h_done, n + 1)
                            if reuses(i):
                                act.wait_ge(h_out[k], i * 16)
                                act.wait_ge(measured, n - 1)
                            act.copy(h_s[k][:], h[k][:]).then_inc(h_copied, 1)
                        pipeline(act, pairs, (0, copy_ea), (1, copy_h))

                    @block.sync
                    def _(sp):
                        def store(i, k):
                            n = group(i, k)
                            sp.wait_ge(h_copied, n + 1)
                            sp.dma_start(h_t[bass.ds(n, 1)].squeeze(0), h_s[k][:].rearrange("p j e -> p (j e)")).then_inc(h_out[k], 16)
                        pipeline(sp, pairs, (0, store))
                        for s in h_out:
                            sp.wait_ge(s, 16 * pairs)
                free()

        def edges_1b():
            with ExitStack() as ctx:
                space = workspace(nc, ctx, "l1_edges_b")
                sb, ps, sem, free = space
                stage_keys, turn_keys, compare, total, empty, scatter, settle, summed = segment_steps(
                    space, skey, sprev, swidx, agg1, D + 1, ident, nodes)
                h_s, live = ([sb(f"{n}{k}", [P, GE]) for k in range(2)] for n in ("h_s", "live"))
                msg = [sb(f"msg{k}", [P, G, D + 1]) for k in range(2)]
                product = [ps(f"product{k}", [P, G, D]) for k in range(2)]
                h_in = [sem("h_in0"), sem("h_in1")]
                relu_done, product_done, msg_done = sem("relu_done"), sem("product_done"), sem("msg_done")
                ones_set = sem("ones_set")
                with nc.Block() as block:
                    @block.sync
                    def _(sp):
                        def load(i, k):
                            n = group(i, k)
                            if reuses(i):
                                sp.wait_ge(relu_done, n - 1)
                            sp.dma_start(h_s[k][:], h_t[bass.ds(n, 1)].squeeze(0)).then_inc(h_in[k], 16)
                        pipeline(sp, pairs, (0, load))

                    @block.scalar
                    def _(act):
                        def relu(i, k):
                            n = group(i, k)
                            act.wait_ge(h_in[k], i * 16 + 16)
                            if reuses(i):
                                act.wait_ge(product_done, n - 1)
                            act.activation(live[k][:], h_s[k][:], ACT.Relu, bias=bn_shift[:], scale=bn_scale[:]).then_inc(relu_done, 1)
                        pipeline(act, pairs, (0, relu), (2, lambda i, k: empty(act, i, k)))

                    @block.tensor
                    def _(pe):
                        def multiply(i, k):
                            n = group(i, k)
                            pe.wait_ge(relu_done, n + 1)
                            if reuses(i):
                                pe.wait_ge(msg_done, n - 1)
                            for j in range(G):
                                last = pe.matmul(product[k][:, j, :], live[k][:, j * P:(j + 1) * P], w1_2[:], start=True, stop=True)
                            last.then_inc(product_done, 1)

                        def total_messages(i, k):
                            pe.wait_ge(msg_done, group(i, k) + 1)
                            total(pe, i, k, msg[k])
                        pe.wait_ge(ones_set, 2)
                        pipeline(pe, pairs, (0, lambda i, k: turn_keys(pe, i, k)), (1, multiply), (2, total_messages))

                    @block.vector
                    def _(dve):
                        def add(i, k):
                            n = group(i, k)
                            dve.wait_ge(product_done, n + 1)
                            if reuses(i):
                                dve.wait_ge(summed, n * G - G)
                            dve.tensor_tensor(msg[k][:, :, 0:D], product[k][:], b_12[:].unsqueeze(1).to_broadcast([P, G, D]),
                                              ALU.add).then_inc(msg_done, 1)
                        for k in range(2):
                            dve.memset(msg[k][:, :, D:D + 1], 1.0).then_inc(ones_set, 1)
                        pipeline(dve, pairs, (0, lambda i, k: stage_keys(dve, i, k)),
                                 (1, lambda i, k: compare(dve, i, k)), (1, add))

                    @block.gpsimd
                    def _(pool):
                        pipeline(pool, pairs, (0, lambda i, k: scatter(pool, i, k)))
                        settle(pool, pairs)
                free()

        def nodes_1():
            with ExitStack() as ctx:
                space = workspace(nc, ctx, "l1_nodes")
                sb, ps, sem, free = space
                measure, root, balance, apply_norm, normed = norm_steps(space, "ln", half)
                ag = [sb(f"ag{k}", [P, G, D + 1]) for k in range(2)]
                count, per = ([sb(f"{n}{k}", [P, G, 1]) for k in range(2)] for n in ("count", "per"))
                xg, u, x2s, x2_t, x2b_s = ([sb(f"{n}{k}", [P, G, D]) for k in range(2)]
                                           for n in ("xg", "u", "x2s", "x2_t", "x2b_s"))
                qkvs = [sb(f"qkvs{k}", [P, G, 4 * D]) for k in range(2)]
                turn = [ps(f"turn{k}", [P, G, P]) for k in range(2)]
                y = [ps(f"y{j}", [P, 4 * D]) for j in range(G)]
                a_in, x_in, q_out, kv_out, skip_out, x2b_out = (
                    [sem(f"{n}{k}") for k in range(2)] for n in ("a_in", "x_in", "q_out", "kv_out", "skip_out", "x2b_out"))
                counted, inverted, scaled, mixed, turned = (sem(n) for n in ("counted", "inverted", "scaled", "mixed", "turned"))
                copied, y_done, biased, x2b_done = (sem(n) for n in ("copied", "y_done", "biased", "x2b_done"))
                outs = q_out + kv_out + skip_out + x2b_out
                with nc.Block() as block:
                    @block.sync
                    def _(sp):
                        def load(i, k):
                            n = group(i, k)
                            if reuses(i):
                                sp.wait_ge(mixed, n - 1)
                            sp.dma_start(ag[k][:], by_group(agg1, D + 1)[bass.ds(n, 1)].squeeze(0)).then_inc(a_in[k], 16)
                            sp.dma_start(xg[k][:], by_group(x1, D)[bass.ds(n, 1)].squeeze(0)).then_inc(x_in[k], 16)

                        def store(i, k):
                            n = group(i, k)
                            sp.wait_ge(x2b_done, n + 1)
                            sp.dma_start(by_group(x2b, D)[bass.ds(n, 1)].squeeze(0), x2b_s[k][:]).then_inc(x2b_out[k], 16)
                            sp.wait_ge(biased, n * G + G)
                            sp.dma_start(by_group(q_tab, D)[bass.ds(n, 1)].squeeze(0), qkvs[k][:, :, 0:D]).then_inc(q_out[k], 16)
                            sp.dma_start(by_group(kv_tab, 2 * D)[bass.ds(n, 1)].squeeze(0), qkvs[k][:, :, D:3 * D]).then_inc(kv_out[k], 16)
                            sp.dma_start(by_group(skip_tab, D)[bass.ds(n, 1)].squeeze(0), qkvs[k][:, :, 3 * D:4 * D]).then_inc(skip_out[k], 16)
                        pipeline(sp, pairs, (0, load), (2, store))
                        for s in outs:
                            sp.wait_ge(s, 16 * pairs)

                    @block.vector
                    def _(dve):
                        def mix(i, k):
                            n = group(i, k)
                            dve.wait_ge(a_in[k], i * 16 + 16)
                            dve.tensor_scalar(count[k][:], ag[k][:, :, D:D + 1], 1.0, None, ALU.add).then_inc(counted, 1)
                            dve.wait_ge(counted, n + 1)
                            dve.reciprocal(per[k][:], count[k][:]).then_inc(inverted, 1)
                            dve.wait_ge(inverted, n + 1)
                            if reuses(i):
                                dve.wait_ge(normed, n * G - G)
                            dve.tensor_tensor(u[k][:], ag[k][:, :, 0:D], per[k][:].to_broadcast([P, G, D]),
                                              ALU.mult).then_inc(scaled, 1)
                            dve.wait_ge(scaled, n + 1)
                            dve.wait_ge(x_in[k], i * 16 + 16)
                            dve.scalar_tensor_tensor(u[k][:], xg[k][:], 2.0, u[k][:], ALU.mult, ALU.add).then_inc(mixed, 1)
                            dve.wait_ge(mixed, n + 1)
                            measure(dve, i, k, u[k])

                        def bias(i, k):
                            n = group(i, k)
                            if reuses(i):
                                for s in (q_out[k], kv_out[k], skip_out[k]):
                                    dve.wait_ge(s, i * 16)
                            for j in range(G):
                                dve.wait_ge(y_done, n * G + j + 1)
                                dve.tensor_tensor(qkvs[k][:, j, :], y[j][:], b_qkvs[:], ALU.add).then_inc(biased, 1)
                        pipeline(dve, pairs, (0, mix), (1, bias), (0, lambda i, k: balance(dve, i, k)))

                    @block.gpsimd
                    def _(pool):
                        def shift(i, k):
                            n = group(i, k)
                            if reuses(i):
                                pool.wait_ge(x2b_out[k], i * 16)
                            pool.wait_ge(normed, n * G + G)
                            pool.tensor_tensor(x2b_s[k][:], x2s[k][:], b_2[:].unsqueeze(1).to_broadcast([P, G, D]),
                                               ALU.add).then_inc(x2b_done, 1)
                        pipeline(pool, pairs, (0, lambda i, k: root(pool, i, k)), (1, shift))

                    @block.scalar
                    def _(act):
                        def copy(i, k):
                            n = group(i, k)
                            act.wait_ge(turned, n + 1)
                            if reuses(i):
                                act.wait_ge(y_done, n * G - G)
                            act.copy(x2_t[k][:], turn[k][:]).then_inc(copied, 1)

                        def apply(i, k):
                            n = group(i, k)
                            if reuses(i):
                                act.wait_ge(turned, n - 1)
                                act.wait_ge(x2b_done, n - 1)
                            apply_norm(act, i, k, x2s[k], u[k])
                        pipeline(act, pairs, (1, copy), (0, apply))

                    @block.tensor
                    def _(pe):
                        def turn_x(i, k):
                            n = group(i, k)
                            pe.wait_ge(normed, n * G + G)
                            if reuses(i):
                                pe.wait_ge(copied, n - 1)
                            for j in range(G):
                                last = pe.transpose(turn[k][:, j, :], x2s[k][:, j, :], ident[:])
                            last.then_inc(turned, 1)

                        def project(i, k):
                            n = group(i, k)
                            pe.wait_ge(copied, n + 1)
                            for j in range(G):
                                if not is_first(i, k):
                                    pe.wait_ge(biased, n * G - G + j + 1)
                                pe.matmul(y[j][:], x2_t[k][:, j, :], w_qkvs[:], start=True, stop=True).then_inc(y_done, 1)
                        pipeline(pe, pairs, (1, turn_x), (1, project))
                free()

        def edges_2a():
            with ExitStack() as ctx:
                space = workspace(nc, ctx, "l2_edges_a")
                sb, ps, sem, free = space
                src_s, dst_s = ([sb(f"{n}{k}", [P, G], I32) for k in range(2)] for n in ("src_s", "dst_s"))
                kv, q = [sb(f"kv{k}", [P, G, 2 * D]) for k in range(2)], [sb(f"q{k}", [P, G, D]) for k in range(2)]
                ea_t = [sb(f"ea_t{k}", [ED, G, P]) for k in range(2)]
                key_e, v_e, prod = ([sb(f"{n}{k}", [P, G, D]) for k in range(2)] for n in ("key_e", "v_e", "prod"))
                e = [ps(f"e{k}", [P, G, D]) for k in range(2)]
                index_staged, e_done, v_done, k_done, prod_done, scored, pool_turn = (
                    sem(n) for n in ("index_staged", "e_done", "v_done", "k_done", "prod_done", "scored", "pool_turn"))
                kv_in = [[sem(f"kv_in{k}{j}") for j in range(G)] for k in range(2)]
                q_in = [[sem(f"q_in{k}{j}") for j in range(G)] for k in range(2)]
                ea_in, v_out = [sem("ea_in0"), sem("ea_in1")], [sem("v_out0"), sem("v_out1")]
                with nc.Block() as block:
                    @block.vector
                    def _(dve):
                        def stage(i, k):
                            n = group(i, k)
                            if reuses(i):
                                dve.wait_ge(v_done, n - 1)
                                dve.wait_ge(prod_done, n - 1)
                            dve.tensor_copy(src_s[k][:], src_i[:, bass.ds(n * G, G)]).then_inc(index_staged, 1)
                            dve.tensor_copy(dst_s[k][:], dst_i[:, bass.ds(n * G, G)]).then_inc(index_staged, 1)

                        def score(i, k):
                            n = group(i, k)
                            dve.wait_ge(e_done, n + 1)
                            for j in range(G):
                                dve.wait_ge(kv_in[k][j], i * 16 + 16)
                            if reuses(i):
                                dve.wait_ge(scored, n - 1)
                            dve.tensor_tensor(key_e[k][:], kv[k][:, :, 0:D], e[k][:], ALU.add).then_inc(k_done, 1)
                            if reuses(i):
                                dve.wait_ge(v_out[k], i * 16)
                            dve.tensor_tensor(v_e[k][:], kv[k][:, :, D:2 * D], e[k][:], ALU.add).then_inc(v_done, 1)
                            dve.wait_ge(k_done, n + 1)
                            for j in range(G):
                                dve.wait_ge(q_in[k][j], i * 16 + 16)
                            dve.tensor_tensor(prod[k][:], key_e[k][:], q[k][:], ALU.mult).then_inc(prod_done, 1)
                            dve.wait_ge(prod_done, n + 1)
                            dve.tensor_reduce(scores[:, bass.ds(n * G * H2, G * H2)],
                                              prod[k][:].rearrange("p j (h c) -> p (j h) c", c=C2), AX.X,
                                              ALU.add).then_inc(scored, 1)
                        pipeline(dve, pairs, (0, stage), (1, score))
                        dve.wait_ge(scored, groups)

                    @block.gpsimd
                    def _(pool):
                        def fetch(i, k):
                            pool.wait_ge(index_staged, group(i, k) * 2 + 2)
                            pool.sem_inc(pool_turn, 1)
                            for j in range(G):
                                for to, table, index, done in ((kv, kv_tab, src_s, kv_in), (q, q_tab, dst_s, q_in)):
                                    pool.indirect_dma_start(
                                        to[k][:, j, :], None, table,
                                        bass.IndirectOffsetOnAxis(index[k][:, j:j + 1].bitcast(U32), 0),
                                    ).then_inc(done[k][j], 16)
                        pipeline(pool, pairs, (0, fetch))

                    @block.tensor
                    def _(pe):
                        def edge(i, k):
                            n = group(i, k)
                            pe.wait_ge(ea_in[k], i * 16 + 16)
                            if reuses(i):
                                pe.wait_ge(v_done, n - 1)
                            for j in range(G):
                                last = pe.matmul(e[k][:, j, :], ea_t[k][:, j, :], w_e[:], start=True, stop=True)
                            last.then_inc(e_done, 1)
                        pipeline(pe, pairs, (0, edge))

                    @block.sync
                    def _(sp):
                        def load(i, k):
                            n = group(i, k)
                            if reuses(i):
                                sp.wait_ge(e_done, n - 1)
                            sp.dma_start(ea_t[k][:].rearrange("p j e -> p (j e)"), ea64[bass.ds(n, 1)].squeeze(0)).then_inc(ea_in[k], 16)

                        def store(i, k):
                            n = group(i, k)
                            sp.wait_ge(v_done, n + 1)
                            sp.dma_start(v_edge[bass.ds(n, 1)].squeeze(0), v_e[k][:].rearrange("p j d -> p (j d)")).then_inc(v_out[k], 16)
                        pipeline(sp, pairs, (0, load), (1, store))
                        for s in v_out:
                            sp.wait_ge(s, 16 * pairs)
                free()

        def turn_logits():
            wide = 2 * G * H2
            with ExitStack() as ctx:
                space = workspace(nc, ctx, "turn_logits")
                sb, ps, sem, free = space
                flat, turned = [sb(f"flat{k}", [P, wide]) for k in range(2)], [sb(f"turned{k}", [wide, P]) for k in range(2)]
                turn = [ps(f"turn{k}", [wide, 512]) for k in range(2)]
                s_flat, s_turn, s_copied, pe_turn = sem("s_flat"), sem("s_turn"), sem("s_copied"), sem("pe_turn")
                out_done = [sem("out0"), sem("out1")]
                rows = logit_t.rearrange("(m j) h e -> m (j h) e", j=2 * G)
                with nc.Block() as block:
                    @block.vector
                    def _(dve):
                        def step(m, k, old):
                            if old:
                                dve.wait_ge(s_turn, m)
                            dve.tensor_copy(flat[k][:], scores[:, bass.ds(m * wide, wide)]).then_inc(s_flat, 1)
                        step(0, 0, False)
                        with dve.Fori(1, pairs) as m:
                            step(m, 0, True)

                    @block.tensor
                    def _(pe):
                        def step(m, k, old):
                            pe.wait_ge(s_flat, m + 1)
                            pe.sem_inc(pe_turn, 1)
                            if old:
                                pe.wait_ge(s_copied, m)
                                pe.sem_inc(pe_turn, 1)
                            pe.transpose(turn[k][:, 0:P], flat[k][:], ident[:]).then_inc(s_turn, 1)
                        step(0, 0, False)
                        with pe.Fori(1, pairs) as m:
                            step(m, 0, True)

                    @block.scalar
                    def _(act):
                        def step(m, k, old):
                            act.wait_ge(s_turn, m + 1)
                            if old:
                                act.wait_ge(out_done[k], m * 16)
                            act.copy(turned[k][:], turn[k][:, 0:P]).then_inc(s_copied, 1)
                        step(0, 0, False)
                        with act.Fori(1, pairs) as m:
                            step(m, 0, True)

                    @block.sync
                    def _(sp):
                        with sp.Fori(0, pairs) as m:
                            sp.wait_ge(s_copied, m + 1)
                            sp.dma_start(rows[bass.ds(m, 1)].squeeze(0), turned[0][:]).then_inc(out_done[0], 16)
                        sp.wait_ge(out_done[0], 16 * pairs)
                free()

        def segment_max():
            lanes, span = chunks * H2, edges // chunks
            per = tiles // chunks
            with ExitStack() as ctx:
                space = workspace(nc, ctx, "segment_max")
                sb, _, sem, free = space
                keys = sb("keys", [lanes, span + 2], I32)
                logit = sb("logit", [lanes, span])
                reset = [sb("reset_f", [lanes, span]), sb("reset_b", [lanes, span])]
                best = [sb("best_f", [lanes, span]), sb("best_b", [lanes, span])]
                through = [sb(f"through{d}", [lanes, 1]) for d in range(2)]
                end_s, through_s, carry_s = ([sb(f"{n}{d}", [H2, chunks]) for d in range(2)]
                                             for n in ("end_s", "through_s", "carry_s"))
                start_s = [sb(f"start_s{d}", [H2, chunks]) for d in range(2)]
                entry = [sb(f"entry{d}", [lanes, 1]) for d in range(2)]
                loaded, step, saved, fetched, started, entered, out_done = (
                    sem(n) for n in ("loaded", "step", "saved", "fetched", "started", "entered", "out_done"))
                saved = [sem(f"saved{d}") for d in range(2)]
                fetched = [sem(f"fetched{d}") for d in range(2)]
                started = [sem(f"started{d}") for d in range(2)]
                entered = [sem(f"entered{d}") for d in range(2)]
                scanned, spread = [sem("scanned0"), sem("scanned1")], [sem("spread0"), sem("spread1")]
                line = logit_t.rearrange("(c t) h e -> c h t e", c=chunks)
                out_line = max_t.rearrange("(c t) h e -> c h t e", c=chunks)
                by_head = "(c h) -> h c"
                with nc.Block() as block:
                    @block.sync
                    def _(sp):
                        for c in range(chunks):
                            rows = slice(c * H2, (c + 1) * H2)
                            sp.dma_start(logit[rows, :].rearrange("h (t e) -> h t e", t=per), line[c]).then_inc(loaded, 16)
                            sp.dma_start(keys[rows, :], dst_line[0:1, c * span:c * span + span + 2].to_broadcast(
                                [H2, span + 2])).then_inc(loaded, 16)
                        with nc.allow_non_contiguous_dma(reason="one word for each chunk and head"):
                            for d in range(2):
                                last = best[d][:, span - 1:span] if d == 0 else best[d][:, 0:1]
                                sp.wait_ge(scanned[d], 1)
                                sp.dma_start(ends[d, 0].rearrange("(l a) -> l a", a=1), last).then_inc(saved[d], 16)
                                sp.dma_start(ends[d, 1].rearrange("(l a) -> l a", a=1), through[d][:]).then_inc(saved[d], 16)
                                sp.wait_ge(saved[d], 32)
                                sp.dma_start(end_s[d][:], ends[d, 0].rearrange(by_head, h=H2)).then_inc(fetched[d], 16)
                                sp.dma_start(through_s[d][:], ends[d, 1].rearrange(by_head, h=H2)).then_inc(fetched[d], 16)
                                sp.wait_ge(spread[d], 1)
                                sp.dma_start(starts[d].rearrange(by_head, h=H2), start_s[d][:]).then_inc(started[d], 16)
                                sp.wait_ge(started[d], 16)
                                sp.dma_start(entry[d][:], starts[d].rearrange("(l a) -> l a", a=1)).then_inc(entered[d], 16)
                        sp.wait_ge(scanned[1], 2)
                        for c in range(chunks):
                            rows = slice(c * H2, (c + 1) * H2)
                            sp.dma_start(out_line[c], best[1][rows, :].rearrange("h (t e) -> h t e", t=per)).then_inc(out_done, 16)
                        sp.wait_ge(out_done, 16 * chunks)

                    @block.vector
                    def _(dve):
                        done = 0

                        def chain(ins):
                            nonlocal done
                            ins.then_inc(step, 1)
                            done += 1
                            dve.wait_ge(step, done)
                        dve.wait_ge(loaded, 32 * chunks)
                        for d in range(2):
                            other = keys[:, 0:span] if d == 0 else keys[:, 2:span + 2]
                            chain(dve.tensor_tensor(reset[d][:], keys[:, 1:span + 1], other, ALU.is_equal))
                            chain(dve.tensor_scalar(reset[d][:], reset[d][:], -LOW, LOW, ALU.mult, ALU.add))
                            chain(dve.tensor_reduce(through[d][:], reset[d][:], AX.X, ALU.min))

                        def scan(d, initial):
                            frm = logit if d == 0 else best[0]
                            way = slice(None) if d == 0 else slice(None, None, -1)
                            return dve.tensor_tensor_scan(best[d][:, way], reset[d][:, way], frm[:, way], initial,
                                                          ALU.add, ALU.max)
                        for d in range(2):
                            scan(d, LOW).then_inc(scanned[d], 1)
                            dve.wait_ge(fetched[d], 32)
                            way = slice(None) if d == 0 else slice(None, None, -1)
                            chain(dve.tensor_tensor_scan(carry_s[d][:, way], through_s[d][:, way], end_s[d][:, way], LOW,
                                                         ALU.add, ALU.max))
                            chain(dve.memset(start_s[d][:], LOW))
                            if chunks > 1:
                                to, frm = (slice(1, None), slice(0, -1)) if d == 0 else (slice(0, -1), slice(1, None))
                                chain(dve.tensor_copy(start_s[d][:, to], carry_s[d][:, frm]))
                            dve.sem_inc(spread[d], 1)
                            dve.wait_ge(entered[d], 16)
                            scan(d, entry[d][:]).then_inc(scanned[d], 1)
                            dve.wait_ge(scanned[d], 2)
                free()

        def weigh_edges(name, seg_table, heads, source, scale, minus):
            c = D // heads
            with ExitStack() as ctx:
                space = workspace(nc, ctx, name)
                sb, ps, sem, free = space
                stage_keys, turn_keys, compare, total, empty, scatter, settle, summed = segment_steps(
                    space, dkey, dprev, dwidx, seg_table, D + heads, ident, nodes)
                v = [sb(f"v{k}", [P, G, D]) for k in range(2)]
                top_t = [sb(f"top_t{k}", [G * heads, P]) for k in range(2)]
                diff, ex = ([sb(f"{n}{k}", [P, G * heads]) for k in range(2)] for n in ("diff", "ex"))
                msg = [sb(f"msg{k}", [P, G, D + heads]) for k in range(2)]
                peak = [ps(f"peak{k}", [P, 512]) for k in range(2)]
                v_in, top_in = [sem("v_in0"), sem("v_in1")], [sem("top_in0"), sem("top_in1")]
                peaked, differed, risen, weighed, pe_turn = (
                    sem(n) for n in ("peaked", "differed", "risen", "weighed", "pe_turn"))
                rows = max_t.rearrange("(g j) h e -> g (j h) e", j=G)
                with nc.Block() as block:
                    @block.sync
                    def _(sp):
                        def load(i, k):
                            n = group(i, k)
                            if minus is None:
                                if reuses(i):
                                    sp.wait_ge(peaked, n - 1)
                                sp.dma_start(top_t[k][:], rows[bass.ds(n, 1)].squeeze(0)).then_inc(top_in[k], 16)
                            if reuses(i):
                                sp.wait_ge(weighed, n * 2 - 2)
                            sp.dma_start(v[k][:].rearrange("p j d -> p (j d)"), source[bass.ds(n, 1)].squeeze(0)).then_inc(v_in[k], 16)
                        pipeline(sp, pairs, (0, load))

                    @block.tensor
                    def _(pe):
                        def turn_peaks(i, k):
                            n = group(i, k)
                            pe.wait_ge(top_in[k], i * 16 + 16)
                            pe.sem_inc(pe_turn, 1)
                            if reuses(i):
                                pe.wait_ge(differed, n - 1)
                                pe.sem_inc(pe_turn, 1)
                            pe.transpose(peak[k][:, 0:G * heads], top_t[k][:], ident[0:G * heads, 0:G * heads]).then_inc(peaked, 1)

                        def total_messages(i, k):
                            pe.wait_ge(weighed, group(i, k) * 2 + 2)
                            total(pe, i, k, msg[k])
                        stages = [(0, lambda i, k: turn_keys(pe, i, k)), (2, total_messages)]
                        if minus is None:
                            stages.insert(0, (0, turn_peaks))
                        pipeline(pe, pairs, *stages)

                    @block.vector
                    def _(dve):
                        def differ(i, k):
                            n = group(i, k)
                            dve.wait_ge(peaked, n + 1)
                            if reuses(i):
                                dve.wait_ge(risen, n - 1)
                            dve.tensor_tensor(diff[k][:], scores[:, bass.ds(n * G * heads, G * heads)],
                                              peak[k][:, 0:G * heads], ALU.subtract).then_inc(differed, 1)

                        def weigh(i, k):
                            n = group(i, k)
                            dve.wait_ge(risen, n + 1)
                            dve.wait_ge(v_in[k], i * 16 + 16)
                            if reuses(i):
                                dve.wait_ge(summed, n * G - G)
                            for_heads = ex[k][:].rearrange("p (j h) -> p j h", h=heads)
                            dve.tensor_tensor(msg[k][:, :, 0:D].rearrange("p j (h c) -> p j h c", c=c),
                                              v[k][:].rearrange("p j (h c) -> p j h c", c=c),
                                              for_heads.unsqueeze(3).to_broadcast([P, G, heads, c]),
                                              ALU.mult).then_inc(weighed, 1)
                            dve.tensor_copy(msg[k][:, :, D:D + heads], for_heads).then_inc(weighed, 1)
                        stages = [(0, lambda i, k: stage_keys(dve, i, k)), (1, lambda i, k: compare(dve, i, k)),
                                  (1, weigh)]
                        if minus is None:
                            stages.insert(1, (0, differ))
                        pipeline(dve, pairs, *stages)

                    @block.scalar
                    def _(act):
                        def rise(i, k):
                            n = group(i, k)
                            if reuses(i):
                                act.wait_ge(weighed, n * 2 - 2)
                            if minus is None:
                                act.wait_ge(differed, n + 1)
                                act.activation(ex[k][:], diff[k][:], ACT.Exp, scale=scale).then_inc(risen, 1)
                            else:
                                act.activation(ex[k][:], scores[:, bass.ds(n * G * heads, G * heads)], ACT.Exp,
                                               bias=minus[:], scale=scale).then_inc(risen, 1)
                        pipeline(act, pairs, (0, rise), (2, lambda i, k: empty(act, i, k)))

                    @block.gpsimd
                    def _(pool):
                        pipeline(pool, pairs, (0, lambda i, k: scatter(pool, i, k)))
                        settle(pool, pairs)
                free()

        def nodes_2():
            with ExitStack() as ctx:
                space = workspace(nc, ctx, "l2_nodes")
                sb, ps, sem, free = space
                measure_a, root_a, balance_a, norm_a, a_normed = norm_steps(space, "na", half)
                measure_b, root_b, balance_b, norm_b, b_normed = norm_steps(space, "nb", half)
                measure_x, root_x, balance_x, norm_x, x_normed = norm_steps(space, "nx", half)
                ag = [sb(f"ag{k}", [P, G, D + H2]) for k in range(2)]
                den, per = ([sb(f"{n}{k}", [P, G, H2]) for k in range(2)] for n in ("den", "per"))
                skip, x2g, ua, normed_a, h_t_s, ub, normed_b, ux, x3s, x3_t, x3b_s = (
                    [sb(f"{n}{k}", [P, G, D]) for k in range(2)] for n in (
                        "skip", "x2g", "ua", "normed_a", "h_t_s", "ub", "normed_b", "ux", "x3s", "x3_t", "x3b_s"))
                act_t = [sb(f"act_t{k}", [P, 4, GE]) for k in range(2)]
                ext = [sb(f"ext{k}", [P, G, D + 2 * H3]) for k in range(2)]
                turn_h, turn_x, y = ps("turn_h", [P, G, P]), ps("turn_x", [P, G, P]), ps("y", [P, G, D])
                f = [ps(f"f{m}", [P, GE]) for m in range(2)]
                pe_ext = [ps(f"pe_ext{m}", [P, 512]) for m in range(2)]
                a_in, skip_in, x2_in, ext_out, tgt_out, x3b_out = (
                    [sem(f"{n}{k}") for k in range(2)] for n in ("a_in", "skip_in", "x2_in", "ext_out", "tgt_out", "x3b_out"))
                floored, inverted, conv_done, ua_done, h_turned, h_copied = (
                    sem(n) for n in ("floored", "inverted", "conv_done", "ua_done", "h_turned", "h_copied"))
                f_done, gelu_done, y_done, ub_done, scaled_b, ux_done = (
                    sem(n) for n in ("f_done", "gelu_done", "y_done", "ub_done", "scaled_b", "ux_done"))
                x_turned, x_copied, ext_done, ext_copied, x3b_done = (
                    sem(n) for n in ("x_turned", "x_copied", "ext_done", "ext_copied", "x3b_done"))
                with nc.Block() as block:
                    @block.sync
                    def _(sp):
                        def load(i, k):
                            n = group(i, k)
                            if reuses(i):
                                sp.wait_ge(ua_done, n - 1)
                            sp.dma_start(ag[k][:], by_group(agg2, D + H2)[bass.ds(n, 1)].squeeze(0)).then_inc(a_in[k], 16)
                            sp.dma_start(skip[k][:], by_group(skip_tab, D)[bass.ds(n, 1)].squeeze(0)).then_inc(skip_in[k], 16)

                        def load_x2(i, k):
                            n = group(i, k)
                            if reuses(i):
                                sp.wait_ge(ux_done, n - 1)
                            sp.dma_start(x2g[k][:], by_group(x2b, D)[bass.ds(n, 1)].squeeze(0)).then_inc(x2_in[k], 16)

                        def store(i, k):
                            n = group(i, k)
                            sp.wait_ge(x3b_done, n + 1)
                            sp.dma_start(by_group(x3b, D)[bass.ds(n, 1)].squeeze(0), x3b_s[k][:]).then_inc(x3b_out[k], 16)
                            sp.wait_ge(ext_copied, n * 2 + 2)
                            sp.dma_start(by_group(proj_tab, D + H3)[bass.ds(n, 1)].squeeze(0), ext[k][:, :, 0:D + H3]).then_inc(ext_out[k], 16)
                            sp.dma_start(by_group(tgt_tab, H3)[bass.ds(n, 1)].squeeze(0), ext[k][:, :, D + H3:D + 2 * H3]).then_inc(tgt_out[k], 16)
                        pipeline(sp, pairs, (0, load), (1, load_x2), (3, store))
                        for s in x3b_out + ext_out + tgt_out:
                            sp.wait_ge(s, 16 * pairs)

                    @block.vector
                    def _(dve):
                        def conv(i, k):
                            n = group(i, k)
                            dve.wait_ge(a_in[k], i * 16 + 16)
                            dve.tensor_scalar(den[k][:], ag[k][:, :, D:D + H2], 1e-30, None, ALU.max).then_inc(floored, 1)
                            dve.wait_ge(floored, n + 1)
                            dve.reciprocal(per[k][:], den[k][:]).then_inc(inverted, 1)
                            dve.wait_ge(inverted, n + 1)
                            if reuses(i):
                                dve.wait_ge(a_normed, n * G - G)
                            dve.tensor_tensor(ua[k][:].rearrange("p j (h c) -> p j h c", c=C2),
                                              ag[k][:, :, 0:D].rearrange("p j (h c) -> p j h c", c=C2),
                                              per[k][:].unsqueeze(3).to_broadcast([P, G, H2, C2]), ALU.mult).then_inc(conv_done, 1)
                            dve.wait_ge(conv_done, n + 1)
                            dve.wait_ge(skip_in[k], i * 16 + 16)
                            dve.tensor_tensor(ua[k][:], ua[k][:], skip[k][:], ALU.add).then_inc(ua_done, 1)
                            dve.wait_ge(ua_done, n + 1)
                            measure_a(dve, i, k, ua[k])

                        def after_ffn(i, k):
                            n = group(i, k)
                            dve.wait_ge(y_done, n + 1)
                            if reuses(i):
                                dve.wait_ge(b_normed, n * G - G)
                            dve.tensor_tensor(ub[k][:], y[:], b_f2[:].unsqueeze(1).to_broadcast([P, G, D]), ALU.add).then_inc(ub_done, 1)
                            dve.wait_ge(ub_done, n + 1)
                            measure_b(dve, i, k, ub[k])

                        def residual(i, k):
                            n = group(i, k)
                            dve.wait_ge(b_normed, n * G + G)
                            if reuses(i):
                                dve.wait_ge(x_normed, n * G - G)
                            dve.tensor_tensor(ux[k][:], normed_b[k][:], g_2[:].unsqueeze(1).to_broadcast([P, G, D]), ALU.mult).then_inc(scaled_b, 1)
                            dve.wait_ge(scaled_b, n + 1)
                            dve.wait_ge(x2_in[k], i * 16 + 16)
                            dve.tensor_tensor(ux[k][:], ux[k][:], x2g[k][:], ALU.add).then_inc(ux_done, 1)
                            dve.wait_ge(ux_done, n + 1)
                            measure_x(dve, i, k, ux[k])
                        pipeline(dve, pairs, (0, conv), (1, after_ffn), (0, lambda i, k: balance_a(dve, i, k)),
                                 (1, lambda i, k: balance_b(dve, i, k)), (2, residual), (2, lambda i, k: balance_x(dve, i, k)))

                    @block.gpsimd
                    def _(pool):
                        def shift(i, k):
                            n = group(i, k)
                            if reuses(i):
                                pool.wait_ge(x3b_out[k], i * 16)
                            pool.wait_ge(x_normed, n * G + G)
                            pool.tensor_tensor(x3b_s[k][:], x3s[k][:], b_3[:].unsqueeze(1).to_broadcast([P, G, D]),
                                               ALU.add).then_inc(x3b_done, 1)
                        pipeline(pool, pairs, (0, lambda i, k: root_a(pool, i, k)), (1, lambda i, k: root_b(pool, i, k)),
                                 (2, lambda i, k: root_x(pool, i, k)), (3, shift))

                    @block.scalar
                    def _(act):
                        def apply_a(i, k):
                            if reuses(i):
                                act.wait_ge(h_turned, group(i, k) - 1)
                            norm_a(act, i, k, normed_a[k], ua[k])

                        def copy_h(i, k):
                            n = group(i, k)
                            act.wait_ge(h_turned, n + 1)
                            if reuses(i):
                                act.wait_ge(y_done, n - 1)
                            act.activation(h_t_s[k][:], turn_h[:], ACT.Identity, bias=b_1[:], scale=g_1[:]).then_inc(h_copied, 1)

                        def gelu(i, k):
                            n = group(i, k)
                            if reuses(i):
                                act.wait_ge(y_done, n - 1)
                            for m in range(4):
                                act.wait_ge(f_done, n * 4 + m + 1)
                                act.activation(act_t[k][:, m, :], f[m % 2][:], ACT.Gelu, bias=b_f1[:, m:m + 1]).then_inc(gelu_done, 1)

                        def apply_b(i, k):
                            if reuses(i):
                                act.wait_ge(scaled_b, group(i, k) - 1)
                            norm_b(act, i, k, normed_b[k], ub[k])

                        def apply_x(i, k):
                            n = group(i, k)
                            if reuses(i):
                                act.wait_ge(x_turned, n - 1)
                                act.wait_ge(x3b_done, n - 1)
                            norm_x(act, i, k, x3s[k], ux[k])

                        def copy_x(i, k):
                            n = group(i, k)
                            act.wait_ge(x_turned, n + 1)
                            if reuses(i):
                                act.wait_ge(ext_done, n * 2 - 2)
                            act.copy(x3_t[k][:], turn_x[:]).then_inc(x_copied, 1)

                        def copy_ext(i, k):
                            n = group(i, k)
                            if reuses(i):
                                act.wait_ge(ext_out[k], i * 16)
                                act.wait_ge(tgt_out[k], i * 16)
                            for m in range(2):
                                act.wait_ge(ext_done, n * 2 + m + 1)
                                act.copy(ext[k][:, 2 * m:2 * m + 2, :], pe_ext[m][:, 0:2 * (D + 2 * H3)].rearrange(
                                    "p (j d) -> p j d", j=2)).then_inc(ext_copied, 1)
                        pipeline(act, pairs, (1, copy_h), (1, gelu), (3, copy_x), (3, copy_ext), (0, apply_a), (1, apply_b), (2, apply_x))

                    @block.tensor
                    def _(pe):
                        def turn(i, k):
                            n = group(i, k)
                            pe.wait_ge(a_normed, n * G + G)
                            if not is_first(i, k):
                                pe.wait_ge(h_copied, n)
                            for j in range(G):
                                last = pe.transpose(turn_h[:, j, :], normed_a[k][:, j, :], ident[:])
                            last.then_inc(h_turned, 1)

                        def ffn(i, k):
                            n = group(i, k)
                            pe.wait_ge(h_copied, n + 1)
                            for m in range(4):
                                if m >= 2 or not is_first(i, k):
                                    pe.wait_ge(gelu_done, n * 4 + m - 1)
                                pe.matmul(f[m % 2][:], w_f1[:, m * P:(m + 1) * P], h_t_s[k][:], start=True, stop=True).then_inc(f_done, 1)
                            if not is_first(i, k):
                                pe.wait_ge(ub_done, n)
                            pe.wait_ge(gelu_done, n * 4 + 4)
                            for j in range(G):
                                pe.matmul(y[:, j, :], h_t_s[k][:, j, :], ident[:], start=True, stop=False)
                                for m in range(4):
                                    last = pe.matmul(y[:, j, :], act_t[k][:, m, j * P:(j + 1) * P], w_f2[:, m, :],
                                                     start=False, stop=(m == 3))
                            last.then_inc(y_done, 1)

                        def project(i, k):
                            n = group(i, k)
                            pe.wait_ge(x_normed, n * G + G)
                            if not is_first(i, k):
                                pe.wait_ge(x_copied, n)
                            for j in range(G):
                                last = pe.transpose(turn_x[:, j, :], x3s[k][:, j, :], ident[:])
                            last.then_inc(x_turned, 1)
                            pe.wait_ge(x_copied, n + 1)
                            for m in range(2):
                                if not is_first(i, k):
                                    pe.wait_ge(ext_copied, n * 2 - 1 + m)
                                for j in range(2):
                                    at = j * (D + 2 * H3)
                                    last = pe.matmul(pe_ext[m][:, at:at + D + 2 * H3], x3_t[k][:, 2 * m + j, :], w_proj[:],
                                                     start=True, stop=True)
                                last.then_inc(ext_done, 1)
                        pipeline(pe, pairs, (1, turn), (1, ffn), (3, project))
                free()

        def edges_3a():
            with ExitStack() as ctx:
                space = workspace(nc, ctx, "l3_edges_a")
                sb, _, sem, free = space
                src_s, dst_s = ([sb(f"{n}{k}", [P, G], I32) for k in range(2)] for n in ("src_s", "dst_s"))
                proj = [sb(f"proj{k}", [P, G, D + H3]) for k in range(2)]
                tgt, both = ([sb(f"{n}{k}", [P, G, H3]) for k in range(2)] for n in ("tgt", "both"))
                padded, masked = sb("padded", [P, tiles]), sb("masked", [P, tiles, H3])
                own, whole = sb("own", [P, 1]), sb("whole", [P, 1])
                index_staged, both_done, scored, pool_turn, final = (
                    sem(n) for n in ("index_staged", "both_done", "scored", "pool_turn", "final"))
                proj_in = [[sem(f"proj_in{k}{j}") for j in range(G)] for k in range(2)]
                tgt_in = [[sem(f"tgt_in{k}{j}") for j in range(G)] for k in range(2)]
                p_out = [sem("p_out0"), sem("p_out1")]
                with nc.Block() as block:
                    @block.vector
                    def _(dve):
                        def stage(i, k):
                            n = group(i, k)
                            if reuses(i):
                                dve.wait_ge(p_out[k], i * 16)
                                dve.wait_ge(both_done, n - 1)
                            dve.tensor_copy(src_s[k][:], src_i[:, bass.ds(n * G, G)]).then_inc(index_staged, 1)
                            dve.tensor_copy(dst_s[k][:], dst_i[:, bass.ds(n * G, G)]).then_inc(index_staged, 1)

                        def score(i, k):
                            n = group(i, k)
                            for j in range(G):
                                dve.wait_ge(proj_in[k][j], i * 16 + 16)
                                dve.wait_ge(tgt_in[k][j], i * 16 + 16)
                            if reuses(i):
                                dve.wait_ge(scored, n - 1)
                            dve.tensor_tensor(both[k][:], proj[k][:, :, D:D + H3], tgt[k][:], ALU.add).then_inc(both_done, 1)
                            dve.wait_ge(both_done, n + 1)
                            dve.scalar_tensor_tensor(scores[:, bass.ds(n * G * H3, G * H3)], both[k][:].rearrange("p j h -> p (j h)"),
                                                     0.2, both[k][:].rearrange("p j h -> p (j h)"), ALU.mult, ALU.max).then_inc(scored, 1)
                        pipeline(dve, pairs, (0, stage), (1, score))
                        dve.wait_ge(scored, groups)
                        dve.tensor_scalar(padded[:], dkey[:], float(pad_node), LOW, ALU.is_equal, ALU.mult).then_inc(final, 1)
                        dve.wait_ge(final, 1)
                        dve.tensor_tensor(masked[:], scores[:, 0:tiles * H3].rearrange("p (t h) -> p t h", h=H3),
                                          padded[:].unsqueeze(2).to_broadcast([P, tiles, H3]), ALU.add).then_inc(final, 1)
                        dve.wait_ge(final, 2)
                        dve.tensor_reduce(own[:], masked[:].rearrange("p t h -> p (t h)"), AX.X, ALU.max).then_inc(final, 1)
                        dve.wait_ge(final, 4)
                        dve.tensor_scalar(gmax[:], whole[:], -1.0, None, ALU.mult).then_inc(final, 1)
                        dve.wait_ge(final, 5)

                    @block.gpsimd
                    def _(pool):
                        def fetch(i, k):
                            pool.wait_ge(index_staged, group(i, k) * 2 + 2)
                            pool.sem_inc(pool_turn, 1)
                            for j in range(G):
                                for to, table, index, done in ((proj, proj_tab, src_s, proj_in), (tgt, tgt_tab, dst_s, tgt_in)):
                                    pool.indirect_dma_start(
                                        to[k][:, j, :], None, table,
                                        bass.IndirectOffsetOnAxis(index[k][:, j:j + 1].bitcast(U32), 0),
                                    ).then_inc(done[k][j], 16)
                        pipeline(pool, pairs, (0, fetch))
                        pool.wait_ge(final, 3)
                        pool.partition_all_reduce(whole[:], own[:], P, bass.bass_isa.ReduceOp.max).then_inc(final, 1)

                    @block.sync
                    def _(sp):
                        def store(i, k):
                            n = group(i, k)
                            for j in range(G):
                                sp.wait_ge(proj_in[k][j], i * 16 + 16)
                            sp.dma_start(p_edge[bass.ds(n, 1)].squeeze(0).rearrange("p (j d) -> p j d", j=G), proj[k][:, :, 0:D]).then_inc(p_out[k], 16)
                        pipeline(sp, pairs, (0, store))
                        for s in p_out:
                            sp.wait_ge(s, 16 * pairs)
                free()

        def nodes_3():
            with ExitStack() as ctx:
                space = workspace(nc, ctx, "l3_nodes")
                sb, _, sem, free = space
                measure, root, balance, apply_norm, normed = norm_steps(space, "ln", half)
                ag = [sb(f"ag{k}", [P, G, D + H3]) for k in range(2)]
                den, per = ([sb(f"{n}{k}", [P, G, H3]) for k in range(2)] for n in ("den", "per"))
                xg, u, last_x = ([sb(f"{n}{k}", [P, G, D]) for k in range(2)] for n in ("xg", "u", "last_x"))
                a_in, x_in, x_out = ([sem(f"{n}{k}") for k in range(2)] for n in ("a_in", "x_in", "x_out"))
                raised, inverted, scaled, mixed = (sem(n) for n in ("raised", "inverted", "scaled", "mixed"))
                with nc.Block() as block:
                    @block.sync
                    def _(sp):
                        def load(i, k):
                            n = group(i, k)
                            if reuses(i):
                                sp.wait_ge(mixed, n - 1)
                            sp.dma_start(ag[k][:], by_group(agg3, D + H3)[bass.ds(n, 1)].squeeze(0)).then_inc(a_in[k], 16)
                            sp.dma_start(xg[k][:], by_group(x3b, D)[bass.ds(n, 1)].squeeze(0)).then_inc(x_in[k], 16)

                        def store(i, k):
                            n = group(i, k)
                            sp.wait_ge(normed, n * G + G)
                            sp.dma_start(by_group(out, D)[bass.ds(n, 1)].squeeze(0), last_x[k][:]).then_inc(x_out[k], 16)
                        pipeline(sp, pairs, (0, load), (2, store))
                        for s in x_out:
                            sp.wait_ge(s, 16 * pairs)

                    @block.vector
                    def _(dve):
                        def mix(i, k):
                            n = group(i, k)
                            dve.wait_ge(a_in[k], i * 16 + 16)
                            dve.tensor_scalar(den[k][:], ag[k][:, :, D:D + H3], 1e-16, None, ALU.add).then_inc(raised, 1)
                            dve.wait_ge(raised, n + 1)
                            dve.reciprocal(per[k][:], den[k][:]).then_inc(inverted, 1)
                            dve.wait_ge(inverted, n + 1)
                            if reuses(i):
                                dve.wait_ge(normed, n * G - G)
                            dve.tensor_tensor(u[k][:].rearrange("p j (h c) -> p j h c", c=C3),
                                              ag[k][:, :, 0:D].rearrange("p j (h c) -> p j h c", c=C3),
                                              per[k][:].unsqueeze(3).to_broadcast([P, G, H3, C3]), ALU.mult).then_inc(scaled, 1)
                            dve.wait_ge(scaled, n + 1)
                            dve.wait_ge(x_in[k], i * 16 + 16)
                            dve.tensor_tensor(u[k][:], u[k][:], xg[k][:], ALU.add).then_inc(mixed, 1)
                            dve.wait_ge(mixed, n + 1)
                            measure(dve, i, k, u[k])
                        pipeline(dve, pairs, (0, mix), (1, lambda i, k: balance(dve, i, k)))

                    @block.gpsimd
                    def _(pool):
                        pipeline(pool, pairs, (0, lambda i, k: root(pool, i, k)))

                    @block.scalar
                    def _(act):
                        def apply(i, k):
                            if reuses(i):
                                act.wait_ge(x_out[k], i * 16)
                            apply_norm(act, i, k, last_x[k], u[k])
                        pipeline(act, pairs, (0, apply))
                free()

        load_consts()
        load_weights()
        fill_records()
        order_consts("by_dst", dst_i[:], dkey, dprev, dwidx)
        sort_pass(0, sorted_a)
        sort_pass(8, sorted_b)
        order_consts("by_src", rec[:].bitcast(I32)[:, :, 2], skey, sprev, swidx)
        gather_sum_edges()
        nodes_0()
        edges_1a()
        edges_1b()
        nodes_1()
        edges_2a()
        turn_logits()
        segment_max()
        weigh_edges("l2_edges_b", agg2, H2, v_edge, C2 ** -0.5, None)
        nodes_2()
        edges_3a()
        weigh_edges("l3_edges_b", agg3, H3, p_edge, 1.0, gmax)
        nodes_3()


_WEIGHTS = ["L0_gnn_W", "L0_gnn_b", "L1_gnn_W1", "L1_gnn_b1", "L1_gnn_gamma", "L1_gnn_beta", "L1_gnn_W2", "L1_gnn_b2",
            "L2_gnn_Wq", "L2_gnn_bq", "L2_gnn_Wk", "L2_gnn_bk", "L2_gnn_Wv", "L2_gnn_bv", "L2_gnn_We", "L2_gnn_Wskip",
            "L2_gnn_bskip", "L2_gnn_g1", "L2_gnn_b1", "L2_gnn_g2", "L2_gnn_b2", "L2_gnn_Wf1", "L2_gnn_bf1",
            "L2_gnn_Wf2", "L2_gnn_bf2", "L3_gnn_W_proj", "L3_gnn_a_src", "L3_gnn_a_tgt", "L3_gnn_bias"]


def kernel(x, src, dst, edge_attr_2, edge_attr_64, **weights):
    import numpy as np
    import concourse.bacc as bacc
    from concourse.bass_utils import run_bass_kernel_spmd

    n_nodes, n_edges = np.shape(x)[0], np.shape(src)[0]
    pairs = -(-(max(n_nodes, n_edges) + 1) // (2 * GE))
    rows = 2 * GE * pairs
    tiles = rows // P

    def padded(a, fill):
        a = np.asarray(a)
        more = np.full((rows - a.shape[0],) + a.shape[1:], fill, a.dtype)
        return np.concatenate([a, more])

    def by_edge(a):
        return np.ascontiguousarray(np.swapaxes(a.reshape((tiles, P) + a.shape[1:]), 0, 1))

    src_p, dst_p = padded(src, rows - 1), padded(dst, rows - 1)
    edge = np.full((1,), -1, dst_p.dtype)
    arrays = {
        "in_x": padded(x, 0),
        "in_src": by_edge(src_p),
        "in_dst": by_edge(dst_p),
        "in_dst_line": np.concatenate([edge, dst_p, edge])[None],
        "in_ea2": by_edge(padded(edge_attr_2, 0)),
        "in_ea64": np.ascontiguousarray(np.swapaxes(padded(edge_attr_64, 0).reshape(rows // GE, GE, ED), 1, 2)),
    }
    for name in _WEIGHTS:
        arrays[f"in_{name}"] = np.ascontiguousarray(np.asarray(weights[name]))
    nc = bacc.Bacc("TRN2", target_bir_lowering=False, num_devices=1)
    aps = {name: nc.dram_tensor(name, a.shape, mybir.dt.from_np(a.dtype), kind="ExternalInput").ap()
           for name, a in arrays.items()}
    out = nc.dram_tensor("out_rows", (rows, D), F32, kind="ExternalOutput").ap()
    gnn(nc, *(aps[f"in_{n}"] for n in ("x", "src", "dst", "dst_line", "ea2", "ea64")),
        {n: aps[f"in_{n}"] for n in _WEIGHTS}, out, n_edges)
    result = run_bass_kernel_spmd(nc, [arrays], core_ids=[0])
    return result.results[0]["out_rows"][:n_nodes]
```

```python
from contextlib import ExitStack

import concourse.bass as bass
from concourse import mybir

F32 = mybir.dt.float32
BF16 = mybir.dt.bfloat16
I32 = mybir.dt.int32
U32 = mybir.dt.uint32
ALU = mybir.AluOpType
ACT = mybir.ActivationFunctionType
AX = mybir.AxisListType

P = 128
G = 4
GE = G * P
D = 128
H2, C2 = 8, 16
H3, C3 = 4, 32
ED = 64
SLICE = 2 * P
RING = 4
SKIP = 1 << 17
EPS = 1e-5
LOW = -3e38


def pipeline(eng, pairs, *stages):
    most = max(lag for lag, _ in stages)
    start = 1 + (most + 1) // 2
    for n in range(2 * start):
        for lag, step in stages:
            if n >= lag:
                step(*divmod(n - lag, 2))
    with eng.Fori(start, pairs) as i:
        for k in range(2):
            for lag, step in stages:
                step(i + (k - lag) // 2, (k - lag) % 2)
    for n in range(2 * pairs, 2 * pairs + most):
        for lag, step in stages:
            if n - lag < 2 * pairs:
                step(*divmod(n - lag, 2))


def rotation(eng, groups, *stages):
    least = min(lag for lag, _ in stages)
    stages = [(lag - least, step) for lag, step in stages]
    most = max(lag for lag, _ in stages)
    start = -(-(most + RING) // RING)
    whole = max(start, groups // RING)
    for n in range(start * RING):
        for lag, step in stages:
            if 0 <= n - lag < groups:
                step(*divmod(n - lag, RING))
    if whole > start:
        with eng.Fori(start, whole) as i:
            for k in range(RING):
                for lag, step in stages:
                    step(i + (k - lag) // RING, (k - lag) % RING)
    for n in range(whole * RING, groups + most):
        for lag, step in stages:
            if n - lag < groups:
                step(*divmod(n - lag, RING))


def place(i, k):
    return i * RING + k


def follows(i, k, m):
    return not (isinstance(i, int) and i * RING + k < m)


def before(i, k):
    return (i, 0) if k else (i - 1, 1)


def is_first(i, k):
    return isinstance(i, int) and i == 0 and k == 0


def reuses(i):
    return not (isinstance(i, int) and i == 0)


def group(i, k):
    return i * 2 + k


def workspace(nc, ctx, name):
    sems = []

    def sb(n, shape, dt=F32):
        return ctx.enter_context(nc.sbuf_tensor(f"{name}_{n}", shape, dt))

    def ps(n, shape):
        return ctx.enter_context(nc.psum_tensor(f"{name}_{n}", shape, F32))

    def sem(n):
        made = nc.alloc_semaphore(name=f"{name}_{n}")
        sems.append(made)
        return made

    def free():
        nc.clear_and_free_semaphores(sems)
        nc.all_engine_barrier()
    return sb, ps, sem, free


def segment_steps(space, key, prev, widx, table, width, ident, nodes):
    sb, ps, sem, _ = space

    keys = [sb(f"keys{k}", [P, G]) for k in range(2)]
    same = [sb(f"same{k}", [P, G, P]) for k in range(2)]
    carry = [sb(f"carry{k}", [P, G, P]) for k in range(2)]
    rows = [sb(f"rows{k}", [P, G, width]) for k in range(2)]
    at = [sb(f"at{k}", [P, G], I32) for k in range(2)]
    keys_t = [ps(f"keys_t{k}", [P, G, P]) for k in range(2)]
    sums = [ps(f"sums{j}", [P, 512]) for j in range(G)]
    keys_staged = sem("keys_staged")
    keys_turned = sem("keys_turned")
    compared = sem("compared")
    summed = sem("summed")
    evacuated = sem("evacuated")
    at_staged = sem("at_staged")
    pool_turn = sem("scatter_turn")
    scattered = [[sem(f"scattered{k}{j}") for j in range(G)] for k in range(2)]

    def stage_keys(dve, i, k):
        n = group(i, k)
        if reuses(i):
            dve.wait_ge(compared, n * 2 - 2)
        dve.tensor_copy(keys[k][:], key[:, bass.ds(n * G, G)]).then_inc(keys_staged, 1)

    def turn_keys(pe, i, k):
        n = group(i, k)
        pe.wait_ge(keys_staged, n + 1)
        for j in range(G):
            last = pe.transpose(keys_t[k][:, j, :], keys[k][:, j:j + 1].to_broadcast([P, P]),
                                ident[:])
        last.then_inc(keys_turned, 1)

    def compare(dve, i, k):
        n = group(i, k)
        dve.wait_ge(keys_turned, n + 1)
        if reuses(i):
            dve.wait_ge(summed, n * G - G)
        own = key[:, bass.ds(n * G, G)].unsqueeze(2).to_broadcast([P, G, P])
        closing = prev[:, bass.ds(n * G, G)].unsqueeze(2).to_broadcast([P, G, P])
        dve.tensor_tensor(same[k][:], keys_t[k][:], own, ALU.is_equal).then_inc(compared, 1)
        dve.tensor_tensor(carry[k][:], keys_t[k][:], closing, ALU.is_equal).then_inc(compared, 1)

    def total(pe, i, k, messages):
        n = group(i, k)
        pe.wait_ge(compared, n * 2 + 2)
        for j in range(G):
            out = sums[j][:, 0:width]
            first = is_first(i, k) and j == 0
            ins = pe.matmul(out, same[k][:, j, :], messages[:, j, :], start=True, stop=first)
            if not first:
                pe.wait_ge(evacuated, n * G + j)
                pi, pk = (i, k) if j else before(i, k)
                ins = pe.matmul(out, carry[k][:, j, :], rows[pk][:, (j - 1) % G, :],
                                start=False, stop=True)
            ins.then_inc(summed, 1)

    def empty(act, i, k):
        n = group(i, k)
        if reuses(i):
            for j in range(G):
                act.wait_ge(scattered[k][j], i * 16)
        act.copy(at[k][:], widx[:, bass.ds(n * G, G)]).then_inc(at_staged, 1)
        for j in range(G):
            act.wait_ge(summed, n * G + j + 1)
            act.copy(rows[k][:, j, :], sums[j][:, 0:width]).then_inc(evacuated, 1)

    def scatter(pool, i, k):
        n = group(i, k)
        pool.wait_ge(at_staged, n + 1)
        pool.sem_inc(pool_turn, 1)
        pool.wait_ge(evacuated, n * G + G)
        pool.sem_inc(pool_turn, 1)
        for j in range(G):
            pool.indirect_dma_start(
                table, bass.IndirectOffsetOnAxis(at[k][:, j:j + 1].bitcast(U32), 0),
                rows[k][:, j, :], None, bounds_check=nodes - 1, oob_is_err=False,
            ).then_inc(scattered[k][j], 16)

    def settle(pool, pairs):
        for k in range(2):
            for j in range(G):
                pool.wait_ge(scattered[k][j], 16 * pairs)

    return stage_keys, turn_keys, compare, total, empty, scatter, settle, summed


def norm_steps(space, name, half):
    def sb(n, s):
        return [space[0](f"{name}_{n}{k}", s) for k in range(RING)]

    def sem(n):
        return space[2](f"{name}_{n}")

    stats, moments = sb("stats", [P, G, 6]), sb("moments", [P, G, 2])
    spread, rstd, shift = sb("spread", [P, G, 1]), sb("rstd", [P, G, 1]), sb("shift", [P, G, 1])
    s_stats, s_moments, s_spread = sem("s_stats"), sem("s_moments"), sem("s_spread")
    s_rstd, s_shift, normed, turn = sem("s_rstd"), sem("s_shift"), sem("normed"), sem("turn")

    def measure(dve, i, k, u):
        n = place(i, k)
        if reuses(i):
            dve.wait_ge(normed, (n - RING + 1) * G)
        for j in range(G):
            dve.bn_stats(stats[k][:, j, :], u[:, j, :]).then_inc(s_stats, 1)
        for j in range(G):
            dve.wait_ge(s_stats, n * G + j + 1)
            dve.sem_inc(turn, 1)
            dve.bn_aggr(moments[k][:, j, :], stats[k][:, j, :]).then_inc(s_moments, 1)
        dve.wait_ge(s_moments, n * G + G)
        dve.tensor_scalar(spread[k][:], moments[k][:, :, 1:2], EPS, None, ALU.add).then_inc(s_spread, 1)

    def root(pool, i, k):
        n = place(i, k)
        pool.wait_ge(s_spread, n + 1)
        pool.tensor_tensor(rstd[k][:], spread[k][:], half[:].unsqueeze(2), ALU.pow).then_inc(s_rstd, 1)

    def balance(dve, i, k):
        n = place(i, k)
        dve.wait_ge(s_rstd, n + 1)
        dve.scalar_tensor_tensor(shift[k][:], moments[k][:, :, 0:1], -1.0, rstd[k][:],
                                 ALU.mult, ALU.mult).then_inc(s_shift, 1)

    def apply(act, i, k, out, u):
        n = place(i, k)
        act.wait_ge(s_shift, n + 1)
        for j in range(G):
            act.activation(out[:, j, :], u[:, j, :], ACT.Identity, bias=shift[k][:, j, :],
                           scale=rstd[k][:, j, :]).then_inc(normed, 1)

    return measure, root, balance, apply, normed


def gnn(nc, x, src, dst, dst_line, ea2, ea64, w, out, n_edges):
    nodes = x.shape[0]
    tiles = src.shape[1]
    edges = tiles * P
    groups = tiles // G
    pairs = groups // 2
    pad_node = nodes - 1
    assert nodes == groups * GE and groups % 2 == 0 and pairs > 3

    top = ExitStack()
    with top:
        def dram(name, shape, dt=F32):
            return nc.dram_tensor(name, shape, dt).ap()

        def sb0(name, shape, dt=F32):
            return top.enter_context(nc.sbuf_tensor(name, shape, dt))

        def all_out(eng, *queues):
            for queue in queues:
                for k in range(RING):
                    eng.wait_ge(queue[k], 16 * len(range(k, groups, RING)))

        agg0 = dram("agg0", [nodes, D])
        agg1 = [dram(f"agg1{s}", [nodes + SLICE, D + 1]) for s in range(2)]
        agg2, agg3 = dram("agg2", [nodes, D + H2]), dram("agg3", [nodes, D + H3])
        x1, x2b, x3b = dram("x1", [nodes, D]), dram("x2b", [nodes, D]), dram("x3b", [nodes, D])
        to_row, to_col = dram("to_row", [nodes, D]), dram("to_col", [nodes, D])
        q_tab, kv_tab, skip_tab = dram("q_tab", [nodes, D]), dram("kv_tab", [nodes, 2 * D]), dram("skip_tab", [nodes, D])
        proj_tab, tgt_tab = dram("proj_tab", [nodes, D + H3]), dram("tgt_tab", [nodes, H3])
        h_t = dram("h_t", [groups, P, GE])
        v_edge, p_edge = dram("v_edge", [groups, P, GE]), dram("p_edge", [groups, P, GE])
        logit_t, max_t = dram("logit_t", [tiles, H2, P]), dram("max_t", [tiles, H2, P])
        chunks = max(c for c in range(1, P // H2 + 1) if tiles % c == 0)
        ends, starts = dram("ends", [2, 2, chunks * H2]), dram("starts", [2, chunks * H2])

        def by_group(t, width):
            return t.rearrange("(g p j) d -> g p j d", p=P, j=G)

        ident = sb0("ident", [P, P])
        half = sb0("half", [P, G])
        is_last = sb0("is_last", [P, 1])
        dst_i, src_i = sb0("dst_i", [P, tiles], I32), sb0("src_i", [P, tiles], I32)
        dkey, dprev, dwidx = sb0("dkey", [P, tiles]), sb0("dprev", [P, tiles]), sb0("dwidx", [P, tiles], I32)
        skey, sidx = sb0("skey", [P, tiles]), sb0("sidx", [P, tiles], I32)
        scores = sb0("scores", [P, tiles * H2])
        gmax = sb0("gmax", [P, 1])

        zeros = sb0("zeros", [P, 8 * (D + H2)])
        agg0_zeroed = nc.alloc_semaphore(name="agg0_zeroed")

        def zero_rows(eng, table, at, done):
            view = table[0:nodes].rearrange("(g p j) d -> g p (j d)", p=P, j=8)
            eng.dma_start(view[bass.ds(at, 1)].squeeze(0), zeros[:, 0:8 * table.shape[1]]).then_inc(done, 16)

        def load_consts():
            with ExitStack() as ctx:
                space = workspace(nc, ctx, "consts")
                _, _, sem, free = space
                made, loaded, zero_made = sem("made"), [sem(f"loaded{m}") for m in range(2)], sem("zero_made")
                with nc.Block() as block:
                    @block.gpsimd
                    def _(pool):
                        pool.memset(ident[:], 0.0).then_inc(made, 1)
                        pool.memset(is_last[:], 0.0).then_inc(made, 1)
                        pool.memset(half[:], -0.5).then_inc(made, 1)
                        pool.wait_ge(made, 3)
                        pool.affine_select(out=ident[:], in_=ident[:], compare_op=ALU.not_equal, fill=1.0, base=0,
                                           pattern=[[-1, P]], channel_multiplier=1).then_inc(made, 1)
                        pool.affine_select(out=is_last[:], in_=is_last[:], compare_op=ALU.not_equal, fill=1.0,
                                           base=1 - P, pattern=[[0, 1]], channel_multiplier=1).then_inc(made, 1)
                        pool.wait_ge(made, 5)

                    @block.vector
                    def _(dve):
                        dve.memset(zeros[:], 0.0).then_inc(zero_made, 1)

                    @block.sync
                    def _(sp):
                        sp.dma_start(dst_i[:], dst).then_inc(loaded[0], 16)
                        sp.dma_start(src_i[:], src).then_inc(loaded[1], 16)
                        for s in loaded:
                            sp.wait_ge(s, 16)

                    @block.scalar
                    def _(act):
                        act.wait_ge(zero_made, 1)
                        for m in range(pairs):
                            zero_rows(act, agg0, m, agg0_zeroed)
                free()

        def order_consts():
            with ExitStack() as ctx:
                space = workspace(nc, ctx, "order")
                sb, _, sem, free = space
                nxt = sb("nxt", [P, tiles])
                drop = sb("drop", [P, tiles])
                off = sb("off", [P, 1])
                step, moved, key_ready = sem("step"), [sem("moved0"), sem("moved1")], sem("key_ready")
                with nc.Block() as block:
                    @block.vector
                    def _(dve):
                        dve.memset(nxt[:], -1.0).then_inc(key_ready, 1)
                        dve.tensor_copy(dkey[:], dst_i[:]).then_inc(key_ready, 1)
                        dve.memset(dprev[:], -1.0).then_inc(step, 1)
                        dve.tensor_scalar(off[:], is_last[:], 1.0, None, ALU.subtract).then_inc(step, 1)
                        dve.wait_ge(step, 2)
                        dve.wait_ge(key_ready, 2)
                        dve.tensor_scalar(dprev[:, 1:], dkey[:, :tiles - 1], is_last[:], off[:], ALU.mult,
                                          ALU.add).then_inc(step, 1)
                        for s in moved:
                            dve.wait_ge(s, 16)
                        dve.tensor_tensor(drop[:], dkey[:], nxt[:], ALU.is_equal).then_inc(step, 1)
                        dve.wait_ge(step, 4)
                        dve.scalar_tensor_tensor(nxt[:], drop[:], float(SKIP), dkey[:], ALU.mult,
                                                 ALU.add).then_inc(step, 1)
                        dve.wait_ge(step, 5)
                        dve.tensor_copy(dwidx[:], nxt[:]).then_inc(step, 1)
                        dve.tensor_copy(skey[:], src_i[:]).then_inc(step, 1)
                        dve.wait_ge(step, 7)

                    @block.sync
                    def _(sp):
                        sp.wait_ge(key_ready, 2)
                        sp.dma_start(nxt[0:P - 1, :], dkey[1:P, :]).then_inc(moved[0], 16)
                        sp.dma_start(nxt[P - 1:P, 0:tiles - 1], dkey[0:1, 1:tiles]).then_inc(moved[1], 16)
                        for s in moved:
                            sp.wait_ge(s, 16)
                free()

        def gather_sum_edges():
            with ExitStack() as ctx:
                space = workspace(nc, ctx, "l0_edges")
                sb, ps, sem, free = space
                stage_keys, turn_keys, compare, total, empty, scatter, settle, summed = segment_steps(
                    space, dkey, dprev, dwidx, agg0, D, ident, nodes)
                fetched = [sb(f"fetched{k}", [P, G, D]) for k in range(2)]
                index = [sb(f"index{k}", [P, G], I32) for k in range(2)]
                index_staged, pool_turn, cleared = sem("index_staged"), sem("pool_turn"), sem("cleared")
                gathered = [[sem(f"gathered{k}{j}") for j in range(G)] for k in range(2)]
                with nc.Block() as block:
                    @block.vector
                    def _(dve):
                        def step(i, k):
                            n = group(i, k)
                            if reuses(i):
                                dve.wait_ge(summed, n * G - G)
                            dve.tensor_copy(index[k][:], src_i[:, bass.ds(n * G, G)]).then_inc(index_staged, 1)
                            stage_keys(dve, i, k)
                            compare(dve, i, k)
                        pipeline(dve, pairs, (0, step))

                    @block.gpsimd
                    def _(pool):
                        def step(i, k):
                            pool.wait_ge(index_staged, group(i, k) + 1)
                            pool.sem_inc(pool_turn, 1)
                            for j in range(G):
                                pool.indirect_dma_start(
                                    fetched[k][:, j, :], None, x,
                                    bass.IndirectOffsetOnAxis(index[k][:, j:j + 1].bitcast(U32), 0),
                                ).then_inc(gathered[k][j], 16)
                        pipeline(pool, pairs, (0, step), (1, lambda i, k: scatter(pool, i, k)))
                        settle(pool, pairs)

                    @block.tensor
                    def _(pe):
                        def step(i, k):
                            turn_keys(pe, i, k)
                            for j in range(G):
                                pe.wait_ge(gathered[k][j], i * 16 + 16)
                            total(pe, i, k, fetched[k])
                        pipeline(pe, pairs, (0, step))

                    @block.scalar
                    def _(act):
                        pipeline(act, pairs, (0, lambda i, k: empty(act, i, k)))

                    @block.sync
                    def _(sp):
                        def clear(i, k):
                            sp.wait_ge(index_staged, group(i, k) + 1)
                            for table in (agg1 if k else (agg2, agg3)):
                                zero_rows(sp, table, i, cleared)
                        for table in agg1:
                            sp.dma_start(table[nodes:].rearrange("(p j) d -> p (j d)", p=P),
                                         zeros[:, 0:SLICE // P * (D + 1)]).then_inc(cleared, 16)
                        pipeline(sp, pairs, (0, clear))
                        sp.wait_ge(cleared, 16 * (4 * pairs + 2))
                free()

        w0_t = sb0("w0_t", [P, D])
        w1_ab, w1_c, w1_2 = sb0("w1_ab", [P, 2 * D]), sb0("w1_c", [2, D]), sb0("w1_2", [P, D])
        w_qkvs, w_e = sb0("w_qkvs", [P, 4 * D]), sb0("w_e", [ED, D])
        w_f1, w_f2 = sb0("w_f1", [P, 4 * D]), sb0("w_f2", [P, 4, D])
        w_proj = sb0("w_proj", [P, D + 2 * H3])
        b_0, b_11, b_12 = sb0("b_0", [P, D]), sb0("b_11", [P, D]), sb0("b_12", [P, D])
        b_qkvs, b_f2, g_2, b_2, b_3 = (sb0(n, [P, m * D]) for n, m in (
            ("b_qkvs", 4), ("b_f2", 1), ("g_2", 1), ("b_2", 1), ("b_3", 1)))
        gamma, beta, g_1, b_1, b_f1 = (sb0(n, [P, m]) for n, m in (
            ("gamma", 1), ("beta", 1), ("g_1", 1), ("b_1", 1), ("b_f1", 4)))
        bn_scale, bn_shift = sb0("bn_scale", [P, 1]), sb0("bn_shift", [P, 1])

        def load_weights():
            with ExitStack() as ctx:
                space = workspace(nc, ctx, "weights")
                sb, ps, sem, free = space
                w0, proj_t, attend = sb("w0", [P, D]), sb("proj_t", [P, D]), sb("attend", [P, 2 * H3])
                turned, mixed = ps("turned", [P, 2, P]), ps("mixed", [P, 2 * H3])
                loaded, cleared, attend_loaded = sem("loaded"), sem("cleared"), sem("attend_loaded")
                s_turned, s_copied, s_mixed, s_done = sem("s_turned"), sem("s_copied"), sem("s_mixed"), sem("s_done")

                def row(name):
                    return w[name].rearrange("(a n) -> a n", a=1).to_broadcast([P, D])

                def column(name, m=1):
                    return w[name].rearrange("(m p) -> p m", p=P)
                plain = [(w0[:], w["L0_gnn_W"]), (w1_ab[:, 0:D], w["L1_gnn_W1"][0:D, :]),
                         (w1_ab[:, D:2 * D], w["L1_gnn_W1"][D:2 * D, :]), (w1_c[:], w["L1_gnn_W1"][2 * D:2 * D + 2, :]),
                         (w1_2[:], w["L1_gnn_W2"]), (w_e[:], w["L2_gnn_We"]), (w_f1[:], w["L2_gnn_Wf1"]),
                         (w_f2[:], w["L2_gnn_Wf2"].rearrange("(c p) n -> p c n", p=P)),
                         (w_proj[:, 0:D], w["L3_gnn_W_proj"]),
                         (b_0[:], row("L0_gnn_b")), (b_11[:], row("L1_gnn_b1")), (b_12[:], row("L1_gnn_b2")),
                         (b_f2[:], row("L2_gnn_bf2")), (g_2[:], row("L2_gnn_g2")), (b_2[:], row("L2_gnn_b2")),
                         (b_3[:], row("L3_gnn_bias"))]
                for m, n in enumerate(("q", "k", "v", "skip")):
                    plain.append((w_qkvs[:, m * D:(m + 1) * D], w[f"L2_gnn_W{n}"]))
                    plain.append((b_qkvs[:, m * D:(m + 1) * D], row(f"L2_gnn_b{n}")))
                columns = [(gamma, "L1_gnn_gamma"), (beta, "L1_gnn_beta"), (g_1, "L2_gnn_g1"), (b_1, "L2_gnn_b1"),
                           (b_f1, "L2_gnn_bf1")]
                total = 16 * (len(plain) + len(columns))
                with nc.Block() as block:
                    @block.sync
                    def _(sp):
                        for to, frm in plain:
                            sp.dma_start(to, frm).then_inc(loaded, 16)
                        with nc.allow_non_contiguous_dma(reason="short columns, once"):
                            for to, name in columns:
                                sp.dma_start(to[:], column(name)).then_inc(loaded, 16)
                            sp.wait_ge(cleared, 1)
                            for m, name in enumerate(("L3_gnn_a_src", "L3_gnn_a_tgt")):
                                for h in range(H3):
                                    sp.dma_start(attend[h * C3:(h + 1) * C3, m * H3 + h:m * H3 + h + 1],
                                                 w[name][0, h, :].rearrange("(c a) -> c a", a=1)).then_inc(attend_loaded, 16)
                        sp.wait_ge(loaded, total)
                        sp.wait_ge(attend_loaded, 16 * 2 * H3)

                    @block.vector
                    def _(dve):
                        dve.memset(attend[:], 0.0).then_inc(cleared, 1)
                        dve.wait_ge(loaded, total)
                        dve.tensor_tensor(w_qkvs[:, 3 * D:4 * D], w_qkvs[:, 3 * D:4 * D], ident[:], ALU.add).then_inc(s_done, 1)
                        dve.wait_ge(s_turned, 2)
                        dve.tensor_copy(w0_t[:], turned[:, 0, :]).then_inc(s_copied, 1)
                        dve.tensor_copy(proj_t[:], turned[:, 1, :]).then_inc(s_copied, 1)
                        dve.wait_ge(s_mixed, 1)
                        dve.tensor_copy(w_proj[:, D:D + 2 * H3], mixed[:]).then_inc(s_done, 1)
                        dve.wait_ge(s_done, 2)

                    @block.scalar
                    def _(act):
                        act.wait_ge(agg0_zeroed, 16 * pairs)

                    @block.tensor
                    def _(pe):
                        pe.wait_ge(loaded, total)
                        pe.transpose(turned[:, 0, :], w0[:], ident[:]).then_inc(s_turned, 1)
                        pe.transpose(turned[:, 1, :], w_proj[:, 0:D], ident[:]).then_inc(s_turned, 1)
                        pe.wait_ge(s_copied, 2)
                        pe.wait_ge(attend_loaded, 16 * 2 * H3)
                        pe.matmul(mixed[:], proj_t[:], attend[:], start=True, stop=True).then_inc(s_mixed, 1)
                nc.clear_and_free_semaphores([agg0_zeroed])
                free()

        def nodes_0():
            with ExitStack() as ctx:
                space = workspace(nc, ctx, "l0_nodes")
                sb, ps, sem, free = space
                measure, root, balance, apply_norm, normed = norm_steps(space, "ln", half)
                xg, ag, ag_t, u, x1s, x1_t, row_s, col_s = (
                    [sb(f"{n}{k}", [P, G, D]) for k in range(RING)]
                    for n in ("xg", "ag", "ag_t", "u", "x1s", "x1_t", "row_s", "col_s"))
                turn_a, turn_b = ps("turn_a", [P, G, P]), ps("turn_b", [P, G, P])
                y, row_p, col_p = ([ps(f"{n}{m}", [P, G, D]) for m in range(2)] for n in ("y", "row_p", "col_p"))
                x_in, a_in, x1_out, row_out, col_out = (
                    [sem(f"{n}{k}") for k in range(RING)] for n in ("x_in", "a_in", "x1_out", "row_out", "col_out"))
                a_turned, a_copied, y_done, biased, mixed = (
                    sem(n) for n in ("a_turned", "a_copied", "y_done", "biased", "mixed"))
                x_turned, x_copied, ab_done, row_done, col_done = (
                    sem(n) for n in ("x_turned", "x_copied", "ab_done", "row_done", "col_done"))
                with nc.Block() as block:
                    @block.sync
                    def _(sp):
                        def load(i, k):
                            n = place(i, k)
                            if reuses(i):
                                sp.wait_ge(a_turned, n - RING + 1)
                            sp.dma_start(ag[k][:], by_group(agg0, D)[bass.ds(n, 1)].squeeze(0)).then_inc(a_in[k], 16)
                            if reuses(i):
                                sp.wait_ge(mixed, n - RING + 1)
                            sp.dma_start(xg[k][:], by_group(x, D)[bass.ds(n, 1)].squeeze(0)).then_inc(x_in[k], 16)

                        def store(i, k):
                            n = place(i, k)
                            sp.wait_ge(normed, n * G + G)
                            sp.dma_start(by_group(x1, D)[bass.ds(n, 1)].squeeze(0), x1s[k][:]).then_inc(x1_out[k], 16)
                            sp.wait_ge(row_done, n + 1)
                            sp.dma_start(by_group(to_row, D)[bass.ds(n, 1)].squeeze(0), row_s[k][:]).then_inc(row_out[k], 16)
                            sp.wait_ge(col_done, n + 1)
                            sp.dma_start(by_group(to_col, D)[bass.ds(n, 1)].squeeze(0), col_s[k][:]).then_inc(col_out[k], 16)
                        rotation(sp, groups, (0, load), (7, store))
                        all_out(sp, x1_out, row_out, col_out)

                    @block.tensor
                    def _(pe):
                        def turn(i, k):
                            n = place(i, k)
                            pe.wait_ge(a_in[k], i * 16 + 16)
                            if follows(i, k, 1):
                                pe.wait_ge(a_copied, n)
                            for j in range(G):
                                last = pe.transpose(turn_a[:, j, :], ag[k][:, j, :], ident[:])
                            last.then_inc(a_turned, 1)

                        def project(i, k):
                            n = place(i, k)
                            pe.wait_ge(a_copied, n + 1)
                            if follows(i, k, 2):
                                pe.wait_ge(biased, n - 1)
                            for j in range(G):
                                last = pe.matmul(y[k % 2][:, j, :], ag_t[k][:, j, :], w0_t[:], start=True, stop=True)
                            last.then_inc(y_done, 1)

                        def turn_x1(i, k):
                            n = place(i, k)
                            pe.wait_ge(normed, n * G + G)
                            if follows(i, k, 1):
                                pe.wait_ge(x_copied, n)
                            for j in range(G):
                                last = pe.transpose(turn_b[:, j, :], x1s[k][:, j, :], ident[:])
                            last.then_inc(x_turned, 1)

                        def project_x1(i, k):
                            n = place(i, k)
                            pe.wait_ge(x_copied, n + 1)
                            if follows(i, k, 2):
                                pe.wait_ge(row_done, n - 1)
                                pe.wait_ge(col_done, n - 1)
                            for j in range(G):
                                pe.matmul(row_p[k % 2][:, j, :], x1_t[k][:, j, :], w1_ab[:, 0:D], start=True, stop=True)
                                last = pe.matmul(col_p[k % 2][:, j, :], x1_t[k][:, j, :], w1_ab[:, D:2 * D], start=True, stop=True)
                            last.then_inc(ab_done, 1)
                        rotation(pe, groups, (1, turn), (4, turn_x1), (2, project), (5, project_x1))

                    @block.vector
                    def _(dve):
                        def mix(i, k):
                            n = place(i, k)
                            dve.wait_ge(y_done, n + 1)
                            if reuses(i):
                                dve.wait_ge(normed, (n - RING + 1) * G)
                            dve.tensor_tensor(u[k][:], y[k % 2][:], b_0[:].unsqueeze(1).to_broadcast([P, G, D]),
                                              ALU.add).then_inc(biased, 1)
                            dve.wait_ge(x_in[k], i * 16 + 16)
                            dve.wait_ge(biased, n + 1)
                            dve.scalar_tensor_tensor(u[k][:], u[k][:], 0.0, xg[k][:], ALU.max, ALU.add).then_inc(mixed, 1)
                            dve.wait_ge(mixed, n + 1)
                            measure(dve, i, k, u[k])

                        def row(i, k):
                            n = place(i, k)
                            dve.wait_ge(ab_done, n + 1)
                            if reuses(i):
                                dve.wait_ge(row_out[k], i * 16)
                            dve.tensor_tensor(row_s[k][:], row_p[k % 2][:], b_11[:].unsqueeze(1).to_broadcast([P, G, D]),
                                              ALU.add).then_inc(row_done, 1)
                        rotation(dve, groups, (3, lambda i, k: balance(dve, i, k)), (6, row), (2, mix))

                    @block.gpsimd
                    def _(pool):
                        rotation(pool, groups, (0, lambda i, k: root(pool, i, k)))

                    @block.scalar
                    def _(act):
                        def copy_a(i, k):
                            n = place(i, k)
                            act.wait_ge(a_turned, n + 1)
                            if reuses(i):
                                act.wait_ge(y_done, n - RING + 1)
                            act.copy(ag_t[k][:], turn_a[:]).then_inc(a_copied, 1)

                        def copy_x1(i, k):
                            n = place(i, k)
                            act.wait_ge(x_turned, n + 1)
                            if reuses(i):
                                act.wait_ge(ab_done, n - RING + 1)
                            act.copy(x1_t[k][:], turn_b[:]).then_inc(x_copied, 1)

                        def col(i, k):
                            n = place(i, k)
                            act.wait_ge(ab_done, n + 1)
                            if reuses(i):
                                act.wait_ge(col_out[k], i * 16)
                            act.copy(col_s[k][:], col_p[k % 2][:]).then_inc(col_done, 1)

                        def apply(i, k):
                            n = place(i, k)
                            if reuses(i):
                                act.wait_ge(x1_out[k], i * 16)
                                act.wait_ge(x_turned, n - RING + 1)
                            apply_norm(act, i, k, x1s[k], u[k])
                        rotation(act, groups, (1, copy_a), (4, copy_x1), (3, apply), (6, col))
                free()

        def edges_1a():
            valid = n_edges - (groups - 1) * GE
            with ExitStack() as ctx:
                space = workspace(nc, ctx, "l1_edges_a")
                sb, ps, sem, free = space
                row_i, col_i = ([sb(f"{n}{k}", [P, G], I32) for k in range(2)] for n in ("row_i", "col_i"))
                ea_t = [sb(f"ea_t{k}", [2, GE]) for k in range(2)]
                keys = [sb(f"keys{k}", [P, G]) for k in range(2)]
                keys_t = [ps(f"keys_t{k}", [P, G, P]) for k in range(2)]
                weight, own, spare = sb("weight", [P, SLICE]), sb("own", [P, G]), sb("spare", [P, G])
                heavy = [sb(f"heavy{k}", [P, G, SLICE]) for k in range(2)]
                heaviest, gap = sb("heaviest", [P, tiles]), sb("gap", [P, tiles])
                at_row, at_col, both, h_s = ([sb(f"{n}{k}", [P, G, D]) for k in range(2)]
                                             for n in ("at_row", "at_col", "both", "h_s"))
                stats, moments, spread, rstd = sb("stats", [P, groups, 6]), sb("moments", [P, 2]), sb("spread", [P, 1]), sb("rstd", [P, 1])
                h = [ps(f"h{k}", [P, G, P]) for k in range(2)]
                index_staged, added, keys_staged, keys_turned, matched, picked, numbered = (
                    sem(n) for n in ("index_staged", "added", "keys_staged", "keys_turned", "matched", "picked", "numbered"))
                ea_in = [sem("ea_in0"), sem("ea_in1")]
                h_done, h_copied, measured, pool_turn, final = (
                    sem(n) for n in ("h_done", "h_copied", "measured", "pool_turn", "final"))
                row_in = [[sem(f"row_in{k}{j}") for j in range(G)] for k in range(2)]
                col_in = [[sem(f"col_in{k}{j}") for j in range(G)] for k in range(2)]
                h_out = [sem("h_out0"), sem("h_out1")]
                with nc.Block() as block:
                    @block.vector
                    def _(dve):
                        def stage(i, k):
                            n = group(i, k)
                            if reuses(i):
                                dve.wait_ge(added, n - 1)
                            dve.tensor_copy(row_i[k][:], src_i[:, bass.ds(n * G, G)]).then_inc(index_staged, 1)
                            dve.tensor_copy(col_i[k][:], dst_i[:, bass.ds(n * G, G)]).then_inc(index_staged, 1)
                            if reuses(i):
                                dve.wait_ge(keys_turned, n - 1)
                                dve.wait_ge(matched, n * G - G)
                            dve.tensor_copy(keys[k][:], skey[:, bass.ds(n * G, G)]).then_inc(keys_staged, 1)

                        def add(i, k):
                            n = group(i, k)
                            if reuses(i):
                                dve.wait_ge(h_done, n - 1)
                            for j in range(G):
                                dve.wait_ge(row_in[k][j], i * 16 + 16)
                                dve.wait_ge(col_in[k][j], i * 16 + 16)
                            dve.tensor_tensor(both[k][:], at_row[k][:], at_col[k][:], ALU.add).then_inc(added, 1)

                        def match(i, k):
                            n = group(i, k)
                            dve.wait_ge(keys_turned, n + 1)
                            if reuses(i):
                                dve.wait_ge(picked, n - 1)
                            for j in range(G):
                                at = j - j % 2
                                dve.scalar_tensor_tensor(
                                    heavy[k][:, j, :], keys_t[k][:, at:at + 2, :].rearrange("p j e -> p (j e)"), keys[k][:, j:j + 1],
                                    weight[:], ALU.is_equal, ALU.mult).then_inc(matched, 1)

                        def pick(i, k):
                            n = group(i, k)
                            dve.wait_ge(matched, n * G + G)
                            dve.tensor_reduce(heaviest[:, bass.ds(n * G, G)], heavy[k][:], AX.X, ALU.max).then_inc(picked, 1)

                        def measure(i, k):
                            n = group(i, k)
                            dve.wait_ge(h_copied, n + 1)
                            dve.bn_stats(stats[:, bass.ds(n, 1), :].squeeze(1), h_s[k][:].rearrange("p j e -> p (j e)")
                                         ).then_inc(measured, 1)
                        dve.wait_ge(numbered, 3)
                        pipeline(dve, pairs, (0, stage), (1, add), (0, match), (1, measure), (0, pick))
                        dve.wait_ge(picked, groups)
                        by_slot = "p (g j) -> p g j"
                        own_all = own[:].unsqueeze(1).to_broadcast([P, groups, G])
                        spare_all = spare[:].unsqueeze(1).to_broadcast([P, groups, G])
                        dve.tensor_tensor(heaviest[:].rearrange(by_slot, j=G), heaviest[:].rearrange(by_slot, j=G),
                                          own_all, ALU.is_equal).then_inc(picked, 1)
                        dve.tensor_tensor(gap[:].rearrange(by_slot, j=G), skey[:].rearrange(by_slot, j=G), spare_all,
                                          ALU.subtract).then_inc(picked, 1)
                        dve.wait_ge(picked, groups + 2)
                        dve.tensor_tensor(gap[:], gap[:], heaviest[:], ALU.mult).then_inc(picked, 1)
                        dve.wait_ge(picked, groups + 3)
                        dve.tensor_tensor(sidx[:].rearrange(by_slot, j=G), gap[:].rearrange(by_slot, j=G), spare_all,
                                          ALU.add).then_inc(picked, 1)
                        dve.wait_ge(picked, groups + 4)
                        dve.wait_ge(measured, groups)
                        dve.wait_ge(h_copied, groups)
                        dve.bn_stats(stats[:, groups - 1, :], h_s[1][:].rearrange("p j e -> p (j e)")[:, 0:valid]).then_inc(final, 1)
                        dve.wait_ge(final, 1)
                        dve.bn_aggr(moments[:], stats[:].rearrange("p g s -> p (g s)")).then_inc(final, 1)
                        dve.wait_ge(final, 2)
                        dve.tensor_scalar(spread[:], moments[:, 1:2], EPS, None, ALU.add).then_inc(final, 1)
                        dve.wait_ge(final, 4)
                        dve.tensor_tensor(bn_scale[:], gamma[:], rstd[:], ALU.mult).then_inc(final, 1)
                        dve.wait_ge(final, 5)
                        dve.tensor_tensor(spread[:], moments[:, 0:1], bn_scale[:], ALU.mult).then_inc(final, 1)
                        dve.wait_ge(final, 6)
                        dve.tensor_tensor(bn_shift[:], beta[:], spread[:], ALU.subtract).then_inc(final, 1)
                        dve.wait_ge(final, 7)

                    @block.gpsimd
                    def _(pool):
                        exact = {"allow_small_or_imprecise_dtypes": True}
                        pool.iota(weight[:], [[-1, SLICE]], base=SLICE, channel_multiplier=0, **exact).then_inc(numbered, 1)
                        pool.iota(own[:], [[0, G // 2], [-P, 2]], base=SLICE, channel_multiplier=-1, **exact).then_inc(numbered, 1)
                        pool.iota(spare[:], [[0, G // 2], [P, 2]], base=nodes, channel_multiplier=1, **exact).then_inc(numbered, 1)

                        def fetch(i, k):
                            pool.wait_ge(index_staged, group(i, k) * 2 + 2)
                            pool.sem_inc(pool_turn, 1)
                            for j in range(G):
                                for to, table, index, done in ((at_row, to_row, row_i, row_in), (at_col, to_col, col_i, col_in)):
                                    pool.indirect_dma_start(
                                        to[k][:, j, :], None, table,
                                        bass.IndirectOffsetOnAxis(index[k][:, j:j + 1].bitcast(U32), 0),
                                    ).then_inc(done[k][j], 16)
                        pipeline(pool, pairs, (0, fetch))
                        pool.wait_ge(final, 3)
                        pool.tensor_tensor(rstd[:], spread[:], half[:, 0:1], ALU.pow).then_inc(final, 1)

                    @block.tensor
                    def _(pe):
                        def turn(i, k):
                            n = group(i, k)
                            pe.wait_ge(keys_staged, n + 1)
                            if reuses(i):
                                pe.wait_ge(matched, n * G - G)
                            for j in range(G):
                                last = pe.transpose(keys_t[k][:, j, :], keys[k][:, j:j + 1].to_broadcast([P, P]), ident[:])
                            last.then_inc(keys_turned, 1)

                        def mix(i, k):
                            n = group(i, k)
                            pe.wait_ge(ea_in[k], i * 16 + 16)
                            pe.wait_ge(added, n + 1)
                            if reuses(i):
                                pe.wait_ge(h_copied, n - 1)
                            pe.matmul(h[k][:], w1_c[:], ea_t[k][:], start=True, stop=False, skip_group_check=True)
                            for j in range(G):
                                last = pe.matmul(h[k][:, j, :], both[k][:, j, :], ident[:], start=False, stop=True,
                                                 skip_group_check=True)
                            last.then_inc(h_done, 1)
                        pipeline(pe, pairs, (0, turn), (1, mix))

                    @block.scalar
                    def _(act):
                        def copy_h(i, k):
                            n = group(i, k)
                            act.wait_ge(h_done, n + 1)
                            if reuses(i):
                                act.wait_ge(h_out[k], i * 16)
                                act.wait_ge(measured, n - 1)
                            act.copy(h_s[k][:], h[k][:]).then_inc(h_copied, 1)
                        pipeline(act, pairs, (0, copy_h))

                    @block.sync
                    def _(sp):
                        def load(i, k):
                            n = group(i, k)
                            if reuses(i):
                                sp.wait_ge(h_done, n - 1)
                            sp.dma_start(ea_t[k][:], ea2[bass.ds(n, 1)].squeeze(0)).then_inc(ea_in[k], 16)

                        def store(i, k):
                            n = group(i, k)
                            sp.wait_ge(h_copied, n + 1)
                            sp.dma_start(h_t[bass.ds(n, 1)].squeeze(0), h_s[k][:].rearrange("p j e -> p (j e)")).then_inc(h_out[k], 16)
                        pipeline(sp, pairs, (0, load), (1, store))
                        for s in h_out:
                            sp.wait_ge(s, 16 * pairs)
                free()

        def edges_1b():
            width = D + 1
            with ExitStack() as ctx:
                space = workspace(nc, ctx, "l1_edges_b")
                sb, ps, sem, free = space
                keys = [sb(f"keys{k}", [P, G]) for k in range(2)]
                same = [sb(f"same{k}", [P, G, SLICE]) for k in range(2)]
                rows = [sb(f"rows{k}", [P, G, width]) for k in range(2)]
                at = [sb(f"at{k}", [P, G], I32) for k in range(2)]
                h_s, live = ([sb(f"{n}{k}", [P, GE]) for k in range(2)] for n in ("h_s", "live"))
                msg = [sb(f"msg{k}", [P, G, width]) for k in range(2)]
                keys_t, product = ([ps(f"{n}{k}", [P, G, P]) for k in range(2)] for n in ("keys_t", "product"))
                sums = [ps(f"sums{m}", [P, 512]) for m in range(4)]
                h_in = [sem("h_in0"), sem("h_in1")]
                relu_done, product_done, msg_done, ones_set = (
                    sem(n) for n in ("relu_done", "product_done", "msg_done", "ones_set"))
                keys_staged, keys_turned, compared, summed, evacuated, at_staged, pool_turn = (
                    sem(n) for n in ("keys_staged", "keys_turned", "compared", "summed", "evacuated", "at_staged", "pool_turn"))
                added = [[sem(f"added{k}{j}") for j in range(G)] for k in range(2)]
                with nc.Block() as block:
                    @block.sync
                    def _(sp):
                        def load(i, k):
                            n = group(i, k)
                            if reuses(i):
                                sp.wait_ge(relu_done, n - 1)
                            sp.dma_start(h_s[k][:], h_t[bass.ds(n, 1)].squeeze(0)).then_inc(h_in[k], 16)
                        pipeline(sp, pairs, (0, load))

                    @block.scalar
                    def _(act):
                        def relu(i, k):
                            n = group(i, k)
                            act.wait_ge(h_in[k], i * 16 + 16)
                            if reuses(i):
                                act.wait_ge(product_done, n - 1)
                            act.activation(live[k][:], h_s[k][:], ACT.Relu, bias=bn_shift[:], scale=bn_scale[:]).then_inc(relu_done, 1)

                        def empty(i, k):
                            n = group(i, k)
                            if reuses(i):
                                for j in range(G):
                                    act.wait_ge(added[k][j], i * 16)
                            act.copy(at[k][:], sidx[:, bass.ds(n * G, G)]).then_inc(at_staged, 1)
                            for j in range(G):
                                act.wait_ge(summed, n * G + j + 1)
                                act.copy(rows[k][:, j, :], sums[j][:, 0:width]).then_inc(evacuated, 1)
                        pipeline(act, pairs, (0, relu), (2, empty))

                    @block.tensor
                    def _(pe):
                        def turn_keys(i, k):
                            n = group(i, k)
                            pe.wait_ge(keys_staged, n + 1)
                            if reuses(i):
                                pe.wait_ge(compared, n * G - G)
                            for j in range(G):
                                last = pe.transpose(keys_t[k][:, j, :], keys[k][:, j:j + 1].to_broadcast([P, P]), ident[:])
                            last.then_inc(keys_turned, 1)

                        def multiply(i, k):
                            n = group(i, k)
                            pe.wait_ge(relu_done, n + 1)
                            if reuses(i):
                                pe.wait_ge(msg_done, n - 1)
                            for j in range(G):
                                last = pe.matmul(product[k][:, j, :], live[k][:, j * P:(j + 1) * P], w1_2[:], start=True, stop=True)
                            last.then_inc(product_done, 1)

                        def total(i, k):
                            n = group(i, k)
                            pe.wait_ge(msg_done, n + 1)
                            pe.wait_ge(compared, n * G + G)
                            for j in range(G):
                                if not is_first(i, k):
                                    pe.wait_ge(evacuated, n * G - G + j + 1)
                                half_at = (j % 2) * P
                                for step, frm in enumerate((j - j % 2, j - j % 2 + 1)):
                                    last = pe.matmul(sums[j][:, 0:width], same[k][:, frm, half_at:half_at + P], msg[k][:, frm, :],
                                                     start=(step == 0), stop=(step == 1))
                                last.then_inc(summed, 1)
                        pe.wait_ge(ones_set, 2)
                        pipeline(pe, pairs, (0, turn_keys), (1, multiply), (2, total))

                    @block.vector
                    def _(dve):
                        def stage_keys(i, k):
                            n = group(i, k)
                            if reuses(i):
                                dve.wait_ge(compared, n * G - G)
                            dve.tensor_copy(keys[k][:], skey[:, bass.ds(n * G, G)]).then_inc(keys_staged, 1)

                        def compare(i, k):
                            n = group(i, k)
                            dve.wait_ge(keys_turned, n + 1)
                            if reuses(i):
                                dve.wait_ge(summed, n * G - G)
                            for j in range(G):
                                at_slice = j - j % 2
                                dve.tensor_scalar(same[k][:, j, :], keys_t[k][:, at_slice:at_slice + 2, :].rearrange("p j e -> p (j e)"),
                                                  keys[k][:, j:j + 1], None, ALU.is_equal).then_inc(compared, 1)

                        def add(i, k):
                            n = group(i, k)
                            dve.wait_ge(product_done, n + 1)
                            if reuses(i):
                                dve.wait_ge(summed, n * G - G)
                            dve.tensor_tensor(msg[k][:, :, 0:D], product[k][:], b_12[:].unsqueeze(1).to_broadcast([P, G, D]),
                                              ALU.add).then_inc(msg_done, 1)
                        for k in range(2):
                            dve.memset(msg[k][:, :, D:width], 1.0).then_inc(ones_set, 1)
                        pipeline(dve, pairs, (0, stage_keys), (1, compare), (1, add))

                    @block.gpsimd
                    def _(pool):
                        def add_rows(i, k):
                            n = group(i, k)
                            pool.wait_ge(at_staged, n + 1)
                            pool.sem_inc(pool_turn, 1)
                            for j in range(G):
                                pool.wait_ge(evacuated, n * G + j + 1)
                                pool.sem_inc(pool_turn, 1)
                                if j % 2 == 0 and not is_first(i, k):
                                    pi, pk = before(i, k)
                                    for m in (j, j + 1):
                                        pool.wait_ge(added[pk][m], pi * 16 + 16)
                                        pool.sem_inc(pool_turn, 1)
                                pool.indirect_dma_start(
                                    agg1[j // 2], bass.IndirectOffsetOnAxis(at[k][:, j:j + 1].bitcast(U32), 0),
                                    rows[k][:, j, :], None, compute_op=ALU.add,
                                ).then_inc(added[k][j], 16)
                        pipeline(pool, pairs, (0, add_rows))
                        for k in range(2):
                            for j in range(G):
                                pool.wait_ge(added[k][j], 16 * pairs)
                free()

        def nodes_1():
            with ExitStack() as ctx:
                space = workspace(nc, ctx, "l1_nodes")
                sb, ps, sem, free = space
                measure, root, balance, apply_norm, normed = norm_steps(space, "ln", half)
                ag, ag_odd = ([sb(f"{n}{k}", [P, G, D + 1]) for k in range(RING)] for n in ("ag", "ag_odd"))
                count, per = ([sb(f"{n}{k}", [P, G, 1]) for k in range(RING)] for n in ("count", "per"))
                xg, u, x2s, x2_t, x2b_s = ([sb(f"{n}{k}", [P, G, D]) for k in range(RING)]
                                           for n in ("xg", "u", "x2s", "x2_t", "x2b_s"))
                qkvs = [sb(f"qkvs{m}", [P, G, 4 * D]) for m in range(2)]
                turn = [ps(f"turn{m}", [P, G, P]) for m in range(2)]
                y = [ps(f"y{j}", [P, 4 * D]) for j in range(G)]
                a_in, a_odd_in, x_in, x2b_out = (
                    [sem(f"{n}{k}") for k in range(RING)] for n in ("a_in", "a_odd_in", "x_in", "x2b_out"))
                q_out, kv_out, skip_out = ([sem(f"{n}{k}") for k in range(RING)] for n in ("q_out", "kv_out", "skip_out"))
                joined, counted, inverted, scaled, mixed, turned = (
                    sem(n) for n in ("joined", "counted", "inverted", "scaled", "mixed", "turned"))
                copied, y_done, biased, x2b_done = (sem(n) for n in ("copied", "y_done", "biased", "x2b_done"))
                with nc.Block() as block:
                    @block.sync
                    def _(sp):
                        def load(i, k):
                            n = place(i, k)
                            if reuses(i):
                                sp.wait_ge(scaled, (n - RING + 1) * G)
                            for to, table, done in ((ag, agg1[0], a_in), (ag_odd, agg1[1], a_odd_in)):
                                sp.dma_start(to[k][:], by_group(table[0:nodes], D + 1)[bass.ds(n, 1)].squeeze(0)).then_inc(done[k], 16)
                            if reuses(i):
                                sp.wait_ge(mixed, n - RING + 1)
                            sp.dma_start(xg[k][:], by_group(x1, D)[bass.ds(n, 1)].squeeze(0)).then_inc(x_in[k], 16)

                        def store(i, k):
                            n = place(i, k)
                            sp.wait_ge(x2b_done, n + 1)
                            sp.dma_start(by_group(x2b, D)[bass.ds(n, 1)].squeeze(0), x2b_s[k][:]).then_inc(x2b_out[k], 16)
                            sp.wait_ge(biased, n * G + G)
                            whole = qkvs[k % 2]
                            sp.dma_start(by_group(q_tab, D)[bass.ds(n, 1)].squeeze(0), whole[:, :, 0:D]).then_inc(q_out[k], 16)
                            sp.dma_start(by_group(kv_tab, 2 * D)[bass.ds(n, 1)].squeeze(0), whole[:, :, D:3 * D]).then_inc(kv_out[k], 16)
                            sp.dma_start(by_group(skip_tab, D)[bass.ds(n, 1)].squeeze(0), whole[:, :, 3 * D:4 * D]).then_inc(skip_out[k], 16)
                        rotation(sp, groups, (0, load), (8, store))
                        all_out(sp, q_out, kv_out, skip_out, x2b_out)

                    @block.vector
                    def _(dve):
                        def invert(i, k):
                            n = place(i, k)
                            dve.wait_ge(joined, n + 1)
                            dve.tensor_scalar(count[k][:], ag[k][:, :, D:D + 1], 1.0, None, ALU.add).then_inc(counted, 1)
                            dve.wait_ge(counted, n + 1)
                            if reuses(i):
                                dve.wait_ge(scaled, (n - RING + 1) * G)
                            dve.reciprocal(per[k][:], count[k][:]).then_inc(inverted, 1)

                        def mix(i, k):
                            n = place(i, k)
                            dve.wait_ge(scaled, n * G + G)
                            dve.wait_ge(x_in[k], i * 16 + 16)
                            dve.scalar_tensor_tensor(u[k][:], xg[k][:], 2.0, u[k][:], ALU.mult, ALU.add).then_inc(mixed, 1)
                            dve.wait_ge(mixed, n + 1)
                            measure(dve, i, k, u[k])

                        def bias(i, k):
                            n = place(i, k)
                            if follows(i, k, 2):
                                pi, pk = (i, k - 2) if k >= 2 else (i - 1, k + 2)
                                for s in (q_out[pk], kv_out[pk], skip_out[pk]):
                                    dve.wait_ge(s, pi * 16 + 16)
                            for j in range(G):
                                dve.wait_ge(y_done, n * G + j + 1)
                                dve.tensor_tensor(qkvs[k % 2][:, j, :], y[j][:], b_qkvs[:], ALU.add).then_inc(biased, 1)
                        rotation(dve, groups, (4, lambda i, k: balance(dve, i, k)), (2, invert), (3, mix), (6, bias))

                    @block.gpsimd
                    def _(pool):
                        def join(i, k):
                            n = place(i, k)
                            pool.wait_ge(a_in[k], i * 16 + 16)
                            pool.wait_ge(a_odd_in[k], i * 16 + 16)
                            pool.tensor_tensor(ag[k][:], ag[k][:], ag_odd[k][:], ALU.add).then_inc(joined, 1)

                        def shift(i, k):
                            n = place(i, k)
                            if reuses(i):
                                pool.wait_ge(x2b_out[k], i * 16)
                            pool.wait_ge(normed, n * G + G)
                            pool.tensor_tensor(x2b_s[k][:], x2s[k][:], b_2[:].unsqueeze(1).to_broadcast([P, G, D]),
                                               ALU.add).then_inc(x2b_done, 1)
                        rotation(pool, groups, (1, join), (5, shift), (3, lambda i, k: root(pool, i, k)))

                    @block.scalar
                    def _(act):
                        def scale(i, k):
                            n = place(i, k)
                            act.wait_ge(inverted, n + 1)
                            if reuses(i):
                                act.wait_ge(normed, (n - RING + 1) * G)
                            for j in range(G):
                                act.activation(u[k][:, j, :], ag[k][:, j, 0:D], ACT.Copy, scale=per[k][:, j, :]).then_inc(scaled, 1)

                        def copy(i, k):
                            n = place(i, k)
                            act.wait_ge(turned, n + 1)
                            if reuses(i):
                                act.wait_ge(y_done, (n - RING + 1) * G)
                            act.copy(x2_t[k][:], turn[k % 2][:]).then_inc(copied, 1)

                        def apply(i, k):
                            n = place(i, k)
                            if reuses(i):
                                act.wait_ge(turned, n - RING + 1)
                                act.wait_ge(x2b_done, n - RING + 1)
                            apply_norm(act, i, k, x2s[k], u[k])
                        rotation(act, groups, (4, apply), (5, copy), (2, scale))

                    @block.tensor
                    def _(pe):
                        def turn_x(i, k):
                            n = place(i, k)
                            pe.wait_ge(normed, n * G + G)
                            if follows(i, k, 2):
                                pe.wait_ge(copied, n - 1)
                            for j in range(G):
                                last = pe.transpose(turn[k % 2][:, j, :], x2s[k][:, j, :], ident[:])
                            last.then_inc(turned, 1)

                        def project(i, k):
                            n = place(i, k)
                            pe.wait_ge(copied, n + 1)
                            for j in range(G):
                                if follows(i, k, 1):
                                    pe.wait_ge(biased, n * G - G + j + 1)
                                pe.matmul(y[j][:], x2_t[k][:, j, :], w_qkvs[:], start=True, stop=True).then_inc(y_done, 1)
                        rotation(pe, groups, (5, turn_x), (6, project))
                free()

        def edges_2a():
            with ExitStack() as ctx:
                space = workspace(nc, ctx, "l2_edges_a")
                sb, ps, sem, free = space
                src_s, dst_s = ([sb(f"{n}{k}", [P, G], I32) for k in range(2)] for n in ("src_s", "dst_s"))
                kv, q = [sb(f"kv{k}", [P, G, 2 * D]) for k in range(2)], [sb(f"q{k}", [P, G, D]) for k in range(2)]
                ea_t = [sb(f"ea_t{k}", [ED, G, P]) for k in range(2)]
                key_e, v_e, prod = ([sb(f"{n}{k}", [P, G, D]) for k in range(2)] for n in ("key_e", "v_e", "prod"))
                e = [ps(f"e{k}", [P, G, D]) for k in range(2)]
                index_staged, e_done, v_done, k_done, prod_done, scored, pool_turn = (
                    sem(n) for n in ("index_staged", "e_done", "v_done", "k_done", "prod_done", "scored", "pool_turn"))
                kv_in = [[sem(f"kv_in{k}{j}") for j in range(G)] for k in range(2)]
                q_in = [[sem(f"q_in{k}{j}") for j in range(G)] for k in range(2)]
                ea_in, v_out = [sem("ea_in0"), sem("ea_in1")], [sem("v_out0"), sem("v_out1")]
                with nc.Block() as block:
                    @block.vector
                    def _(dve):
                        def stage(i, k):
                            n = group(i, k)
                            if reuses(i):
                                dve.wait_ge(v_done, n - 1)
                                dve.wait_ge(prod_done, n - 1)
                            dve.tensor_copy(src_s[k][:], src_i[:, bass.ds(n * G, G)]).then_inc(index_staged, 1)
                            dve.tensor_copy(dst_s[k][:], dst_i[:, bass.ds(n * G, G)]).then_inc(index_staged, 1)

                        def score(i, k):
                            n = group(i, k)
                            dve.wait_ge(e_done, n + 1)
                            for j in range(G):
                                dve.wait_ge(kv_in[k][j], i * 16 + 16)
                            if reuses(i):
                                dve.wait_ge(scored, n - 1)
                            dve.tensor_tensor(key_e[k][:], kv[k][:, :, 0:D], e[k][:], ALU.add).then_inc(k_done, 1)
                            if reuses(i):
                                dve.wait_ge(v_out[k], i * 16)
                            dve.tensor_tensor(v_e[k][:], kv[k][:, :, D:2 * D], e[k][:], ALU.add).then_inc(v_done, 1)
                            dve.wait_ge(k_done, n + 1)
                            for j in range(G):
                                dve.wait_ge(q_in[k][j], i * 16 + 16)
                            dve.tensor_tensor(prod[k][:], key_e[k][:], q[k][:], ALU.mult).then_inc(prod_done, 1)
                            dve.wait_ge(prod_done, n + 1)
                            dve.tensor_reduce(scores[:, bass.ds(n * G * H2, G * H2)],
                                              prod[k][:].rearrange("p j (h c) -> p (j h) c", c=C2), AX.X,
                                              ALU.add).then_inc(scored, 1)
                        pipeline(dve, pairs, (0, stage), (1, score))
                        dve.wait_ge(scored, groups)

                    @block.gpsimd
                    def _(pool):
                        def fetch(i, k):
                            pool.wait_ge(index_staged, group(i, k) * 2 + 2)
                            pool.sem_inc(pool_turn, 1)
                            for j in range(G):
                                for to, table, index, done in ((kv, kv_tab, src_s, kv_in), (q, q_tab, dst_s, q_in)):
                                    pool.indirect_dma_start(
                                        to[k][:, j, :], None, table,
                                        bass.IndirectOffsetOnAxis(index[k][:, j:j + 1].bitcast(U32), 0),
                                    ).then_inc(done[k][j], 16)
                        pipeline(pool, pairs, (0, fetch))

                    @block.tensor
                    def _(pe):
                        def edge(i, k):
                            n = group(i, k)
                            pe.wait_ge(ea_in[k], i * 16 + 16)
                            if reuses(i):
                                pe.wait_ge(v_done, n - 1)
                            for j in range(G):
                                last = pe.matmul(e[k][:, j, :], ea_t[k][:, j, :], w_e[:], start=True, stop=True)
                            last.then_inc(e_done, 1)
                        pipeline(pe, pairs, (0, edge))

                    @block.sync
                    def _(sp):
                        def load(i, k):
                            n = group(i, k)
                            if reuses(i):
                                sp.wait_ge(e_done, n - 1)
                            sp.dma_start(ea_t[k][:].rearrange("p j e -> p (j e)"), ea64[bass.ds(n, 1)].squeeze(0)).then_inc(ea_in[k], 16)

                        def store(i, k):
                            n = group(i, k)
                            sp.wait_ge(v_done, n + 1)
                            sp.dma_start(v_edge[bass.ds(n, 1)].squeeze(0), v_e[k][:].rearrange("p j d -> p (j d)")).then_inc(v_out[k], 16)
                        pipeline(sp, pairs, (0, load), (1, store))
                        for s in v_out:
                            sp.wait_ge(s, 16 * pairs)
                free()

        def turn_logits():
            wide = 2 * G * H2
            with ExitStack() as ctx:
                space = workspace(nc, ctx, "turn_logits")
                sb, ps, sem, free = space
                flat, turned = [sb(f"flat{k}", [P, wide]) for k in range(2)], [sb(f"turned{k}", [wide, P]) for k in range(2)]
                turn = [ps(f"turn{k}", [wide, 512]) for k in range(2)]
                s_flat, s_turn, s_copied, pe_turn = sem("s_flat"), sem("s_turn"), sem("s_copied"), sem("pe_turn")
                out_done = [sem("out0"), sem("out1")]
                rows = logit_t.rearrange("(m j) h e -> m (j h) e", j=2 * G)
                with nc.Block() as block:
                    @block.vector
                    def _(dve):
                        def step(m, k, old):
                            if old:
                                dve.wait_ge(s_turn, m)
                            dve.tensor_copy(flat[k][:], scores[:, bass.ds(m * wide, wide)]).then_inc(s_flat, 1)
                        step(0, 0, False)
                        with dve.Fori(1, pairs) as m:
                            step(m, 0, True)

                    @block.tensor
                    def _(pe):
                        def step(m, k, old):
                            pe.wait_ge(s_flat, m + 1)
                            pe.sem_inc(pe_turn, 1)
                            if old:
                                pe.wait_ge(s_copied, m)
                                pe.sem_inc(pe_turn, 1)
                            pe.transpose(turn[k][:, 0:P], flat[k][:], ident[:]).then_inc(s_turn, 1)
                        step(0, 0, False)
                        with pe.Fori(1, pairs) as m:
                            step(m, 0, True)

                    @block.scalar
                    def _(act):
                        def step(m, k, old):
                            act.wait_ge(s_turn, m + 1)
                            if old:
                                act.wait_ge(out_done[k], m * 16)
                            act.copy(turned[k][:], turn[k][:, 0:P]).then_inc(s_copied, 1)
                        step(0, 0, False)
                        with act.Fori(1, pairs) as m:
                            step(m, 0, True)

                    @block.sync
                    def _(sp):
                        with sp.Fori(0, pairs) as m:
                            sp.wait_ge(s_copied, m + 1)
                            sp.dma_start(rows[bass.ds(m, 1)].squeeze(0), turned[0][:]).then_inc(out_done[0], 16)
                        sp.wait_ge(out_done[0], 16 * pairs)
                free()

        def segment_max():
            lanes, span = chunks * H2, edges // chunks
            per = tiles // chunks
            with ExitStack() as ctx:
                space = workspace(nc, ctx, "segment_max")
                sb, _, sem, free = space
                keys = sb("keys", [lanes, span + 2], I32)
                logit = sb("logit", [lanes, span])
                reset = [sb("reset_f", [lanes, span]), sb("reset_b", [lanes, span])]
                best = [sb("best_f", [lanes, span]), sb("best_b", [lanes, span])]
                through = [sb(f"through{d}", [lanes, 1]) for d in range(2)]
                end_s, through_s, carry_s = ([sb(f"{n}{d}", [H2, chunks]) for d in range(2)]
                                             for n in ("end_s", "through_s", "carry_s"))
                start_s = [sb(f"start_s{d}", [H2, chunks]) for d in range(2)]
                entry = [sb(f"entry{d}", [lanes, 1]) for d in range(2)]
                loaded, step, saved, fetched, started, entered, out_done = (
                    sem(n) for n in ("loaded", "step", "saved", "fetched", "started", "entered", "out_done"))
                saved = [sem(f"saved{d}") for d in range(2)]
                fetched = [sem(f"fetched{d}") for d in range(2)]
                started = [sem(f"started{d}") for d in range(2)]
                entered = [sem(f"entered{d}") for d in range(2)]
                scanned, spread = [sem("scanned0"), sem("scanned1")], [sem("spread0"), sem("spread1")]
                line = logit_t.rearrange("(c t) h e -> c h t e", c=chunks)
                out_line = max_t.rearrange("(c t) h e -> c h t e", c=chunks)
                by_head = "(c h) -> h c"
                with nc.Block() as block:
                    @block.sync
                    def _(sp):
                        for c in range(chunks):
                            rows = slice(c * H2, (c + 1) * H2)
                            sp.dma_start(logit[rows, :].rearrange("h (t e) -> h t e", t=per), line[c]).then_inc(loaded, 16)
                            sp.dma_start(keys[rows, :], dst_line[0:1, c * span:c * span + span + 2].to_broadcast(
                                [H2, span + 2])).then_inc(loaded, 16)
                        with nc.allow_non_contiguous_dma(reason="one word for each chunk and head"):
                            for d in range(2):
                                last = best[d][:, span - 1:span] if d == 0 else best[d][:, 0:1]
                                sp.wait_ge(scanned[d], 1)
                                sp.dma_start(ends[d, 0].rearrange("(l a) -> l a", a=1), last).then_inc(saved[d], 16)
                                sp.dma_start(ends[d, 1].rearrange("(l a) -> l a", a=1), through[d][:]).then_inc(saved[d], 16)
                                sp.wait_ge(saved[d], 32)
                                sp.dma_start(end_s[d][:], ends[d, 0].rearrange(by_head, h=H2)).then_inc(fetched[d], 16)
                                sp.dma_start(through_s[d][:], ends[d, 1].rearrange(by_head, h=H2)).then_inc(fetched[d], 16)
                                sp.wait_ge(spread[d], 1)
                                sp.dma_start(starts[d].rearrange(by_head, h=H2), start_s[d][:]).then_inc(started[d], 16)
                                sp.wait_ge(started[d], 16)
                                sp.dma_start(entry[d][:], starts[d].rearrange("(l a) -> l a", a=1)).then_inc(entered[d], 16)
                        sp.wait_ge(scanned[1], 2)
                        for c in range(chunks):
                            rows = slice(c * H2, (c + 1) * H2)
                            sp.dma_start(out_line[c], best[1][rows, :].rearrange("h (t e) -> h t e", t=per)).then_inc(out_done, 16)
                        sp.wait_ge(out_done, 16 * chunks)

                    @block.vector
                    def _(dve):
                        done = 0

                        def chain(ins):
                            nonlocal done
                            ins.then_inc(step, 1)
                            done += 1
                            dve.wait_ge(step, done)
                        dve.wait_ge(loaded, 32 * chunks)
                        for d in range(2):
                            other = keys[:, 0:span] if d == 0 else keys[:, 2:span + 2]
                            chain(dve.tensor_tensor(reset[d][:], keys[:, 1:span + 1], other, ALU.is_equal))
                            chain(dve.tensor_scalar(reset[d][:], reset[d][:], -LOW, LOW, ALU.mult, ALU.add))
                            chain(dve.tensor_reduce(through[d][:], reset[d][:], AX.X, ALU.min))

                        def scan(d, initial):
                            frm = logit if d == 0 else best[0]
                            way = slice(None) if d == 0 else slice(None, None, -1)
                            return dve.tensor_tensor_scan(best[d][:, way], reset[d][:, way], frm[:, way], initial,
                                                          ALU.add, ALU.max)
                        for d in range(2):
                            scan(d, LOW).then_inc(scanned[d], 1)
                            dve.wait_ge(fetched[d], 32)
                            way = slice(None) if d == 0 else slice(None, None, -1)
                            chain(dve.tensor_tensor_scan(carry_s[d][:, way], through_s[d][:, way], end_s[d][:, way], LOW,
                                                         ALU.add, ALU.max))
                            chain(dve.memset(start_s[d][:], LOW))
                            if chunks > 1:
                                to, frm = (slice(1, None), slice(0, -1)) if d == 0 else (slice(0, -1), slice(1, None))
                                chain(dve.tensor_copy(start_s[d][:, to], carry_s[d][:, frm]))
                            dve.sem_inc(spread[d], 1)
                            dve.wait_ge(entered[d], 16)
                            scan(d, entry[d][:]).then_inc(scanned[d], 1)
                            dve.wait_ge(scanned[d], 2)
                free()

        def weigh_edges(name, seg_table, heads, source, scale, minus):
            c = D // heads
            with ExitStack() as ctx:
                space = workspace(nc, ctx, name)
                sb, ps, sem, free = space
                stage_keys, turn_keys, compare, total, empty, scatter, settle, summed = segment_steps(
                    space, dkey, dprev, dwidx, seg_table, D + heads, ident, nodes)
                v = [sb(f"v{k}", [P, G, D]) for k in range(2)]
                top_t = [sb(f"top_t{k}", [G * heads, P]) for k in range(2)]
                diff, ex = ([sb(f"{n}{k}", [P, G * heads]) for k in range(2)] for n in ("diff", "ex"))
                msg = [sb(f"msg{k}", [P, G, D + heads]) for k in range(2)]
                peak = [ps(f"peak{k}", [P, 512]) for k in range(2)]
                v_in, top_in = [sem("v_in0"), sem("v_in1")], [sem("top_in0"), sem("top_in1")]
                peaked, differed, risen, weighed, pe_turn = (
                    sem(n) for n in ("peaked", "differed", "risen", "weighed", "pe_turn"))
                rows = max_t.rearrange("(g j) h e -> g (j h) e", j=G)
                with nc.Block() as block:
                    @block.sync
                    def _(sp):
                        def load(i, k):
                            n = group(i, k)
                            if minus is None:
                                if reuses(i):
                                    sp.wait_ge(peaked, n - 1)
                                sp.dma_start(top_t[k][:], rows[bass.ds(n, 1)].squeeze(0)).then_inc(top_in[k], 16)
                            if reuses(i):
                                sp.wait_ge(weighed, n * 2 - 2)
                            sp.dma_start(v[k][:].rearrange("p j d -> p (j d)"), source[bass.ds(n, 1)].squeeze(0)).then_inc(v_in[k], 16)
                        pipeline(sp, pairs, (0, load))

                    @block.tensor
                    def _(pe):
                        def turn_peaks(i, k):
                            n = group(i, k)
                            pe.wait_ge(top_in[k], i * 16 + 16)
                            pe.sem_inc(pe_turn, 1)
                            if reuses(i):
                                pe.wait_ge(differed, n - 1)
                                pe.sem_inc(pe_turn, 1)
                            pe.transpose(peak[k][:, 0:G * heads], top_t[k][:], ident[0:G * heads, 0:G * heads]).then_inc(peaked, 1)

                        def total_messages(i, k):
                            pe.wait_ge(weighed, group(i, k) * 2 + 2)
                            total(pe, i, k, msg[k])
                        stages = [(0, lambda i, k: turn_keys(pe, i, k)), (2, total_messages)]
                        if minus is None:
                            stages.insert(0, (0, turn_peaks))
                        pipeline(pe, pairs, *stages)

                    @block.vector
                    def _(dve):
                        def differ(i, k):
                            n = group(i, k)
                            dve.wait_ge(peaked, n + 1)
                            if reuses(i):
                                dve.wait_ge(risen, n - 1)
                            dve.tensor_tensor(diff[k][:], scores[:, bass.ds(n * G * heads, G * heads)],
                                              peak[k][:, 0:G * heads], ALU.subtract).then_inc(differed, 1)

                        def weigh(i, k):
                            n = group(i, k)
                            dve.wait_ge(risen, n + 1)
                            dve.wait_ge(v_in[k], i * 16 + 16)
                            if reuses(i):
                                dve.wait_ge(summed, n * G - G)
                            for_heads = ex[k][:].rearrange("p (j h) -> p j h", h=heads)
                            dve.tensor_tensor(msg[k][:, :, 0:D].rearrange("p j (h c) -> p j h c", c=c),
                                              v[k][:].rearrange("p j (h c) -> p j h c", c=c),
                                              for_heads.unsqueeze(3).to_broadcast([P, G, heads, c]),
                                              ALU.mult).then_inc(weighed, 1)
                            dve.tensor_copy(msg[k][:, :, D:D + heads], for_heads).then_inc(weighed, 1)
                        stages = [(0, lambda i, k: stage_keys(dve, i, k)), (1, lambda i, k: compare(dve, i, k)),
                                  (1, weigh)]
                        if minus is None:
                            stages.insert(1, (0, differ))
                        pipeline(dve, pairs, *stages)

                    @block.scalar
                    def _(act):
                        def rise(i, k):
                            n = group(i, k)
                            if reuses(i):
                                act.wait_ge(weighed, n * 2 - 2)
                            if minus is None:
                                act.wait_ge(differed, n + 1)
                                act.activation(ex[k][:], diff[k][:], ACT.Exp, scale=scale).then_inc(risen, 1)
                            else:
                                act.activation(ex[k][:], scores[:, bass.ds(n * G * heads, G * heads)], ACT.Exp,
                                               bias=minus[:], scale=scale).then_inc(risen, 1)
                        pipeline(act, pairs, (0, rise), (2, lambda i, k: empty(act, i, k)))

                    @block.gpsimd
                    def _(pool):
                        pipeline(pool, pairs, (0, lambda i, k: scatter(pool, i, k)))
                        settle(pool, pairs)
                free()

        def nodes_2():
            with ExitStack() as ctx:
                space = workspace(nc, ctx, "l2_nodes")
                sb, ps, sem, free = space
                measure_a, root_a, balance_a, norm_a, a_normed = norm_steps(space, "na", half)
                measure_b, root_b, balance_b, norm_b, b_normed = norm_steps(space, "nb", half)
                measure_x, root_x, balance_x, norm_x, x_normed = norm_steps(space, "nx", half)
                ag = [sb(f"ag{k}", [P, G, D + H2]) for k in range(RING)]
                den, per = ([sb(f"{n}{k}", [P, G, H2]) for k in range(RING)] for n in ("den", "per"))
                skip, x2g, ua, h_t_s, ub, ux, x3s = (
                    [sb(f"{n}{k}", [P, G, D]) for k in range(RING)] for n in (
                        "skip", "x2g", "ua", "h_t_s", "ub", "ux", "x3s"))
                normed_a, normed_b, x3_t, x3b_s = (
                    [sb(f"{n}{m}", [P, G, D]) for m in range(2)] for n in ("normed_a", "normed_b", "x3_t", "x3b_s"))
                act_t = [sb(f"act_t{m}", [P, 4, GE]) for m in range(2)]
                ext = [sb(f"ext{m}", [P, G, D + 2 * H3]) for m in range(2)]
                turn_h, turn_x, y = ps("turn_h", [P, G, P]), ps("turn_x", [P, G, P]), ps("y", [P, G, D])
                f = [ps(f"f{m}", [P, GE]) for m in range(2)]
                pe_ext = [ps(f"pe_ext{m}", [P, 512]) for m in range(2)]
                a_in, skip_in, x2_in, ext_out, tgt_out, x3b_out = (
                    [sem(f"{n}{k}") for k in range(RING)] for n in ("a_in", "skip_in", "x2_in", "ext_out", "tgt_out", "x3b_out"))
                floored, inverted, conv_done, ua_done, h_turned, h_copied = (
                    sem(n) for n in ("floored", "inverted", "conv_done", "ua_done", "h_turned", "h_copied"))
                f_done, gelu_done, y_done, ub_done, scaled_b, ux_done = (
                    sem(n) for n in ("f_done", "gelu_done", "y_done", "ub_done", "scaled_b", "ux_done"))
                x_turned, x_copied, ext_done, ext_copied, x3b_done = (
                    sem(n) for n in ("x_turned", "x_copied", "ext_done", "ext_copied", "x3b_done"))

                def two_back(i, k):
                    return (i, k - 2) if k >= 2 else (i - 1, k + 2)
                with nc.Block() as block:
                    @block.sync
                    def _(sp):
                        def load(i, k):
                            n = place(i, k)
                            if reuses(i):
                                sp.wait_ge(ua_done, n - RING + 1)
                            sp.dma_start(ag[k][:], by_group(agg2, D + H2)[bass.ds(n, 1)].squeeze(0)).then_inc(a_in[k], 16)
                            sp.dma_start(skip[k][:], by_group(skip_tab, D)[bass.ds(n, 1)].squeeze(0)).then_inc(skip_in[k], 16)

                        def load_x2(i, k):
                            n = place(i, k)
                            if reuses(i):
                                sp.wait_ge(ux_done, n - RING + 1)
                            sp.dma_start(x2g[k][:], by_group(x2b, D)[bass.ds(n, 1)].squeeze(0)).then_inc(x2_in[k], 16)

                        def store(i, k):
                            n = place(i, k)
                            sp.wait_ge(x3b_done, n + 1)
                            sp.dma_start(by_group(x3b, D)[bass.ds(n, 1)].squeeze(0), x3b_s[k % 2][:]).then_inc(x3b_out[k], 16)
                            sp.wait_ge(ext_copied, n * 2 + 2)
                            sp.dma_start(by_group(proj_tab, D + H3)[bass.ds(n, 1)].squeeze(0), ext[k % 2][:, :, 0:D + H3]).then_inc(ext_out[k], 16)
                            sp.dma_start(by_group(tgt_tab, H3)[bass.ds(n, 1)].squeeze(0), ext[k % 2][:, :, D + H3:D + 2 * H3]).then_inc(tgt_out[k], 16)
                        rotation(sp, groups, (0, load), (7, load_x2), (15, store))
                        all_out(sp, x3b_out, ext_out, tgt_out)

                    @block.vector
                    def _(dve):
                        def conv(i, k):
                            n = place(i, k)
                            dve.wait_ge(a_in[k], i * 16 + 16)
                            dve.tensor_scalar(den[k][:], ag[k][:, :, D:D + H2], 1e-30, None, ALU.max).then_inc(floored, 1)
                            dve.wait_ge(floored, n + 1)
                            dve.reciprocal(per[k][:], den[k][:]).then_inc(inverted, 1)
                            dve.wait_ge(inverted, n + 1)
                            if reuses(i):
                                dve.wait_ge(a_normed, (n - RING + 1) * G)
                            dve.tensor_tensor(ua[k][:].rearrange("p j (h c) -> p j h c", c=C2),
                                              ag[k][:, :, 0:D].rearrange("p j (h c) -> p j h c", c=C2),
                                              per[k][:].unsqueeze(3).to_broadcast([P, G, H2, C2]), ALU.mult).then_inc(conv_done, 1)

                        def moments_a(i, k):
                            dve.wait_ge(ua_done, place(i, k) + 1)
                            measure_a(dve, i, k, ua[k])

                        def after_ffn(i, k):
                            n = place(i, k)
                            dve.wait_ge(y_done, n + 1)
                            if reuses(i):
                                dve.wait_ge(b_normed, (n - RING + 1) * G)
                            dve.tensor_tensor(ub[k][:], y[:], b_f2[:].unsqueeze(1).to_broadcast([P, G, D]), ALU.add).then_inc(ub_done, 1)
                            dve.wait_ge(ub_done, n + 1)
                            measure_b(dve, i, k, ub[k])

                        def scale_b(i, k):
                            n = place(i, k)
                            dve.wait_ge(b_normed, n * G + G)
                            if reuses(i):
                                dve.wait_ge(x_normed, (n - RING + 1) * G)
                            dve.tensor_tensor(ux[k][:], normed_b[k % 2][:], g_2[:].unsqueeze(1).to_broadcast([P, G, D]), ALU.mult).then_inc(scaled_b, 1)

                        def moments_x(i, k):
                            dve.wait_ge(ux_done, place(i, k) + 1)
                            measure_x(dve, i, k, ux[k])
                        rotation(dve, groups, (4, lambda i, k: balance_a(dve, i, k)), (8, lambda i, k: balance_b(dve, i, k)),
                                 (11, lambda i, k: balance_x(dve, i, k)), (3, moments_a), (10, moments_x), (1, conv),
                                 (9, scale_b), (7, after_ffn))

                    @block.gpsimd
                    def _(pool):
                        def add_skip(i, k):
                            n = place(i, k)
                            pool.wait_ge(conv_done, n + 1)
                            pool.wait_ge(skip_in[k], i * 16 + 16)
                            pool.tensor_tensor(ua[k][:], ua[k][:], skip[k][:], ALU.add).then_inc(ua_done, 1)

                        def add_x2(i, k):
                            n = place(i, k)
                            pool.wait_ge(scaled_b, n + 1)
                            pool.wait_ge(x2_in[k], i * 16 + 16)
                            pool.tensor_tensor(ux[k][:], ux[k][:], x2g[k][:], ALU.add).then_inc(ux_done, 1)

                        def shift(i, k):
                            n = place(i, k)
                            if follows(i, k, 2):
                                pi, pk = two_back(i, k)
                                pool.wait_ge(x3b_out[pk], pi * 16 + 16)
                            pool.wait_ge(x_normed, n * G + G)
                            pool.tensor_tensor(x3b_s[k % 2][:], x3s[k][:], b_3[:].unsqueeze(1).to_broadcast([P, G, D]),
                                               ALU.add).then_inc(x3b_done, 1)
                        rotation(pool, groups, (2, add_skip), (3, lambda i, k: root_a(pool, i, k)), (10, lambda i, k: root_x(pool, i, k)),
                                 (12, shift), (9, add_x2), (7, lambda i, k: root_b(pool, i, k)))

                    @block.scalar
                    def _(act):
                        def apply_a(i, k):
                            if follows(i, k, 2):
                                act.wait_ge(h_turned, place(i, k) - 1)
                            norm_a(act, i, k, normed_a[k % 2], ua[k])

                        def copy_h(i, k):
                            n = place(i, k)
                            act.wait_ge(h_turned, n + 1)
                            if reuses(i):
                                act.wait_ge(y_done, n - RING + 1)
                            act.activation(h_t_s[k][:], turn_h[:], ACT.Identity, bias=b_1[:], scale=g_1[:]).then_inc(h_copied, 1)

                        def gelu(i, k):
                            n = place(i, k)
                            if follows(i, k, 2):
                                act.wait_ge(y_done, n - 1)
                            for m in range(4):
                                act.wait_ge(f_done, n * 4 + m + 1)
                                act.activation(act_t[k % 2][:, m, :], f[m % 2][:], ACT.Gelu, bias=b_f1[:, m:m + 1]).then_inc(gelu_done, 1)

                        def apply_b(i, k):
                            if follows(i, k, 2):
                                act.wait_ge(scaled_b, place(i, k) - 1)
                            norm_b(act, i, k, normed_b[k % 2], ub[k])

                        def apply_x(i, k):
                            n = place(i, k)
                            if reuses(i):
                                act.wait_ge(x_turned, n - RING + 1)
                                act.wait_ge(x3b_done, n - RING + 1)
                            norm_x(act, i, k, x3s[k], ux[k])

                        def copy_x(i, k):
                            n = place(i, k)
                            act.wait_ge(x_turned, n + 1)
                            if follows(i, k, 2):
                                act.wait_ge(ext_done, n * 2 - 2)
                            act.copy(x3_t[k % 2][:], turn_x[:]).then_inc(x_copied, 1)

                        def copy_ext(i, k):
                            n = place(i, k)
                            if follows(i, k, 2):
                                pi, pk = two_back(i, k)
                                act.wait_ge(ext_out[pk], pi * 16 + 16)
                                act.wait_ge(tgt_out[pk], pi * 16 + 16)
                            for m in range(2):
                                act.wait_ge(ext_done, n * 2 + m + 1)
                                act.copy(ext[k % 2][:, 2 * m:2 * m + 2, :], pe_ext[m][:, 0:2 * (D + 2 * H3)].rearrange(
                                    "p (j d) -> p j d", j=2)).then_inc(ext_copied, 1)
                        rotation(act, groups, (5, copy_h), (6, gelu), (12, copy_x), (4, apply_a), (8, apply_b), (11, apply_x),
                                 (13, copy_ext))

                    @block.tensor
                    def _(pe):
                        def turn(i, k):
                            n = place(i, k)
                            pe.wait_ge(a_normed, n * G + G)
                            if follows(i, k, 1):
                                pe.wait_ge(h_copied, n)
                            for j in range(G):
                                last = pe.transpose(turn_h[:, j, :], normed_a[k % 2][:, j, :], ident[:])
                            last.then_inc(h_turned, 1)

                        def widen(i, k):
                            n = place(i, k)
                            pe.wait_ge(h_copied, n + 1)
                            for m in range(4):
                                if m >= 2 or follows(i, k, 1):
                                    pe.wait_ge(gelu_done, n * 4 + m - 1)
                                pe.matmul(f[m % 2][:], w_f1[:, m * P:(m + 1) * P], h_t_s[k][:], start=True, stop=True).then_inc(f_done, 1)

                        def narrow(i, k):
                            n = place(i, k)
                            if follows(i, k, 1):
                                pe.wait_ge(ub_done, n)
                            pe.wait_ge(gelu_done, n * 4 + 4)
                            for j in range(G):
                                pe.matmul(y[:, j, :], h_t_s[k][:, j, :], ident[:], start=True, stop=False)
                                for m in range(4):
                                    last = pe.matmul(y[:, j, :], act_t[k % 2][:, m, j * P:(j + 1) * P], w_f2[:, m, :],
                                                     start=False, stop=(m == 3))
                            last.then_inc(y_done, 1)

                        def turn_x3(i, k):
                            n = place(i, k)
                            pe.wait_ge(x_normed, n * G + G)
                            if follows(i, k, 1):
                                pe.wait_ge(x_copied, n)
                            for j in range(G):
                                last = pe.transpose(turn_x[:, j, :], x3s[k][:, j, :], ident[:])
                            last.then_inc(x_turned, 1)

                        def project(i, k):
                            n = place(i, k)
                            pe.wait_ge(x_copied, n + 1)
                            for m in range(2):
                                if follows(i, k, 1):
                                    pe.wait_ge(ext_copied, n * 2 - 1 + m)
                                for j in range(2):
                                    at = j * (D + 2 * H3)
                                    last = pe.matmul(pe_ext[m][:, at:at + D + 2 * H3], x3_t[k % 2][:, 2 * m + j, :], w_proj[:],
                                                     start=True, stop=True)
                                last.then_inc(ext_done, 1)
                        rotation(pe, groups, (5, turn), (12, turn_x3), (6, widen), (7, narrow), (13, project))
                free()

        def edges_3a():
            with ExitStack() as ctx:
                space = workspace(nc, ctx, "l3_edges_a")
                sb, _, sem, free = space
                src_s, dst_s = ([sb(f"{n}{k}", [P, G], I32) for k in range(2)] for n in ("src_s", "dst_s"))
                proj = [sb(f"proj{k}", [P, G, D + H3]) for k in range(2)]
                tgt, both = ([sb(f"{n}{k}", [P, G, H3]) for k in range(2)] for n in ("tgt", "both"))
                padded, masked = sb("padded", [P, tiles]), sb("masked", [P, tiles, H3])
                own, whole = sb("own", [P, 1]), sb("whole", [P, 1])
                index_staged, both_done, scored, pool_turn, final = (
                    sem(n) for n in ("index_staged", "both_done", "scored", "pool_turn", "final"))
                proj_in = [[sem(f"proj_in{k}{j}") for j in range(G)] for k in range(2)]
                tgt_in = [[sem(f"tgt_in{k}{j}") for j in range(G)] for k in range(2)]
                p_out = [sem("p_out0"), sem("p_out1")]
                with nc.Block() as block:
                    @block.vector
                    def _(dve):
                        def stage(i, k):
                            n = group(i, k)
                            if reuses(i):
                                dve.wait_ge(p_out[k], i * 16)
                                dve.wait_ge(both_done, n - 1)
                            dve.tensor_copy(src_s[k][:], src_i[:, bass.ds(n * G, G)]).then_inc(index_staged, 1)
                            dve.tensor_copy(dst_s[k][:], dst_i[:, bass.ds(n * G, G)]).then_inc(index_staged, 1)

                        def score(i, k):
                            n = group(i, k)
                            for j in range(G):
                                dve.wait_ge(proj_in[k][j], i * 16 + 16)
                                dve.wait_ge(tgt_in[k][j], i * 16 + 16)
                            if reuses(i):
                                dve.wait_ge(scored, n - 1)
                            dve.tensor_tensor(both[k][:], proj[k][:, :, D:D + H3], tgt[k][:], ALU.add).then_inc(both_done, 1)
                            dve.wait_ge(both_done, n + 1)
                            dve.scalar_tensor_tensor(scores[:, bass.ds(n * G * H3, G * H3)], both[k][:].rearrange("p j h -> p (j h)"),
                                                     0.2, both[k][:].rearrange("p j h -> p (j h)"), ALU.mult, ALU.max).then_inc(scored, 1)
                        pipeline(dve, pairs, (0, stage), (1, score))
                        dve.wait_ge(scored, groups)
                        dve.tensor_scalar(padded[:], dkey[:], float(pad_node), LOW, ALU.is_equal, ALU.mult).then_inc(final, 1)
                        dve.wait_ge(final, 1)
                        dve.tensor_tensor(masked[:], scores[:, 0:tiles * H3].rearrange("p (t h) -> p t h", h=H3),
                                          padded[:].unsqueeze(2).to_broadcast([P, tiles, H3]), ALU.add).then_inc(final, 1)
                        dve.wait_ge(final, 2)
                        dve.tensor_reduce(own[:], masked[:].rearrange("p t h -> p (t h)"), AX.X, ALU.max).then_inc(final, 1)
                        dve.wait_ge(final, 4)
                        dve.tensor_scalar(gmax[:], whole[:], -1.0, None, ALU.mult).then_inc(final, 1)
                        dve.wait_ge(final, 5)

                    @block.gpsimd
                    def _(pool):
                        def fetch(i, k):
                            pool.wait_ge(index_staged, group(i, k) * 2 + 2)
                            pool.sem_inc(pool_turn, 1)
                            for j in range(G):
                                for to, table, index, done in ((proj, proj_tab, src_s, proj_in), (tgt, tgt_tab, dst_s, tgt_in)):
                                    pool.indirect_dma_start(
                                        to[k][:, j, :], None, table,
                                        bass.IndirectOffsetOnAxis(index[k][:, j:j + 1].bitcast(U32), 0),
                                    ).then_inc(done[k][j], 16)
                        pipeline(pool, pairs, (0, fetch))
                        pool.wait_ge(final, 3)
                        pool.partition_all_reduce(whole[:], own[:], P, bass.bass_isa.ReduceOp.max).then_inc(final, 1)

                    @block.sync
                    def _(sp):
                        def store(i, k):
                            n = group(i, k)
                            for j in range(G):
                                sp.wait_ge(proj_in[k][j], i * 16 + 16)
                            sp.dma_start(p_edge[bass.ds(n, 1)].squeeze(0).rearrange("p (j d) -> p j d", j=G), proj[k][:, :, 0:D]).then_inc(p_out[k], 16)
                        pipeline(sp, pairs, (0, store))
                        for s in p_out:
                            sp.wait_ge(s, 16 * pairs)
                free()

        def nodes_3():
            with ExitStack() as ctx:
                space = workspace(nc, ctx, "l3_nodes")
                sb, _, sem, free = space
                measure, root, balance, apply_norm, normed = norm_steps(space, "ln", half)
                ag = [sb(f"ag{k}", [P, G, D + H3]) for k in range(RING)]
                den, per = ([sb(f"{n}{k}", [P, G, H3]) for k in range(RING)] for n in ("den", "per"))
                xg, u, last_x = ([sb(f"{n}{k}", [P, G, D]) for k in range(RING)] for n in ("xg", "u", "last_x"))
                a_in, x_in, x_out = ([sem(f"{n}{k}") for k in range(RING)] for n in ("a_in", "x_in", "x_out"))
                raised, inverted, scaled, mixed = (sem(n) for n in ("raised", "inverted", "scaled", "mixed"))
                with nc.Block() as block:
                    @block.sync
                    def _(sp):
                        def load(i, k):
                            n = place(i, k)
                            if reuses(i):
                                sp.wait_ge(mixed, n - RING + 1)
                            sp.dma_start(ag[k][:], by_group(agg3, D + H3)[bass.ds(n, 1)].squeeze(0)).then_inc(a_in[k], 16)
                            sp.dma_start(xg[k][:], by_group(x3b, D)[bass.ds(n, 1)].squeeze(0)).then_inc(x_in[k], 16)

                        def store(i, k):
                            n = place(i, k)
                            sp.wait_ge(normed, n * G + G)
                            sp.dma_start(by_group(out, D)[bass.ds(n, 1)].squeeze(0), last_x[k][:]).then_inc(x_out[k], 16)
                        rotation(sp, groups, (0, load), (6, store))
                        all_out(sp, x_out)

                    @block.vector
                    def _(dve):
                        def scale(i, k):
                            n = place(i, k)
                            dve.wait_ge(a_in[k], i * 16 + 16)
                            dve.tensor_scalar(den[k][:], ag[k][:, :, D:D + H3], 1e-16, None, ALU.add).then_inc(raised, 1)
                            dve.wait_ge(raised, n + 1)
                            dve.reciprocal(per[k][:], den[k][:]).then_inc(inverted, 1)
                            dve.wait_ge(inverted, n + 1)
                            if reuses(i):
                                dve.wait_ge(normed, (n - RING + 1) * G)
                            dve.tensor_tensor(u[k][:].rearrange("p j (h c) -> p j h c", c=C3),
                                              ag[k][:, :, 0:D].rearrange("p j (h c) -> p j h c", c=C3),
                                              per[k][:].unsqueeze(3).to_broadcast([P, G, H3, C3]), ALU.mult).then_inc(scaled, 1)

                        def moments(i, k):
                            dve.wait_ge(mixed, place(i, k) + 1)
                            measure(dve, i, k, u[k])
                        rotation(dve, groups, (4, lambda i, k: balance(dve, i, k)), (1, scale), (3, moments))

                    @block.gpsimd
                    def _(pool):
                        def mix(i, k):
                            n = place(i, k)
                            pool.wait_ge(scaled, n + 1)
                            pool.wait_ge(x_in[k], i * 16 + 16)
                            pool.tensor_tensor(u[k][:], u[k][:], xg[k][:], ALU.add).then_inc(mixed, 1)
                        rotation(pool, groups, (2, mix), (3, lambda i, k: root(pool, i, k)))

                    @block.scalar
                    def _(act):
                        def apply(i, k):
                            if reuses(i):
                                act.wait_ge(x_out[k], i * 16)
                            apply_norm(act, i, k, last_x[k], u[k])
                        rotation(act, groups, (0, apply))
                free()

        load_consts()
        order_consts()
        load_weights()
        gather_sum_edges()
        nodes_0()
        edges_1a()
        edges_1b()
        nodes_1()
        edges_2a()
        turn_logits()
        segment_max()
        weigh_edges("l2_edges_b", agg2, H2, v_edge, C2 ** -0.5, None)
        nodes_2()
        edges_3a()
        weigh_edges("l3_edges_b", agg3, H3, p_edge, 1.0, gmax)
        nodes_3()


_WEIGHTS = ["L0_gnn_W", "L0_gnn_b", "L1_gnn_W1", "L1_gnn_b1", "L1_gnn_gamma", "L1_gnn_beta", "L1_gnn_W2", "L1_gnn_b2",
            "L2_gnn_Wq", "L2_gnn_bq", "L2_gnn_Wk", "L2_gnn_bk", "L2_gnn_Wv", "L2_gnn_bv", "L2_gnn_We", "L2_gnn_Wskip",
            "L2_gnn_bskip", "L2_gnn_g1", "L2_gnn_b1", "L2_gnn_g2", "L2_gnn_b2", "L2_gnn_Wf1", "L2_gnn_bf1",
            "L2_gnn_Wf2", "L2_gnn_bf2", "L3_gnn_W_proj", "L3_gnn_a_src", "L3_gnn_a_tgt", "L3_gnn_bias"]


def kernel(x, src, dst, edge_attr_2, edge_attr_64, **weights):
    import numpy as np
    import concourse.bacc as bacc
    from concourse.bass_utils import run_bass_kernel_spmd

    n_nodes, n_edges = np.shape(x)[0], np.shape(src)[0]
    pairs = -(-(max(n_nodes, n_edges) + 1) // (2 * GE))
    rows = 2 * GE * pairs
    tiles = rows // P

    def padded(a, fill):
        a = np.asarray(a)
        more = np.full((rows - a.shape[0],) + a.shape[1:], fill, a.dtype)
        return np.concatenate([a, more])

    def by_edge(a):
        return np.ascontiguousarray(np.swapaxes(a.reshape((tiles, P) + a.shape[1:]), 0, 1))

    src_p, dst_p = padded(src, rows - 1), padded(dst, rows - 1)
    edge = np.full((1,), -1, dst_p.dtype)
    arrays = {
        "in_x": padded(x, 0),
        "in_src": by_edge(src_p),
        "in_dst": by_edge(dst_p),
        "in_dst_line": np.concatenate([edge, dst_p, edge])[None],
        "in_ea2": np.ascontiguousarray(np.swapaxes(padded(edge_attr_2, 0).reshape(rows // GE, GE, 2), 1, 2)),
        "in_ea64": np.ascontiguousarray(np.swapaxes(padded(edge_attr_64, 0).reshape(rows // GE, GE, ED), 1, 2)),
    }
    for name in _WEIGHTS:
        arrays[f"in_{name}"] = np.ascontiguousarray(np.asarray(weights[name]))
    nc = bacc.Bacc("TRN2", target_bir_lowering=False, num_devices=1)
    aps = {name: nc.dram_tensor(name, a.shape, mybir.dt.from_np(a.dtype), kind="ExternalInput").ap()
           for name, a in arrays.items()}
    out = nc.dram_tensor("out_rows", (rows, D), F32, kind="ExternalOutput").ap()
    gnn(nc, *(aps[f"in_{n}"] for n in ("x", "src", "dst", "dst_line", "ea2", "ea64")),
        {n: aps[f"in_{n}"] for n in _WEIGHTS}, out, n_edges)
    result = run_bass_kernel_spmd(nc, [arrays], core_ids=[0])
    return result.results[0]["out_rows"][:n_nodes]
```

```python
from contextlib import ExitStack

import concourse.bass as bass
from concourse import mybir

F32 = mybir.dt.float32
BF16 = mybir.dt.bfloat16
I32 = mybir.dt.int32
U32 = mybir.dt.uint32
ALU = mybir.AluOpType
ACT = mybir.ActivationFunctionType
AX = mybir.AxisListType

P = 128
G = 4
GE = G * P
D = 128
H2, C2 = 8, 16
H3, C3 = 4, 32
ED = 64
SLICE = 2 * P
RING = 4
EPS = 1e-5
LOW = -3e38


def pipeline(eng, pairs, *stages):
    most = max(lag for lag, _ in stages)
    start = 1 + (most + 1) // 2
    for n in range(2 * start):
        for lag, step in stages:
            if n >= lag:
                step(*divmod(n - lag, 2))
    with eng.Fori(start, pairs) as i:
        for k in range(2):
            for lag, step in stages:
                step(i + (k - lag) // 2, (k - lag) % 2)
    for n in range(2 * pairs, 2 * pairs + most):
        for lag, step in stages:
            if n - lag < 2 * pairs:
                step(*divmod(n - lag, 2))


def rotation(eng, groups, *stages):
    least = min(lag for lag, _ in stages)
    stages = [(lag - least, step) for lag, step in stages]
    most = max(lag for lag, _ in stages)
    start = -(-(most + RING) // RING)
    whole = max(start, groups // RING)
    for n in range(start * RING):
        for lag, step in stages:
            if 0 <= n - lag < groups:
                step(*divmod(n - lag, RING))
    if whole > start:
        with eng.Fori(start, whole) as i:
            for k in range(RING):
                for lag, step in stages:
                    step(i + (k - lag) // RING, (k - lag) % RING)
    for n in range(whole * RING, groups + most):
        for lag, step in stages:
            if n - lag < groups:
                step(*divmod(n - lag, RING))


def place(i, k):
    return i * RING + k


def follows(i, k, m):
    return not (isinstance(i, int) and i * RING + k < m)


def before(i, k):
    return (i, 0) if k else (i - 1, 1)


def is_first(i, k):
    return isinstance(i, int) and i == 0 and k == 0


def reuses(i):
    return not (isinstance(i, int) and i == 0)


def group(i, k):
    return i * 2 + k


def workspace(nc, ctx, name):
    sems = []

    def sb(n, shape, dt=F32):
        return ctx.enter_context(nc.sbuf_tensor(f"{name}_{n}", shape, dt))

    def ps(n, shape):
        return ctx.enter_context(nc.psum_tensor(f"{name}_{n}", shape, F32))

    def sem(n):
        made = nc.alloc_semaphore(name=f"{name}_{n}")
        sems.append(made)
        return made

    def free():
        nc.clear_and_free_semaphores(sems)
        nc.all_engine_barrier()
    return sb, ps, sem, free


def segment_steps(space, key, prev, table, width, ident, rows_used=None):
    sb, ps, sem, _ = space

    keys = [sb(f"keys{k}", [P, G]) for k in range(2)]
    same = [sb(f"same{k}", [P, G, P]) for k in range(2)]
    cross = [sb(f"cross{k}", [P, G // 2, P]) for k in range(2)]
    carry = [sb(f"carry{k}", [P, G, P]) for k in range(2)]
    rows = [sb(f"rows{k}", [P, G, width]) for k in range(2)]
    keys_t = [ps(f"keys_t{k}", [P, G, P]) for k in range(2)]
    sums = [ps(f"sums{j}", [P, 512]) for j in range(G)]
    keys_staged = sem("keys_staged")
    keys_turned = sem("keys_turned")
    compared = sem("compared")
    summed = sem("summed")
    evacuated = sem("evacuated")
    stored = [sem(f"stored{k}") for k in range(2)]

    def stage_keys(dve, i, k):
        n = group(i, k)
        if reuses(i):
            dve.wait_ge(compared, n * 3 - 3)
        dve.tensor_copy(keys[k][:], key[:, bass.ds(n * G, G)]).then_inc(keys_staged, 1)

    def turn_keys(pe, i, k):
        n = group(i, k)
        pe.wait_ge(keys_staged, n + 1)
        for j in range(G):
            last = pe.transpose(keys_t[k][:, j, :], keys[k][:, j:j + 1].to_broadcast([P, P]),
                                ident[:])
        last.then_inc(keys_turned, 1)

    def compare(dve, i, k):
        n = group(i, k)
        dve.wait_ge(keys_turned, n + 1)
        if reuses(i):
            dve.wait_ge(summed, n * G - G)
        own = key[:, bass.ds(n * G, G)].unsqueeze(2).to_broadcast([P, G, P])
        closing = prev[:, bass.ds(n * G, G)].unsqueeze(2).to_broadcast([P, G, P])
        dve.tensor_tensor(same[k][:], keys_t[k][:], own, ALU.is_equal).then_inc(compared, 1)
        dve.tensor_tensor(cross[k][:], keys_t[k][:].rearrange("p (s t) e -> p s t e", t=2)[:, :, 1, :],
                          keys[k][:].rearrange("p (s t) -> p s t", t=2)[:, :, 0:1].to_broadcast([P, G // 2, P]),
                          ALU.is_equal).then_inc(compared, 1)
        dve.tensor_tensor(carry[k][:], keys_t[k][:], closing, ALU.is_equal).then_inc(compared, 1)

    def total(pe, i, k, messages):
        n = group(i, k)
        pe.wait_ge(compared, n * 3 + 3)
        for j in range(G):
            out = sums[j][:, 0:width]
            alone = is_first(i, k) and j < 2
            if not is_first(i, k):
                pe.wait_ge(evacuated, n * G - G + j + 1)
            if j % 2:
                pe.matmul(out, cross[k][:, j // 2, :], messages[:, j - 1, :], start=True, stop=False)
            ins = pe.matmul(out, same[k][:, j, :], messages[:, j, :], start=(j % 2 == 0), stop=alone)
            if alone:
                ins.then_inc(summed, 1)
        for first in range(0, G, 2):
            if not (is_first(i, k) and first == 0):
                pe.wait_ge(evacuated, n * G + first)
                pi, pk = (i, k) if first else before(i, k)
                for j in (first, first + 1):
                    pe.matmul(sums[j][:, 0:width], carry[k][:, j, :], rows[pk][:, (first - 1) % G, :],
                              start=False, stop=True).then_inc(summed, 1)

    def empty(act, i, k):
        n = group(i, k)
        if reuses(i):
            if rows_used:
                rows_used(act, n)
            else:
                act.wait_ge(stored[k], i * 16)
        for j in range(G):
            act.wait_ge(summed, n * G + j + 1)
            act.copy(rows[k][:, j, :], sums[j][:, 0:width]).then_inc(evacuated, 1)

    def store(sp, i, k):
        n = group(i, k)
        sp.wait_ge(evacuated, n * G + G)
        sp.dma_start(table[bass.ds(n, 1)].squeeze(0), rows[k][:]).then_inc(stored[k], 16)

    def settle(sp, pairs):
        for k in range(2):
            sp.wait_ge(stored[k], 16 * pairs)

    if rows_used:
        return stage_keys, turn_keys, compare, total, empty, rows, summed, evacuated
    return stage_keys, turn_keys, compare, total, empty, store, settle, summed


def norm_steps(space, name, eps=None, half=None):
    def sb(n, s):
        return [space[0](f"{name}_{n}{k}", s) for k in range(RING)]

    def sem(n):
        return space[2](f"{name}_{n}")

    stats = sb("stats", [P, G, 6])
    spread, rstd, shift = (space[0](f"{name}_{n}", [P, RING, G, 1]) for n in ("spread", "rstd", "shift"))
    moments = space[0](f"{name}_moments", [P, RING, G, 2])
    s_stats, s_moments, s_spread = sem("s_stats"), sem("s_moments"), sem("s_spread")
    s_rstd, s_shift, normed, turn = sem("s_rstd"), sem("s_shift"), sem("normed"), sem("turn")

    def measure(dve, i, k, u):
        n = place(i, k)
        if reuses(i):
            dve.wait_ge(normed, (n - RING + 1) * G)
        for j in range(G):
            dve.bn_stats(stats[k][:, j, :], u[:, j, :]).then_inc(s_stats, 1)
        for j in range(G):
            dve.wait_ge(s_stats, n * G + j + 1)
            dve.sem_inc(turn, 1)
            dve.bn_aggr(moments[:, k, j, :], stats[k][:, j, :]).then_inc(s_moments, 1)
        if half is None:
            return
        dve.wait_ge(s_moments, n * G + G)
        dve.tensor_scalar(spread[:, k], moments[:, k, :, 1:2], EPS, None, ALU.add).then_inc(s_spread, 1)

    if half is None:
        deviation = space[0](f"{name}_deviation", [P, RING, G, 1])
        first, square, factor = (space[0](f"{name}_{n}", [P, 2, G, 1]) for n in ("first", "square", "factor"))
        s_newton = sem("s_newton")

    def root_on_act(act, i, k):
        if k % 2:
            act.wait_ge(s_moments, place(i, k) * G + G)
            act.activation(deviation[:, k - 1:k + 1], moments[:, k - 1:k + 1, :, 1:2], ACT.Sqrt, bias=eps[:]).then_inc(s_rstd, 1)

    def balance_newton(dve, i, k):
        if k % 2 == 0:
            return
        m = i * (RING // 2) + k // 2
        both = slice(k - 1, k + 1)
        dve.wait_ge(s_rstd, m + 1)
        dve.reciprocal(first[:], deviation[:, both]).then_inc(s_newton, 1)
        dve.wait_ge(s_newton, m * 5 + 1)
        dve.tensor_tensor(square[:], first[:], first[:], ALU.mult).then_inc(s_newton, 1)
        dve.wait_ge(s_newton, m * 5 + 2)
        dve.scalar_tensor_tensor(factor[:], moments[:, both, :, 1:2], EPS, square[:], ALU.add, ALU.mult).then_inc(s_newton, 1)
        dve.wait_ge(s_newton, m * 5 + 3)
        dve.tensor_scalar(square[:], factor[:], -0.5, 1.5, ALU.mult, ALU.add).then_inc(s_newton, 1)
        dve.wait_ge(s_newton, m * 5 + 4)
        dve.tensor_tensor(rstd[:, both], first[:], square[:], ALU.mult).then_inc(s_newton, 1)
        dve.wait_ge(s_newton, m * 5 + 5)
        dve.scalar_tensor_tensor(shift[:, both], moments[:, both, :, 0:1], -1.0, rstd[:, both],
                                 ALU.mult, ALU.mult).then_inc(s_shift, 2)

    def root(pool, i, k):
        if k % 2:
            pool.wait_ge(s_spread, place(i, k) + 1)
            pool.tensor_tensor(rstd[:, k - 1:k + 1], spread[:, k - 1:k + 1], half[:].unsqueeze(3), ALU.pow).then_inc(s_rstd, 1)

    def balance(dve, i, k):
        dve.wait_ge(s_rstd, i * (RING // 2) + k // 2 + 1)
        dve.scalar_tensor_tensor(shift[:, k], moments[:, k, :, 0:1], -1.0, rstd[:, k],
                                 ALU.mult, ALU.mult).then_inc(s_shift, 1)

    def apply(act, i, k, out, u, some=range(G)):
        n = place(i, k)
        act.wait_ge(s_shift, n + 1)
        for j in some:
            act.activation(out[:, j, :], u[:, j, :], ACT.Identity, bias=shift[:, k, j, :],
                           scale=rstd[:, k, j, :]).then_inc(normed, 1)

    if half is None:
        return measure, root_on_act, balance_newton, apply, normed
    return measure, root, balance, apply, normed


def gnn(nc, x, src, dst, dst_line, ea2, ea64, w, out, n_edges):
    nodes = x.shape[0]
    tiles = src.shape[1]
    edges = tiles * P
    groups = tiles // G
    pairs = groups // 2
    pad_node = nodes - 1
    assert nodes == groups * GE and groups % 2 == 0 and pairs > 3

    top = ExitStack()
    with top:
        def dram(name, shape, dt=F32):
            return nc.dram_tensor(name, shape, dt).ap()

        def sb0(name, shape, dt=F32):
            return top.enter_context(nc.sbuf_tensor(name, shape, dt))

        def all_out(eng, *queues):
            for queue in queues:
                for k in range(RING):
                    eng.wait_ge(queue[k], 16 * len(range(k, groups, RING)))

        agg0, agg2, agg3 = (dram(n, [edges + P, D + h]) for n, h in (("agg0", 0), ("agg2", H2), ("agg3", H3)))
        agg1 = [dram(f"agg1{s}", [nodes + SLICE, D + 1]) for s in range(2)]
        x1, x2b, x3 = dram("x1", [nodes, D]), dram("x2b", [nodes, D]), dram("x3", [nodes, D])
        to_row, to_col = dram("to_row", [nodes, D]), dram("to_col", [nodes, D])
        kv_tab, skip_tab = dram("kv_tab", [nodes, 2 * D]), dram("skip_tab", [nodes, D])
        q_first = dram("q_first", [edges, D])
        proj_tab = dram("proj_tab", [nodes, D + H3])
        tgt_first = dram("tgt_first", [edges, H3])
        h_t = dram("h_t", [groups, P, GE])
        v_edge, p_edge = dram("v_edge", [groups, P, GE]), dram("p_edge", [groups, P, GE])
        logit_t, max_t = dram("logit_t", [tiles, H2, P]), dram("max_t", [tiles, H2, P])
        chunks = max(c for c in range(1, P // H2 + 1) if tiles % c == 0)
        ends, starts = dram("ends", [2, 2, chunks * H2]), dram("starts", [2, chunks * H2])

        def by_group(t, width):
            return t.rearrange("(g p j) d -> g p j d", p=P, j=G)

        def by_edge(t):
            return t[0:edges].rearrange("(g p j) d -> g p j d", p=P, j=G)

        ident = sb0("ident", [P, P])
        half = sb0("half", [P, 2, G])
        is_last, eps = sb0("is_last", [P, 1]), sb0("eps", [P, 1])
        dst_i, src_i = sb0("dst_i", [P, tiles], I32), sb0("src_i", [P, tiles], I32)
        dkey, dprev = sb0("dkey", [P, tiles]), sb0("dprev", [P, tiles])
        skey, sidx = sb0("skey", [P, tiles]), sb0("sidx", [P, tiles], I32)
        scores = sb0("scores", [P, tiles * H2])
        gmax = sb0("gmax", [P, 1])

        node_part, node_col = sb0("node_part", [P, tiles]), sb0("node_col", [P, tiles])
        sum_row, first_row = sb0("sum_row", [P, tiles], I32), sb0("first_row", [P, tiles], I32)
        zeros = sb0("zeros", [P, 8 * (D + 1)])

        def zero_rows(eng, table, at, done):
            view = table[0:nodes].rearrange("(g p j) d -> g p (j d)", p=P, j=8)
            eng.dma_start(view[bass.ds(at, 1)].squeeze(0), zeros[:, 0:8 * table.shape[1]]).then_inc(done, 16)

        def sum_fetcher(space, table, width):
            sb, _, sem, _ = space
            ag = [sb(f"ag{k}", [P, G, width]) for k in range(RING)]
            at = [sb(f"at{k}", [P, G], I32) for k in range(RING)]
            at_staged, turn = sem("at_staged"), sem("fetch_turn")
            a_in = [[sem(f"a_in{k}{j}") for j in range(G)] for k in range(RING)]

            def stage_rows(copy, i, k):
                copy(at[k][:], sum_row[:, bass.ds(place(i, k) * G, G)]).then_inc(at_staged, 1)

            def fetch(pool, i, k):
                pool.wait_ge(at_staged, place(i, k) + 1)
                pool.sem_inc(turn, 1)
                for j in range(G):
                    pool.indirect_dma_start(
                        ag[k][:, j, :], None, table, bass.IndirectOffsetOnAxis(at[k][:, j:j + 1].bitcast(U32), 0),
                    ).then_inc(a_in[k][j], 16)

            def arrived(eng, i, k):
                for j in range(G):
                    eng.wait_ge(a_in[k][j], i * 16 + 16)
            return ag, stage_rows, fetch, arrived

        def load_consts():
            with ExitStack() as ctx:
                space = workspace(nc, ctx, "consts")
                _, _, sem, free = space
                made, loaded, zero_made = sem("made"), [sem(f"loaded{m}") for m in range(2)], sem("zero_made")
                cleared = sem("cleared")
                with nc.Block() as block:
                    @block.gpsimd
                    def _(pool):
                        pool.memset(ident[:], 0.0).then_inc(made, 1)
                        pool.memset(is_last[:], 0.0).then_inc(made, 1)
                        pool.memset(half[:], -0.5).then_inc(made, 1)
                        pool.memset(eps[:], EPS).then_inc(made, 1)
                        pool.wait_ge(made, 4)
                        pool.affine_select(out=ident[:], in_=ident[:], compare_op=ALU.not_equal, fill=1.0, base=0,
                                           pattern=[[-1, P]], channel_multiplier=1).then_inc(made, 1)
                        pool.affine_select(out=is_last[:], in_=is_last[:], compare_op=ALU.not_equal, fill=1.0,
                                           base=1 - P, pattern=[[0, 1]], channel_multiplier=1).then_inc(made, 1)
                        pool.wait_ge(made, 6)

                    @block.vector
                    def _(dve):
                        dve.memset(zeros[:], 0.0).then_inc(zero_made, 1)

                    @block.sync
                    def _(sp):
                        sp.dma_start(dst_i[:], dst).then_inc(loaded[0], 16)
                        sp.dma_start(src_i[:], src).then_inc(loaded[1], 16)
                        for s in loaded:
                            sp.wait_ge(s, 16)

                    @block.scalar
                    def _(act):
                        act.wait_ge(zero_made, 1)
                        for table in (agg0, agg2, agg3):
                            act.dma_start(table[edges:], zeros[:, 0:table.shape[1]]).then_inc(cleared, 16)
                        act.wait_ge(cleared, 48)
                free()

        def order_consts():
            with ExitStack() as ctx:
                space = workspace(nc, ctx, "order")
                sb, _, sem, free = space
                part_i, high_i, low_i = (sb(n, [P, tiles], I32) for n in ("part_i", "high_i", "low_i"))
                high, low = sb("high", [P, tiles]), sb("low", [P, tiles])
                off = sb("off", [P, 1])
                made, step, placed = sem("made"), sem("step"), sem("placed")

                def by_slice(t):
                    return t[:].rearrange("p (s t) -> p s t", t=2)
                with nc.Block() as block:
                    @block.vector
                    def _(dve):
                        dve.tensor_copy(dkey[:], dst_i[:]).then_inc(made, 1)
                        dve.tensor_copy(skey[:], src_i[:]).then_inc(made, 1)
                        dve.memset(dprev[:], -1.0).then_inc(step, 1)
                        dve.tensor_scalar(off[:], is_last[:], 1.0, None, ALU.subtract).then_inc(step, 1)
                        dve.tensor_scalar(part_i[:], dst_i[:], 2, P - 1, ALU.logical_shift_right, ALU.bitwise_and).then_inc(step, 1)
                        dve.tensor_scalar(high_i[:], dst_i[:], 9, None, ALU.logical_shift_right).then_inc(step, 1)
                        dve.tensor_scalar(low_i[:], dst_i[:], G - 1, None, ALU.bitwise_and).then_inc(step, 1)
                        dve.wait_ge(made, 2)
                        dve.wait_ge(step, 5)
                        dve.tensor_scalar(by_slice(dprev)[:, 1:, :], by_slice(dkey)[:, :tiles // 2 - 1, 1:2].to_broadcast(
                            [P, tiles // 2 - 1, 2]), is_last[:], off[:], ALU.mult, ALU.add).then_inc(placed, 1)
                        dve.tensor_copy(node_part[:], part_i[:]).then_inc(placed, 1)
                        dve.tensor_copy(high[:], high_i[:]).then_inc(placed, 1)
                        dve.tensor_scalar(low[:], low_i[:], -tiles / 2, None, ALU.add).then_inc(placed, 1)
                        dve.wait_ge(placed, 4)
                        dve.scalar_tensor_tensor(node_col[:], high[:], float(G), low[:], ALU.mult, ALU.add).then_inc(placed, 1)
                        dve.wait_ge(placed, 5)
                free()

        def locate_sums(count):
            with ExitStack() as ctx:
                space = workspace(nc, ctx, "locate")
                sb, ps, sem, free = space
                by_slot = "p (g j) -> p g j"
                under, all_ones = sb("under", [P, P]), sb("all_ones", [P, P])
                many, last, start, row, has = (sb(n, [P, tiles]) for n in ("many", "last", "start", "row", "has"))
                per_group, before_part, before_group = sb("per_group", [P, groups]), sb("before_part", [P, groups]), sb("before_group", [P, groups + 1])
                whole = sb("whole", [P, groups])
                last_i, high_i, mid_i, low_i = (sb(n, [P, tiles], I32) for n in ("last_i", "high_i", "mid_i", "low_i"))
                high, mid, low = (sb(n, [P, tiles]) for n in ("high", "mid", "low"))
                part_p, whole_p = ps("part_p", [P, groups]), ps("whole_p", [P, groups])
                made, step, summed = sem("made"), sem("step"), sem("summed")
                with nc.Block() as block:
                    @block.gpsimd
                    def _(pool):
                        pool.memset(under[:], 1.0).then_inc(made, 1)
                        pool.memset(all_ones[:], 1.0).then_inc(made, 1)
                        pool.wait_ge(made, 2)
                        pool.affine_select(out=under[:], in_=under[:], compare_op=ALU.is_gt, fill=0.0, base=0,
                                           pattern=[[1, P]], channel_multiplier=-1).then_inc(made, 1)

                    @block.tensor
                    def _(pe):
                        pe.wait_ge(made, 3)
                        pe.wait_ge(step, 2)
                        pe.matmul(part_p[:], under[:], per_group[:], start=True, stop=True).then_inc(summed, 1)
                        pe.matmul(whole_p[:], all_ones[:], per_group[:], start=True, stop=True).then_inc(summed, 1)

                    @block.vector
                    def _(dve):
                        done = 0

                        def chain(ins):
                            nonlocal done
                            ins.then_inc(step, 1)
                            done += 1
                            dve.wait_ge(step, done)
                        chain(dve.tensor_copy(many[:], count[:, 0:tiles]))
                        chain(dve.tensor_reduce(per_group[:], many[:].rearrange(by_slot, j=G), AX.X, ALU.add))
                        chain(dve.memset(before_group[:], 0.0))
                        dve.wait_ge(summed, 2)
                        chain(dve.tensor_copy(whole[:], whole_p[:]))
                        chain(dve.tensor_tensor_scan(before_group[:, 1:], whole[:], whole[:], 0.0, ALU.add, ALU.bypass))
                        chain(dve.tensor_tensor(before_part[:], part_p[:], before_group[:, 0:groups], ALU.add))
                        slots = [last[:].rearrange(by_slot, j=G)[:, :, j] for j in range(G)]
                        for j in range(G):
                            chain(dve.tensor_tensor(slots[j], slots[j - 1] if j else before_part[:],
                                                    many[:].rearrange(by_slot, j=G)[:, :, j], ALU.add))
                        chain(dve.tensor_tensor(start[:], last[:], many[:], ALU.subtract))
                        chain(dve.tensor_scalar(last[:], last[:], 1.0, 0.0, ALU.subtract, ALU.max))
                        chain(dve.tensor_scalar(has[:], many[:], 0.0, None, ALU.is_gt))
                        for edge, to in ((last, sum_row), (start, first_row)):
                            chain(dve.tensor_copy(last_i[:], edge[:]))
                            chain(dve.tensor_scalar(high_i[:], last_i[:], 9, None, ALU.logical_shift_right))
                            chain(dve.tensor_scalar(mid_i[:], last_i[:], 7, G - 1, ALU.logical_shift_right, ALU.bitwise_and))
                            chain(dve.tensor_scalar(low_i[:], last_i[:], P - 1, None, ALU.bitwise_and))
                            chain(dve.tensor_scalar(high[:], high_i[:], float(GE), float(-edges), ALU.mult, ALU.add))
                            chain(dve.tensor_copy(mid[:], mid_i[:]))
                            chain(dve.tensor_copy(low[:], low_i[:]))
                            chain(dve.scalar_tensor_tensor(row[:], low[:], float(G), high[:], ALU.mult, ALU.add))
                            chain(dve.tensor_tensor(row[:], row[:], mid[:], ALU.add))
                            chain(dve.tensor_tensor(row[:], row[:], has[:], ALU.mult))
                            chain(dve.tensor_scalar(to[:], row[:], float(edges), None, ALU.add))
                free()

        def gather_sum_edges(count):
            with ExitStack() as ctx:
                space = workspace(nc, ctx, "l0_edges")
                sb, ps, sem, free = space
                stage_keys, turn_keys, compare, total, empty, store, settle, summed = segment_steps(
                    space, dkey, dprev, by_edge(agg0), D, ident)
                fetched = [sb(f"fetched{k}", [P, G, D]) for k in range(2)]
                index = [sb(f"index{k}", [P, G], I32) for k in range(2)]
                parts, cols = sb("parts", [P, P], BF16), sb("cols", [P, tiles], BF16)
                hot_part = [sb(f"hot_part{k}", [P, G, P], BF16) for k in range(2)]
                hot_col = [sb(f"hot_col{k}", [P, G, tiles], BF16) for k in range(2)]
                index_staged, pool_turn, cleared = sem("index_staged"), sem("pool_turn"), sem("cleared")
                numbered, hot_made, counted = sem("numbered"), sem("hot_made"), sem("counted")
                gathered = [[sem(f"gathered{k}{j}") for j in range(G)] for k in range(2)]
                with nc.Block() as block:
                    @block.vector
                    def _(dve):
                        def stage(i, k):
                            n = group(i, k)
                            if reuses(i):
                                dve.wait_ge(summed, n * G - G)
                            dve.tensor_copy(index[k][:], src_i[:, bass.ds(n * G, G)]).then_inc(index_staged, 1)
                            stage_keys(dve, i, k)

                        def mark(i, k):
                            n = group(i, k)
                            if reuses(i):
                                dve.wait_ge(counted, n - 1)
                            for j in range(G):
                                dve.tensor_scalar(hot_part[k][:, j, :], parts[:], node_part[:, bass.ds(n * G + j, 1)], None,
                                                  ALU.is_equal).then_inc(hot_made, 1)
                                dve.tensor_scalar(hot_col[k][:, j, :], cols[:], node_col[:, bass.ds(n * G + j, 1)], None,
                                                  ALU.is_equal).then_inc(hot_made, 1)
                        dve.wait_ge(numbered, 2)
                        pipeline(dve, pairs, (0, stage), (0, lambda i, k: compare(dve, i, k)), (0, mark))

                    @block.gpsimd
                    def _(pool):
                        exact = {"allow_small_or_imprecise_dtypes": True}
                        pool.iota(parts[:], [[1, P]], base=0, channel_multiplier=0, **exact).then_inc(numbered, 1)
                        pool.iota(cols[:], [[1, tiles]], base=-tiles // 2, channel_multiplier=0, **exact).then_inc(numbered, 1)

                        def step(i, k):
                            pool.wait_ge(index_staged, group(i, k) + 1)
                            pool.sem_inc(pool_turn, 1)
                            for j in range(G):
                                pool.indirect_dma_start(
                                    fetched[k][:, j, :], None, x,
                                    bass.IndirectOffsetOnAxis(index[k][:, j:j + 1].bitcast(U32), 0),
                                ).then_inc(gathered[k][j], 16)
                        pipeline(pool, pairs, (0, step))

                    @block.tensor
                    def _(pe):
                        def step(i, k):
                            for j in range(G):
                                pe.wait_ge(gathered[k][j], i * 16 + 16)
                            total(pe, i, k, fetched[k])

                        def tally(i, k):
                            n = group(i, k)
                            for j in range(G):
                                pe.wait_ge(hot_made, (n * G + j) * 2 + 2)
                                last = pe.matmul(count[:, 0:tiles], hot_part[k][:, j, :], hot_col[k][:, j, :],
                                                 start=is_first(i, k) and j == 0, stop=True, skip_group_check=True)
                            last.then_inc(counted, 1)
                        pipeline(pe, pairs, (0, lambda i, k: turn_keys(pe, i, k)), (1, step), (0, tally))
                        pe.wait_ge(counted, groups)

                    @block.scalar
                    def _(act):
                        pipeline(act, pairs, (0, lambda i, k: empty(act, i, k)))

                    @block.sync
                    def _(sp):
                        def clear(i, k):
                            sp.wait_ge(index_staged, group(i, k) + 1)
                            zero_rows(sp, agg1[k], i, cleared)
                        for table in agg1:
                            sp.dma_start(table[nodes:].rearrange("(p j) d -> p (j d)", p=P),
                                         zeros[:, 0:SLICE // P * (D + 1)]).then_inc(cleared, 16)
                        pipeline(sp, pairs, (0, clear), (1, lambda i, k: store(sp, i, k)))
                        settle(sp, pairs)
                        sp.wait_ge(cleared, 16 * (2 * pairs + 2))
                free()

        w0_t = sb0("w0_t", [P, D])
        w1_ab, w1_c, w1_2 = sb0("w1_ab", [P, 2 * D]), sb0("w1_c", [2, D]), sb0("w1_2", [P, D])
        w_qkvs, w_e = sb0("w_qkvs", [P, 4 * D]), sb0("w_e", [ED, D])
        w_f1, w_f2 = sb0("w_f1", [P, 4 * D]), sb0("w_f2", [P, 4, D])
        w_proj = sb0("w_proj", [P, D + 2 * H3])
        b_0, b_11, b_12 = sb0("b_0", [P, D]), sb0("b_11", [P, D]), sb0("b_12", [P, D])
        b_qkvs, g_2, b_2, b_3 = (sb0(n, [P, m * D]) for n, m in (("b_qkvs", 4), ("g_2", 1), ("b_2", 1), ("b_3", 1)))
        gamma, beta, g_1, b_1, b_f1, b_f2 = (sb0(n, [P, m]) for n, m in (
            ("gamma", 1), ("beta", 1), ("g_1", 1), ("b_1", 1), ("b_f1", 4), ("b_f2", 1)))
        bn_scale, bn_shift = sb0("bn_scale", [P, 1]), sb0("bn_shift", [P, 1])

        def load_weights():
            with ExitStack() as ctx:
                space = workspace(nc, ctx, "weights")
                sb, ps, sem, free = space
                w0, proj_t, attend = sb("w0", [P, D]), sb("proj_t", [P, D]), sb("attend", [P, 2 * H3])
                turned, mixed = ps("turned", [P, 2, P]), ps("mixed", [P, 2 * H3])
                loaded, cleared, attend_loaded = sem("loaded"), sem("cleared"), sem("attend_loaded")
                s_turned, s_copied, s_mixed, s_done = sem("s_turned"), sem("s_copied"), sem("s_mixed"), sem("s_done")

                def row(name):
                    return w[name].rearrange("(a n) -> a n", a=1).to_broadcast([P, D])

                def column(name, m=1):
                    return w[name].rearrange("(m p) -> p m", p=P)
                plain = [(w0[:], w["L0_gnn_W"]), (w1_ab[:, 0:D], w["L1_gnn_W1"][0:D, :]),
                         (w1_ab[:, D:2 * D], w["L1_gnn_W1"][D:2 * D, :]), (w1_c[:], w["L1_gnn_W1"][2 * D:2 * D + 2, :]),
                         (w1_2[:], w["L1_gnn_W2"]), (w_e[:], w["L2_gnn_We"]), (w_f1[:], w["L2_gnn_Wf1"]),
                         (w_f2[:], w["L2_gnn_Wf2"].rearrange("(c p) n -> p c n", p=P)),
                         (w_proj[:, 0:D], w["L3_gnn_W_proj"]),
                         (b_0[:], row("L0_gnn_b")), (b_11[:], row("L1_gnn_b1")), (b_12[:], row("L1_gnn_b2")),
                         (g_2[:], row("L2_gnn_g2")), (b_2[:], row("L2_gnn_b2")),
                         (b_3[:], row("L3_gnn_bias"))]
                for m, n in enumerate(("q", "k", "v", "skip")):
                    plain.append((w_qkvs[:, m * D:(m + 1) * D], w[f"L2_gnn_W{n}"]))
                    plain.append((b_qkvs[:, m * D:(m + 1) * D], row(f"L2_gnn_b{n}")))
                columns = [(gamma, "L1_gnn_gamma"), (beta, "L1_gnn_beta"), (g_1, "L2_gnn_g1"), (b_1, "L2_gnn_b1"),
                           (b_f1, "L2_gnn_bf1"), (b_f2, "L2_gnn_bf2")]
                total = 16 * (len(plain) + len(columns))
                with nc.Block() as block:
                    @block.sync
                    def _(sp):
                        for to, frm in plain:
                            sp.dma_start(to, frm).then_inc(loaded, 16)
                        with nc.allow_non_contiguous_dma(reason="short columns, once"):
                            for to, name in columns:
                                sp.dma_start(to[:], column(name)).then_inc(loaded, 16)
                            sp.wait_ge(cleared, 1)
                            for m, name in enumerate(("L3_gnn_a_src", "L3_gnn_a_tgt")):
                                for h in range(H3):
                                    sp.dma_start(attend[h * C3:(h + 1) * C3, m * H3 + h:m * H3 + h + 1],
                                                 w[name][0, h, :].rearrange("(c a) -> c a", a=1)).then_inc(attend_loaded, 16)
                        sp.wait_ge(loaded, total)
                        sp.wait_ge(attend_loaded, 16 * 2 * H3)

                    @block.vector
                    def _(dve):
                        dve.memset(attend[:], 0.0).then_inc(cleared, 1)
                        dve.wait_ge(loaded, total)
                        dve.tensor_tensor(w_qkvs[:, 3 * D:4 * D], w_qkvs[:, 3 * D:4 * D], ident[:], ALU.add).then_inc(s_done, 1)
                        dve.wait_ge(s_turned, 2)
                        dve.tensor_copy(w0_t[:], turned[:, 0, :]).then_inc(s_copied, 1)
                        dve.tensor_copy(proj_t[:], turned[:, 1, :]).then_inc(s_copied, 1)
                        dve.wait_ge(s_mixed, 1)
                        dve.tensor_copy(w_proj[:, D:D + 2 * H3], mixed[:]).then_inc(s_done, 1)
                        dve.wait_ge(s_done, 2)

                    @block.tensor
                    def _(pe):
                        pe.wait_ge(loaded, total)
                        pe.transpose(turned[:, 0, :], w0[:], ident[:]).then_inc(s_turned, 1)
                        pe.transpose(turned[:, 1, :], w_proj[:, 0:D], ident[:]).then_inc(s_turned, 1)
                        pe.wait_ge(s_copied, 2)
                        pe.wait_ge(attend_loaded, 16 * 2 * H3)
                        pe.matmul(mixed[:], proj_t[:], attend[:], start=True, stop=True).then_inc(s_mixed, 1)
                free()

        def nodes_0():
            with ExitStack() as ctx:
                space = workspace(nc, ctx, "l0_nodes")
                sb, ps, sem, free = space
                measure, root, balance, apply_norm, normed = norm_steps(space, "ln", eps=eps)
                ag, stage_rows, fetch, arrived = sum_fetcher(space, agg0, D)
                xg, ag_t, u, x1s, x1_t, row_s, col_s = (
                    [sb(f"{n}{k}", [P, G, D]) for k in range(RING)]
                    for n in ("xg", "ag_t", "u", "x1s", "x1_t", "row_s", "col_s"))
                turn_a, turn_b = ps("turn_a", [P, G, P]), ps("turn_b", [P, G, P])
                y, row_p, col_p = ([ps(f"{n}{m}", [P, G, D]) for m in range(2)] for n in ("y", "row_p", "col_p"))
                x_in, x1_out, row_out, col_out = (
                    [sem(f"{n}{k}") for k in range(RING)] for n in ("x_in", "x1_out", "row_out", "col_out"))
                a_turned, a_copied, y_done, biased, mixed = (
                    sem(n) for n in ("a_turned", "a_copied", "y_done", "biased", "mixed"))
                x_turned, x_copied, ab_done, row_done, col_done = (
                    sem(n) for n in ("x_turned", "x_copied", "ab_done", "row_done", "col_done"))
                with nc.Block() as block:
                    @block.sync
                    def _(sp):
                        def load(i, k):
                            n = place(i, k)
                            if reuses(i):
                                sp.wait_ge(mixed, n - RING + 1)
                            sp.dma_start(xg[k][:], by_group(x, D)[bass.ds(n, 1)].squeeze(0)).then_inc(x_in[k], 16)

                        def store_x1(i, k):
                            n = place(i, k)
                            sp.wait_ge(normed, n * G + G)
                            sp.dma_start(by_group(x1, D)[bass.ds(n, 1)].squeeze(0), x1s[k][:]).then_inc(x1_out[k], 16)

                        def store(i, k):
                            n = place(i, k)
                            sp.wait_ge(row_done, n + 1)
                            sp.dma_start(by_group(to_row, D)[bass.ds(n, 1)].squeeze(0), row_s[k][:]).then_inc(row_out[k], 16)
                            sp.wait_ge(col_done, n + 1)
                            sp.dma_start(by_group(to_col, D)[bass.ds(n, 1)].squeeze(0), col_s[k][:]).then_inc(col_out[k], 16)
                        rotation(sp, groups, (1, load), (8, store_x1), (11, store))
                        all_out(sp, x1_out, row_out, col_out)

                    @block.tensor
                    def _(pe):
                        def turn(i, k):
                            n = place(i, k)
                            arrived(pe, i, k)
                            if follows(i, k, 1):
                                pe.wait_ge(a_copied, n)
                            for j in range(G):
                                last = pe.transpose(turn_a[:, j, :], ag[k][:, j, :], ident[:])
                            last.then_inc(a_turned, 1)

                        def project(i, k):
                            n = place(i, k)
                            pe.wait_ge(a_copied, n + 1)
                            if follows(i, k, 2):
                                pe.wait_ge(biased, n - 1)
                            for j in range(G):
                                last = pe.matmul(y[k % 2][:, j, :], ag_t[k][:, j, :], w0_t[:], start=True, stop=True)
                            last.then_inc(y_done, 1)

                        def turn_x1(i, k):
                            n = place(i, k)
                            pe.wait_ge(normed, n * G + G)
                            if follows(i, k, 1):
                                pe.wait_ge(x_copied, n)
                            for j in range(G):
                                last = pe.transpose(turn_b[:, j, :], x1s[k][:, j, :], ident[:])
                            last.then_inc(x_turned, 1)

                        def project_x1(i, k):
                            n = place(i, k)
                            pe.wait_ge(x_copied, n + 1)
                            if follows(i, k, 2):
                                pe.wait_ge(row_done, n - 1)
                                pe.wait_ge(col_done, n - 1)
                            for j in range(G):
                                pe.matmul(row_p[k % 2][:, j, :], x1_t[k][:, j, :], w1_ab[:, 0:D], start=True, stop=True)
                                last = pe.matmul(col_p[k % 2][:, j, :], x1_t[k][:, j, :], w1_ab[:, D:2 * D], start=True, stop=True)
                            last.then_inc(ab_done, 1)
                        rotation(pe, groups, (2, turn), (8, turn_x1), (3, project), (9, project_x1))

                    @block.vector
                    def _(dve):
                        def mix(i, k):
                            n = place(i, k)
                            dve.wait_ge(y_done, n + 1)
                            if reuses(i):
                                dve.wait_ge(normed, (n - RING + 1) * G)
                            dve.tensor_tensor(u[k][:], y[k % 2][:], b_0[:].unsqueeze(1).to_broadcast([P, G, D]),
                                              ALU.add).then_inc(biased, 1)
                            dve.wait_ge(x_in[k], i * 16 + 16)
                            dve.wait_ge(biased, n + 1)
                            dve.scalar_tensor_tensor(u[k][:], u[k][:], 0.0, xg[k][:], ALU.max, ALU.add).then_inc(mixed, 1)
                            dve.wait_ge(mixed, n + 1)
                            measure(dve, i, k, u[k])

                        def row(i, k):
                            n = place(i, k)
                            dve.wait_ge(ab_done, n + 1)
                            if reuses(i):
                                dve.wait_ge(row_out[k], i * 16)
                            dve.tensor_tensor(row_s[k][:], row_p[k % 2][:], b_11[:].unsqueeze(1).to_broadcast([P, G, D]),
                                              ALU.add).then_inc(row_done, 1)
                        rotation(dve, groups, (6, lambda i, k: balance(dve, i, k)), (10, row), (4, mix))

                    @block.gpsimd
                    def _(pool):
                        rotation(pool, groups, (0, lambda i, k: fetch(pool, i, k)))

                    @block.scalar
                    def _(act):
                        def stage(i, k):
                            if reuses(i):
                                act.wait_ge(a_turned, place(i, k) - RING + 1)
                            stage_rows(act.copy, i, k)

                        def copy_a(i, k):
                            n = place(i, k)
                            act.wait_ge(a_turned, n + 1)
                            if reuses(i):
                                act.wait_ge(y_done, n - RING + 1)
                            act.copy(ag_t[k][:], turn_a[:]).then_inc(a_copied, 1)

                        def copy_x1(i, k):
                            n = place(i, k)
                            act.wait_ge(x_turned, n + 1)
                            if reuses(i):
                                act.wait_ge(ab_done, n - RING + 1)
                            act.copy(x1_t[k][:], turn_b[:]).then_inc(x_copied, 1)

                        def col(i, k):
                            n = place(i, k)
                            act.wait_ge(ab_done, n + 1)
                            if reuses(i):
                                act.wait_ge(col_out[k], i * 16)
                            act.copy(col_s[k][:], col_p[k % 2][:]).then_inc(col_done, 1)

                        def apply(i, k):
                            n = place(i, k)
                            if reuses(i):
                                act.wait_ge(x1_out[k], i * 16)
                                act.wait_ge(x_turned, n - RING + 1)
                            apply_norm(act, i, k, x1s[k], u[k])
                        rotation(act, groups, (0, stage), (5, lambda i, k: root(act, i, k)), (2, copy_a), (8, copy_x1), (7, apply), (10, col))
                free()

        def edges_1a():
            valid = n_edges - (groups - 1) * GE
            with ExitStack() as ctx:
                space = workspace(nc, ctx, "l1_edges_a")
                sb, ps, sem, free = space
                row_i, col_i = ([sb(f"{n}{k}", [P, G], I32) for k in range(2)] for n in ("row_i", "col_i"))
                ea_t = [sb(f"ea_t{k}", [2, GE]) for k in range(2)]
                keys = [sb(f"keys{k}", [P, G]) for k in range(2)]
                keys_t = [ps(f"keys_t{k}", [P, G, P]) for k in range(2)]
                weight, own, spare = sb("weight", [P, SLICE]), sb("own", [P, G]), sb("spare", [P, G])
                heavy = [sb(f"heavy{k}", [P, G, SLICE]) for k in range(2)]
                heaviest, gap = sb("heaviest", [P, tiles]), sb("gap", [P, tiles])
                at_row, at_col, both, h_s = ([sb(f"{n}{k}", [P, G, D]) for k in range(2)]
                                             for n in ("at_row", "at_col", "both", "h_s"))
                stats, moments, spread, rstd = sb("stats", [P, groups, 6]), sb("moments", [P, 2]), sb("spread", [P, 1]), sb("rstd", [P, 1])
                h = [ps(f"h{k}", [P, G, P]) for k in range(2)]
                index_staged, added, keys_staged, keys_turned, matched, picked, numbered = (
                    sem(n) for n in ("index_staged", "added", "keys_staged", "keys_turned", "matched", "picked", "numbered"))
                ea_in, cleared = [sem("ea_in0"), sem("ea_in1")], sem("cleared")
                h_done, h_copied, measured, pool_turn, final = (
                    sem(n) for n in ("h_done", "h_copied", "measured", "pool_turn", "final"))
                row_in = [[sem(f"row_in{k}{j}") for j in range(G)] for k in range(2)]
                col_in = [[sem(f"col_in{k}{j}") for j in range(G)] for k in range(2)]
                h_out = [sem("h_out0"), sem("h_out1")]
                with nc.Block() as block:
                    @block.vector
                    def _(dve):
                        def stage(i, k):
                            n = group(i, k)
                            if reuses(i):
                                dve.wait_ge(added, n - 1)
                            dve.tensor_copy(row_i[k][:], src_i[:, bass.ds(n * G, G)]).then_inc(index_staged, 1)
                            dve.tensor_copy(col_i[k][:], dst_i[:, bass.ds(n * G, G)]).then_inc(index_staged, 1)
                            if reuses(i):
                                dve.wait_ge(keys_turned, n - 1)
                                dve.wait_ge(matched, n * G - G)
                            dve.tensor_copy(keys[k][:], skey[:, bass.ds(n * G, G)]).then_inc(keys_staged, 1)

                        def add(i, k):
                            n = group(i, k)
                            if reuses(i):
                                dve.wait_ge(h_done, n - 1)
                            for j in range(G):
                                dve.wait_ge(row_in[k][j], i * 16 + 16)
                                dve.wait_ge(col_in[k][j], i * 16 + 16)
                            dve.tensor_tensor(both[k][:], at_row[k][:], at_col[k][:], ALU.add).then_inc(added, 1)

                        def match(i, k):
                            n = group(i, k)
                            dve.wait_ge(keys_turned, n + 1)
                            if reuses(i):
                                dve.wait_ge(picked, n - 1)
                            for j in range(G):
                                at = j - j % 2
                                dve.scalar_tensor_tensor(
                                    heavy[k][:, j, :], keys_t[k][:, at:at + 2, :].rearrange("p j e -> p (j e)"), keys[k][:, j:j + 1],
                                    weight[:], ALU.is_equal, ALU.mult).then_inc(matched, 1)

                        def pick(i, k):
                            n = group(i, k)
                            dve.wait_ge(matched, n * G + G)
                            dve.tensor_reduce(heaviest[:, bass.ds(n * G, G)], heavy[k][:], AX.X, ALU.max).then_inc(picked, 1)

                        def measure(i, k):
                            n = group(i, k)
                            dve.wait_ge(h_copied, n + 1)
                            dve.bn_stats(stats[:, bass.ds(n, 1), :].squeeze(1), h_s[k][:].rearrange("p j e -> p (j e)")
                                         ).then_inc(measured, 1)
                        dve.wait_ge(numbered, 3)
                        pipeline(dve, pairs, (2, add), (0, stage), (1, match), (2, measure), (1, pick))
                        dve.wait_ge(picked, groups)
                        by_slot = "p (g j) -> p g j"
                        own_all = own[:].unsqueeze(1).to_broadcast([P, groups, G])
                        spare_all = spare[:].unsqueeze(1).to_broadcast([P, groups, G])
                        dve.tensor_tensor(heaviest[:].rearrange(by_slot, j=G), heaviest[:].rearrange(by_slot, j=G),
                                          own_all, ALU.is_equal).then_inc(picked, 1)
                        dve.tensor_tensor(gap[:].rearrange(by_slot, j=G), skey[:].rearrange(by_slot, j=G), spare_all,
                                          ALU.subtract).then_inc(picked, 1)
                        dve.wait_ge(picked, groups + 2)
                        dve.tensor_tensor(gap[:], gap[:], heaviest[:], ALU.mult).then_inc(picked, 1)
                        dve.wait_ge(picked, groups + 3)
                        dve.tensor_tensor(sidx[:].rearrange(by_slot, j=G), gap[:].rearrange(by_slot, j=G), spare_all,
                                          ALU.add).then_inc(picked, 1)
                        dve.wait_ge(picked, groups + 4)
                        dve.wait_ge(measured, groups)
                        dve.wait_ge(h_copied, groups)
                        dve.bn_stats(stats[:, groups - 1, :], h_s[1][:].rearrange("p j e -> p (j e)")[:, 0:valid]).then_inc(final, 1)
                        dve.wait_ge(final, 1)
                        dve.bn_aggr(moments[:], stats[:].rearrange("p g s -> p (g s)")).then_inc(final, 1)
                        dve.wait_ge(final, 2)
                        dve.tensor_scalar(spread[:], moments[:, 1:2], EPS, None, ALU.add).then_inc(final, 1)
                        dve.wait_ge(final, 4)
                        dve.tensor_tensor(bn_scale[:], gamma[:], rstd[:], ALU.mult).then_inc(final, 1)
                        dve.wait_ge(final, 5)
                        dve.tensor_tensor(spread[:], moments[:, 0:1], bn_scale[:], ALU.mult).then_inc(final, 1)
                        dve.wait_ge(final, 6)
                        dve.tensor_tensor(bn_shift[:], beta[:], spread[:], ALU.subtract).then_inc(final, 1)
                        dve.wait_ge(final, 7)

                    @block.gpsimd
                    def _(pool):
                        exact = {"allow_small_or_imprecise_dtypes": True}
                        pool.iota(weight[:], [[-1, SLICE]], base=SLICE, channel_multiplier=0, **exact).then_inc(numbered, 1)
                        pool.iota(own[:], [[0, G // 2], [-P, 2]], base=SLICE, channel_multiplier=-1, **exact).then_inc(numbered, 1)
                        pool.iota(spare[:], [[0, G // 2], [P, 2]], base=nodes, channel_multiplier=1, **exact).then_inc(numbered, 1)

                        def fetch(i, k):
                            pool.wait_ge(index_staged, group(i, k) * 2 + 2)
                            pool.sem_inc(pool_turn, 1)
                            for j in range(G):
                                for to, table, index, done in ((at_row, to_row, row_i, row_in), (at_col, to_col, col_i, col_in)):
                                    pool.indirect_dma_start(
                                        to[k][:, j, :], None, table,
                                        bass.IndirectOffsetOnAxis(index[k][:, j:j + 1].bitcast(U32), 0),
                                    ).then_inc(done[k][j], 16)
                        pipeline(pool, pairs, (0, fetch))
                        pool.wait_ge(final, 3)
                        pool.tensor_tensor(rstd[:], spread[:], half[:, 0, 0:1], ALU.pow).then_inc(final, 1)

                    @block.tensor
                    def _(pe):
                        def turn(i, k):
                            n = group(i, k)
                            pe.wait_ge(keys_staged, n + 1)
                            if reuses(i):
                                pe.wait_ge(matched, n * G - G)
                            for j in range(G):
                                last = pe.transpose(keys_t[k][:, j, :], keys[k][:, j:j + 1].to_broadcast([P, P]), ident[:])
                            last.then_inc(keys_turned, 1)

                        def mix(i, k):
                            n = group(i, k)
                            pe.wait_ge(ea_in[k], i * 16 + 16)
                            pe.wait_ge(added, n + 1)
                            if reuses(i):
                                pe.wait_ge(h_copied, n - 1)
                            pe.matmul(h[k][:], w1_c[:], ea_t[k][:], start=True, stop=False, skip_group_check=True)
                            for j in range(G):
                                last = pe.matmul(h[k][:, j, :], both[k][:, j, :], ident[:], start=False, stop=True,
                                                 skip_group_check=True)
                            last.then_inc(h_done, 1)
                        pipeline(pe, pairs, (0, turn), (1, mix))

                    @block.scalar
                    def _(act):
                        def copy_h(i, k):
                            n = group(i, k)
                            act.wait_ge(h_done, n + 1)
                            if reuses(i):
                                act.wait_ge(h_out[k], i * 16)
                                act.wait_ge(measured, n - 1)
                            act.copy(h_s[k][:], h[k][:]).then_inc(h_copied, 1)
                        pipeline(act, pairs, (0, copy_h))

                    @block.sync
                    def _(sp):
                        def load(i, k):
                            n = group(i, k)
                            if reuses(i):
                                sp.wait_ge(h_done, n - 1)
                            sp.dma_start(ea_t[k][:], ea2[bass.ds(n, 1)].squeeze(0)).then_inc(ea_in[k], 16)

                        def clear(i, k):
                            zero_rows(sp, q_first if k else tgt_first, i, cleared)

                        def store(i, k):
                            n = group(i, k)
                            sp.wait_ge(h_copied, n + 1)
                            sp.dma_start(h_t[bass.ds(n, 1)].squeeze(0), h_s[k][:].rearrange("p j e -> p (j e)")).then_inc(h_out[k], 16)
                        pipeline(sp, pairs, (0, load), (1, store), (1, clear))
                        sp.wait_ge(cleared, 16 * 2 * pairs)
                        for s in h_out:
                            sp.wait_ge(s, 16 * pairs)
                free()

        def edges_1b():
            width = D + 1
            with ExitStack() as ctx:
                space = workspace(nc, ctx, "l1_edges_b")
                sb, ps, sem, free = space
                keys = [sb(f"keys{k}", [P, G]) for k in range(2)]
                same = [sb(f"same{k}", [P, G, SLICE]) for k in range(2)]
                rows = [sb(f"rows{k}", [P, G, width]) for k in range(2)]
                at = [sb(f"at{k}", [P, G], I32) for k in range(2)]
                h_s, live = ([sb(f"{n}{k}", [P, GE]) for k in range(2)] for n in ("h_s", "live"))
                msg = [sb(f"msg{k}", [P, G, width]) for k in range(2)]
                keys_t, product = ([ps(f"{n}{k}", [P, G, P]) for k in range(2)] for n in ("keys_t", "product"))
                sums = [ps(f"sums{m}", [P, 512]) for m in range(4)]
                h_in = [sem("h_in0"), sem("h_in1")]
                relu_done, product_done, msg_done, ones_set = (
                    sem(n) for n in ("relu_done", "product_done", "msg_done", "ones_set"))
                keys_staged, keys_turned, compared, summed, evacuated, at_staged, pool_turn = (
                    sem(n) for n in ("keys_staged", "keys_turned", "compared", "summed", "evacuated", "at_staged", "pool_turn"))
                added = [[sem(f"added{k}{j}") for j in range(G)] for k in range(2)]
                with nc.Block() as block:
                    @block.sync
                    def _(sp):
                        def load(i, k):
                            n = group(i, k)
                            if reuses(i):
                                sp.wait_ge(relu_done, n - 1)
                            sp.dma_start(h_s[k][:], h_t[bass.ds(n, 1)].squeeze(0)).then_inc(h_in[k], 16)
                        pipeline(sp, pairs, (0, load))

                    @block.scalar
                    def _(act):
                        def relu(i, k):
                            n = group(i, k)
                            act.wait_ge(h_in[k], i * 16 + 16)
                            if reuses(i):
                                act.wait_ge(product_done, n - 1)
                            act.activation(live[k][:], h_s[k][:], ACT.Relu, bias=bn_shift[:], scale=bn_scale[:]).then_inc(relu_done, 1)

                        def empty(i, k):
                            n = group(i, k)
                            if reuses(i):
                                for j in range(G):
                                    act.wait_ge(added[k][j], i * 16)
                            act.copy(at[k][:], sidx[:, bass.ds(n * G, G)]).then_inc(at_staged, 1)
                            for j in range(G):
                                act.wait_ge(summed, n * G + j + 1)
                                act.copy(rows[k][:, j, :], sums[j][:, 0:width]).then_inc(evacuated, 1)
                        pipeline(act, pairs, (0, relu), (2, empty))

                    @block.tensor
                    def _(pe):
                        def turn_keys(i, k):
                            n = group(i, k)
                            pe.wait_ge(keys_staged, n + 1)
                            if reuses(i):
                                pe.wait_ge(compared, n * G - G)
                            for j in range(G):
                                last = pe.transpose(keys_t[k][:, j, :], keys[k][:, j:j + 1].to_broadcast([P, P]), ident[:])
                            last.then_inc(keys_turned, 1)

                        def multiply(i, k):
                            n = group(i, k)
                            pe.wait_ge(relu_done, n + 1)
                            if reuses(i):
                                pe.wait_ge(msg_done, n - 1)
                            for j in range(G):
                                last = pe.matmul(product[k][:, j, :], live[k][:, j * P:(j + 1) * P], w1_2[:], start=True, stop=True)
                            last.then_inc(product_done, 1)

                        def total(i, k):
                            n = group(i, k)
                            pe.wait_ge(msg_done, n + 1)
                            pe.wait_ge(compared, n * G + G)
                            for j in range(G):
                                if not is_first(i, k):
                                    pe.wait_ge(evacuated, n * G - G + j + 1)
                                half_at = (j % 2) * P
                                for step, frm in enumerate((j - j % 2, j - j % 2 + 1)):
                                    last = pe.matmul(sums[j][:, 0:width], same[k][:, frm, half_at:half_at + P], msg[k][:, frm, :],
                                                     start=(step == 0), stop=(step == 1))
                                last.then_inc(summed, 1)
                        pe.wait_ge(ones_set, 2)
                        pipeline(pe, pairs, (0, turn_keys), (1, multiply), (2, total))

                    @block.vector
                    def _(dve):
                        def stage_keys(i, k):
                            n = group(i, k)
                            if reuses(i):
                                dve.wait_ge(compared, n * G - G)
                            dve.tensor_copy(keys[k][:], skey[:, bass.ds(n * G, G)]).then_inc(keys_staged, 1)

                        def compare(i, k):
                            n = group(i, k)
                            dve.wait_ge(keys_turned, n + 1)
                            if reuses(i):
                                dve.wait_ge(summed, n * G - G)
                            for j in range(G):
                                at_slice = j - j % 2
                                dve.tensor_scalar(same[k][:, j, :], keys_t[k][:, at_slice:at_slice + 2, :].rearrange("p j e -> p (j e)"),
                                                  keys[k][:, j:j + 1], None, ALU.is_equal).then_inc(compared, 1)

                        def add(i, k):
                            n = group(i, k)
                            dve.wait_ge(product_done, n + 1)
                            if reuses(i):
                                dve.wait_ge(summed, n * G - G)
                            dve.tensor_tensor(msg[k][:, :, 0:D], product[k][:], b_12[:].unsqueeze(1).to_broadcast([P, G, D]),
                                              ALU.add).then_inc(msg_done, 1)
                        for k in range(2):
                            dve.memset(msg[k][:, :, D:width], 1.0).then_inc(ones_set, 1)
                        pipeline(dve, pairs, (0, stage_keys), (1, compare), (1, add))

                    @block.gpsimd
                    def _(pool):
                        def add_rows(i, k):
                            n = group(i, k)
                            pool.wait_ge(at_staged, n + 1)
                            pool.sem_inc(pool_turn, 1)
                            for j in range(G):
                                pool.wait_ge(evacuated, n * G + j + 1)
                                pool.sem_inc(pool_turn, 1)
                                if j % 2 == 0 and not is_first(i, k):
                                    pi, pk = before(i, k)
                                    for m in (j, j + 1):
                                        pool.wait_ge(added[pk][m], pi * 16 + 16)
                                        pool.sem_inc(pool_turn, 1)
                                pool.indirect_dma_start(
                                    agg1[j // 2], bass.IndirectOffsetOnAxis(at[k][:, j:j + 1].bitcast(U32), 0),
                                    rows[k][:, j, :], None, compute_op=ALU.add,
                                ).then_inc(added[k][j], 16)
                        pipeline(pool, pairs, (0, add_rows))
                        for k in range(2):
                            for j in range(G):
                                pool.wait_ge(added[k][j], 16 * pairs)
                free()

        def nodes_1():
            with ExitStack() as ctx:
                space = workspace(nc, ctx, "l1_nodes")
                sb, ps, sem, free = space
                measure, root, balance, apply_norm, normed = norm_steps(space, "ln", half=half)
                ag, ag_odd = ([sb(f"{n}{k}", [P, G, D + 1]) for k in range(RING)] for n in ("ag", "ag_odd"))
                count, per = ([sb(f"{n}{k}", [P, G, 1]) for k in range(RING)] for n in ("count", "per"))
                xg, u, x2s, x2_t, x2b_s = ([sb(f"{n}{k}", [P, G, D]) for k in range(RING)]
                                           for n in ("xg", "u", "x2s", "x2_t", "x2b_s"))
                qkvs = [sb(f"qkvs{m}", [P, G, 4 * D]) for m in range(2)]
                turn = [ps(f"turn{m}", [P, G, P]) for m in range(2)]
                y = [ps(f"y{j}", [P, 4 * D]) for j in range(G)]
                a_in, a_odd_in, x_in, x2b_out = (
                    [sem(f"{n}{k}") for k in range(RING)] for n in ("a_in", "a_odd_in", "x_in", "x2b_out"))
                kv_out, skip_out = ([sem(f"{n}{k}") for k in range(RING)] for n in ("kv_out", "skip_out"))
                first_s = [sb(f"first_s{k}", [P, G], I32) for k in range(RING)]
                q_out = [[sem(f"q_out{k}{j}") for j in range(G)] for k in range(RING)]
                first_staged, pool_turn = sem("first_staged"), sem("pool_turn")
                joined, counted, inverted, scaled, mixed, turned = (
                    sem(n) for n in ("joined", "counted", "inverted", "scaled", "mixed", "turned"))
                copied, y_done, biased, x2b_done = (sem(n) for n in ("copied", "y_done", "biased", "x2b_done"))
                with nc.Block() as block:
                    @block.sync
                    def _(sp):
                        def load(i, k):
                            n = place(i, k)
                            if reuses(i):
                                sp.wait_ge(scaled, (n - RING + 1) * G)
                            for to, table, done in ((ag, agg1[0], a_in), (ag_odd, agg1[1], a_odd_in)):
                                sp.dma_start(to[k][:], by_group(table[0:nodes], D + 1)[bass.ds(n, 1)].squeeze(0)).then_inc(done[k], 16)
                            if reuses(i):
                                sp.wait_ge(mixed, n - RING + 1)
                            sp.dma_start(xg[k][:], by_group(x1, D)[bass.ds(n, 1)].squeeze(0)).then_inc(x_in[k], 16)

                        def store(i, k):
                            n = place(i, k)
                            sp.wait_ge(x2b_done, n + 1)
                            sp.dma_start(by_group(x2b, D)[bass.ds(n, 1)].squeeze(0), x2b_s[k][:]).then_inc(x2b_out[k], 16)
                            sp.wait_ge(biased, n * G + G)
                            whole = qkvs[k % 2]
                            sp.dma_start(by_group(kv_tab, 2 * D)[bass.ds(n, 1)].squeeze(0), whole[:, :, D:3 * D]).then_inc(kv_out[k], 16)
                            sp.dma_start(by_group(skip_tab, D)[bass.ds(n, 1)].squeeze(0), whole[:, :, 3 * D:4 * D]).then_inc(skip_out[k], 16)
                        rotation(sp, groups, (0, load), (10, store))
                        all_out(sp, kv_out, skip_out, x2b_out)

                    @block.vector
                    def _(dve):
                        def invert(i, k):
                            n = place(i, k)
                            for j in (a_in[k], a_odd_in[k]):
                                dve.wait_ge(j, i * 16 + 16)
                            dve.tensor_tensor(ag[k][:], ag[k][:], ag_odd[k][:], ALU.add).then_inc(joined, 1)
                            dve.wait_ge(joined, n + 1)
                            dve.tensor_scalar(count[k][:], ag[k][:, :, D:D + 1], 1.0, None, ALU.add).then_inc(counted, 1)
                            dve.wait_ge(counted, n + 1)
                            if reuses(i):
                                dve.wait_ge(scaled, (n - RING + 1) * G)
                            dve.reciprocal(per[k][:], count[k][:]).then_inc(inverted, 1)

                        def mix(i, k):
                            n = place(i, k)
                            dve.wait_ge(scaled, n * G + G)
                            dve.wait_ge(x_in[k], i * 16 + 16)
                            dve.scalar_tensor_tensor(u[k][:], xg[k][:], 2.0, u[k][:], ALU.mult, ALU.add).then_inc(mixed, 1)
                            dve.wait_ge(mixed, n + 1)
                            measure(dve, i, k, u[k])

                        def bias(i, k):
                            n = place(i, k)
                            if follows(i, k, 2):
                                pi, pk = (i, k - 2) if k >= 2 else (i - 1, k + 2)
                                for s in (*q_out[pk], kv_out[pk], skip_out[pk]):
                                    dve.wait_ge(s, pi * 16 + 16)
                            for j in range(G):
                                dve.wait_ge(y_done, n * G + j + 1)
                                dve.tensor_tensor(qkvs[k % 2][:, j, :], y[j][:], b_qkvs[:], ALU.add).then_inc(biased, 1)
                        rotation(dve, groups, (6, lambda i, k: balance(dve, i, k)), (2, invert), (3, mix), (8, bias))

                    @block.gpsimd
                    def _(pool):
                        def scatter_q(i, k):
                            n = place(i, k)
                            pool.wait_ge(first_staged, n + 1)
                            pool.sem_inc(pool_turn, 1)
                            pool.wait_ge(biased, n * G + G)
                            pool.sem_inc(pool_turn, 1)
                            for j in range(G):
                                pool.indirect_dma_start(
                                    q_first, bass.IndirectOffsetOnAxis(first_s[k][:, j:j + 1].bitcast(U32), 0),
                                    qkvs[k % 2][:, j, 0:D], None, bounds_check=edges - 1, oob_is_err=False,
                                ).then_inc(q_out[k][j], 16)

                        def shift(i, k):
                            n = place(i, k)
                            if reuses(i):
                                pool.wait_ge(x2b_out[k], i * 16)
                            pool.wait_ge(normed, n * G + G)
                            pool.tensor_tensor(x2b_s[k][:], x2s[k][:], b_2[:].unsqueeze(1).to_broadcast([P, G, D]),
                                               ALU.add).then_inc(x2b_done, 1)
                        rotation(pool, groups, (4, lambda i, k: root(pool, i, k)), (9, scatter_q), (7, shift))
                        for j in range(G):
                            all_out(pool, [q_out[k][j] for k in range(RING)])

                    @block.scalar
                    def _(act):
                        def stage(i, k):
                            if reuses(i):
                                for j in range(G):
                                    act.wait_ge(q_out[k][j], i * 16)
                            act.copy(first_s[k][:], first_row[:, bass.ds(place(i, k) * G, G)]).then_inc(first_staged, 1)

                        def scale(i, k):
                            n = place(i, k)
                            act.wait_ge(inverted, n + 1)
                            if reuses(i):
                                act.wait_ge(normed, (n - RING + 1) * G)
                            for j in range(G):
                                act.activation(u[k][:, j, :], ag[k][:, j, 0:D], ACT.Copy, scale=per[k][:, j, :]).then_inc(scaled, 1)

                        def copy(i, k):
                            n = place(i, k)
                            act.wait_ge(turned, n + 1)
                            if reuses(i):
                                act.wait_ge(y_done, (n - RING + 1) * G)
                            act.copy(x2_t[k][:], turn[k % 2][:]).then_inc(copied, 1)

                        def apply(i, k):
                            n = place(i, k)
                            if reuses(i):
                                act.wait_ge(turned, n - RING + 1)
                                act.wait_ge(x2b_done, n - RING + 1)
                            apply_norm(act, i, k, x2s[k], u[k])
                        rotation(act, groups, (7, copy), (6, apply), (2, scale), (7, stage))

                    @block.tensor
                    def _(pe):
                        def turn_x(i, k):
                            n = place(i, k)
                            pe.wait_ge(normed, n * G + G)
                            if follows(i, k, 2):
                                pe.wait_ge(copied, n - 1)
                            for j in range(G):
                                last = pe.transpose(turn[k % 2][:, j, :], x2s[k][:, j, :], ident[:])
                            last.then_inc(turned, 1)

                        def project(i, k):
                            n = place(i, k)
                            pe.wait_ge(copied, n + 1)
                            for j in range(G):
                                if follows(i, k, 1):
                                    pe.wait_ge(biased, n * G - G + j + 1)
                                pe.matmul(y[j][:], x2_t[k][:, j, :], w_qkvs[:], start=True, stop=True).then_inc(y_done, 1)
                        rotation(pe, groups, (7, turn_x), (8, project))
                free()

        def edges_2a():
            wide = 2 * G * H2
            with ExitStack() as ctx:
                space = workspace(nc, ctx, "l2_edges_a")
                sb, ps, sem, free = space
                src_s = [sb(f"src_s{k}", [P, G], I32) for k in range(2)]
                kv, q = [sb(f"kv{k}", [P, G, 2 * D]) for k in range(2)], [sb(f"q{k}", [P, G, D]) for k in range(2)]
                ea_t = [sb(f"ea_t{k}", [ED, G, P]) for k in range(2)]
                key_e, v_e, prod = ([sb(f"{n}{k}", [P, G, D]) for k in range(2)] for n in ("key_e", "v_e", "prod"))
                e = ps("e", [P, G, D])
                index_staged, e_done, v_done, k_done, prod_done, scored, pool_turn = (
                    sem(n) for n in ("index_staged", "e_done", "v_done", "k_done", "prod_done", "scored", "pool_turn"))
                kv_in = [[sem(f"kv_in{k}{j}") for j in range(G)] for k in range(2)]
                q_in = [sem("q_in0"), sem("q_in1")]
                stage_keys, turn_keys, compare, total, empty, q_rows, summed, evacuated = segment_steps(
                    space, dkey, dprev, None, D, ident, lambda eng, n: eng.wait_ge(prod_done, n - 1))
                ea_in, v_out = [sem("ea_in0"), sem("ea_in1")], [sem("v_out0"), sem("v_out1")]
                flat, turned, turn = sb("flat", [P, wide]), sb("turned", [wide, P]), ps("turn", [wide, 512])
                s_flat, s_turn, s_copied, pe_turn, logit_out = (
                    sem(n) for n in ("s_flat", "s_turn", "s_copied", "pe_turn", "logit_out"))
                logit_rows = logit_t.rearrange("(m j) h e -> m (j h) e", j=2 * G)
                with nc.Block() as block:
                    @block.vector
                    def _(dve):
                        def stage(i, k):
                            n = group(i, k)
                            if reuses(i):
                                dve.wait_ge(v_done, n - 1)
                            dve.tensor_copy(src_s[k][:], src_i[:, bass.ds(n * G, G)]).then_inc(index_staged, 1)
                            stage_keys(dve, i, k)

                        def add_e(i, k):
                            n = group(i, k)
                            dve.wait_ge(e_done, n + 1)
                            for j in range(G):
                                dve.wait_ge(kv_in[k][j], i * 16 + 16)
                            if reuses(i):
                                dve.wait_ge(scored, n - 1)
                            dve.tensor_tensor(key_e[k][:], kv[k][:, :, 0:D], e[:], ALU.add).then_inc(k_done, 1)
                            if reuses(i):
                                dve.wait_ge(v_out[k], i * 16)
                            dve.tensor_tensor(v_e[k][:], kv[k][:, :, D:2 * D], e[:], ALU.add).then_inc(v_done, 1)

                        def score(i, k):
                            n = group(i, k)
                            dve.wait_ge(k_done, n + 1)
                            dve.wait_ge(evacuated, n * G + G)
                            dve.tensor_tensor(prod[k][:], key_e[k][:], q_rows[k][:], ALU.mult).then_inc(prod_done, 1)
                            dve.wait_ge(prod_done, n + 1)
                            dve.tensor_reduce(scores[:, bass.ds(n * G * H2, G * H2)],
                                              prod[k][:].rearrange("p j (h c) -> p (j h) c", c=C2), AX.X,
                                              ALU.add).then_inc(scored, 1)

                        def flatten(i, k):
                            if k == 0:
                                return
                            dve.wait_ge(scored, group(i, k) + 1)
                            if reuses(i):
                                dve.wait_ge(s_turn, i)
                            dve.tensor_copy(flat[:], scores[:, bass.ds(i * wide, wide)]).then_inc(s_flat, 1)
                        pipeline(dve, pairs, (2, add_e), (0, stage), (1, lambda i, k: compare(dve, i, k)), (2, score), (2, flatten))
                        dve.wait_ge(scored, groups)

                    @block.gpsimd
                    def _(pool):
                        def fetch(i, k):
                            pool.wait_ge(index_staged, group(i, k) + 1)
                            pool.sem_inc(pool_turn, 1)
                            for j in range(G):
                                pool.indirect_dma_start(
                                    kv[k][:, j, :], None, kv_tab,
                                    bass.IndirectOffsetOnAxis(src_s[k][:, j:j + 1].bitcast(U32), 0),
                                ).then_inc(kv_in[k][j], 16)
                        pipeline(pool, pairs, (0, fetch))

                    @block.tensor
                    def _(pe):
                        def edge(i, k):
                            n = group(i, k)
                            pe.wait_ge(ea_in[k], i * 16 + 16)
                            if not is_first(i, k):
                                pe.wait_ge(v_done, n)
                            for j in range(G):
                                last = pe.matmul(e[:, j, :], ea_t[k][:, j, :], w_e[:], start=True, stop=True)
                            last.then_inc(e_done, 1)

                        def turn_logits(i, k):
                            if k == 0:
                                return
                            pe.wait_ge(s_flat, i + 1)
                            pe.sem_inc(pe_turn, 1)
                            if reuses(i):
                                pe.wait_ge(s_copied, i)
                                pe.sem_inc(pe_turn, 1)
                            pe.transpose(turn[:, 0:P], flat[:], ident[:]).then_inc(s_turn, 1)
                        
                        def spread_q(i, k):
                            pe.wait_ge(q_in[k], i * 16 + 16)
                            total(pe, i, k, q[k])
                        pipeline(pe, pairs, (0, lambda i, k: turn_keys(pe, i, k)), (1, edge), (1, spread_q), (3, turn_logits))

                    @block.scalar
                    def _(act):
                        def copy_logits(i, k):
                            if k == 0:
                                return
                            act.wait_ge(s_turn, i + 1)
                            if reuses(i):
                                act.wait_ge(logit_out, i * 16)
                            act.copy(turned[:], turn[:, 0:P]).then_inc(s_copied, 1)
                        
                        def load(i, k):
                            n = group(i, k)
                            if reuses(i):
                                act.wait_ge(summed, n * G - G)
                            act.dma_start(q[k][:], by_edge(q_first)[bass.ds(n, 1)].squeeze(0)).then_inc(q_in[k], 16)
                            if reuses(i):
                                act.wait_ge(e_done, n - 1)
                            act.dma_start(ea_t[k][:].rearrange("p j e -> p (j e)"), ea64[bass.ds(n, 1)].squeeze(0)).then_inc(ea_in[k], 16)
                        pipeline(act, pairs, (2, lambda i, k: empty(act, i, k)), (0, load), (4, copy_logits))

                    @block.sync
                    def _(sp):
                        def store(i, k):
                            n = group(i, k)
                            sp.wait_ge(v_done, n + 1)
                            sp.dma_start(v_edge[bass.ds(n, 1)].squeeze(0), v_e[k][:].rearrange("p j d -> p (j d)")).then_inc(v_out[k], 16)

                        def store_logits(i, k):
                            if k == 0:
                                return
                            sp.wait_ge(s_copied, i + 1)
                            sp.dma_start(logit_rows[bass.ds(i, 1)].squeeze(0), turned[:]).then_inc(logit_out, 16)
                        pipeline(sp, pairs, (0, store), (2, store_logits))
                        sp.wait_ge(logit_out, 16 * pairs)
                        for s in v_out:
                            sp.wait_ge(s, 16 * pairs)
                free()

        def segment_max():
            lanes, span = chunks * H2, edges // chunks
            per = tiles // chunks
            with ExitStack() as ctx:
                space = workspace(nc, ctx, "segment_max")
                sb, _, sem, free = space
                keys = sb("keys", [lanes, span + 2], I32)
                logit = sb("logit", [lanes, span])
                reset = [sb("reset_f", [lanes, span]), sb("reset_b", [lanes, span])]
                best = [sb("best_f", [lanes, span]), sb("best_b", [lanes, span])]
                through = [sb(f"through{d}", [lanes, 1]) for d in range(2)]
                end_s, through_s, carry_s = ([sb(f"{n}{d}", [H2, chunks]) for d in range(2)]
                                             for n in ("end_s", "through_s", "carry_s"))
                start_s = [sb(f"start_s{d}", [H2, chunks]) for d in range(2)]
                entry = [sb(f"entry{d}", [lanes, 1]) for d in range(2)]
                loaded, step, saved, fetched, started, entered, out_done = (
                    sem(n) for n in ("loaded", "step", "saved", "fetched", "started", "entered", "out_done"))
                saved = [sem(f"saved{d}") for d in range(2)]
                fetched = [sem(f"fetched{d}") for d in range(2)]
                started = [sem(f"started{d}") for d in range(2)]
                entered = [sem(f"entered{d}") for d in range(2)]
                scanned, spread = [sem("scanned0"), sem("scanned1")], [sem("spread0"), sem("spread1")]
                line = logit_t.rearrange("(c t) h e -> c h t e", c=chunks)
                out_line = max_t.rearrange("(c t) h e -> c h t e", c=chunks)
                by_head = "(c h) -> h c"
                with nc.Block() as block:
                    @block.sync
                    def _(sp):
                        for c in range(chunks):
                            rows = slice(c * H2, (c + 1) * H2)
                            sp.dma_start(logit[rows, :].rearrange("h (t e) -> h t e", t=per), line[c]).then_inc(loaded, 16)
                            sp.dma_start(keys[rows, :], dst_line[0:1, c * span:c * span + span + 2].to_broadcast(
                                [H2, span + 2])).then_inc(loaded, 16)
                        with nc.allow_non_contiguous_dma(reason="one word for each chunk and head"):
                            for d in range(2):
                                last = best[d][:, span - 1:span] if d == 0 else best[d][:, 0:1]
                                sp.wait_ge(scanned[d], 1)
                                sp.dma_start(ends[d, 0].rearrange("(l a) -> l a", a=1), last).then_inc(saved[d], 16)
                                sp.dma_start(ends[d, 1].rearrange("(l a) -> l a", a=1), through[d][:]).then_inc(saved[d], 16)
                                sp.wait_ge(saved[d], 32)
                                sp.dma_start(end_s[d][:], ends[d, 0].rearrange(by_head, h=H2)).then_inc(fetched[d], 16)
                                sp.dma_start(through_s[d][:], ends[d, 1].rearrange(by_head, h=H2)).then_inc(fetched[d], 16)
                                sp.wait_ge(spread[d], 1)
                                sp.dma_start(starts[d].rearrange(by_head, h=H2), start_s[d][:]).then_inc(started[d], 16)
                                sp.wait_ge(started[d], 16)
                                sp.dma_start(entry[d][:], starts[d].rearrange("(l a) -> l a", a=1)).then_inc(entered[d], 16)
                        sp.wait_ge(scanned[1], 2)
                        for c in range(chunks):
                            rows = slice(c * H2, (c + 1) * H2)
                            sp.dma_start(out_line[c], best[1][rows, :].rearrange("h (t e) -> h t e", t=per)).then_inc(out_done, 16)
                        sp.wait_ge(out_done, 16 * chunks)

                    @block.vector
                    def _(dve):
                        done = 0

                        def chain(ins):
                            nonlocal done
                            ins.then_inc(step, 1)
                            done += 1
                            dve.wait_ge(step, done)
                        dve.wait_ge(loaded, 32 * chunks)
                        for d in range(2):
                            other = keys[:, 0:span] if d == 0 else keys[:, 2:span + 2]
                            chain(dve.tensor_tensor(reset[d][:], keys[:, 1:span + 1], other, ALU.is_equal))
                            chain(dve.tensor_scalar(reset[d][:], reset[d][:], -LOW, LOW, ALU.mult, ALU.add))
                            chain(dve.tensor_reduce(through[d][:], reset[d][:], AX.X, ALU.min))

                        def scan(d, initial):
                            frm = logit if d == 0 else best[0]
                            way = slice(None) if d == 0 else slice(None, None, -1)
                            return dve.tensor_tensor_scan(best[d][:, way], reset[d][:, way], frm[:, way], initial,
                                                          ALU.add, ALU.max)
                        for d in range(2):
                            scan(d, LOW).then_inc(scanned[d], 1)
                            dve.wait_ge(fetched[d], 32)
                            way = slice(None) if d == 0 else slice(None, None, -1)
                            chain(dve.tensor_tensor_scan(carry_s[d][:, way], through_s[d][:, way], end_s[d][:, way], LOW,
                                                         ALU.add, ALU.max))
                            chain(dve.memset(start_s[d][:], LOW))
                            if chunks > 1:
                                to, frm = (slice(1, None), slice(0, -1)) if d == 0 else (slice(0, -1), slice(1, None))
                                chain(dve.tensor_copy(start_s[d][:, to], carry_s[d][:, frm]))
                            dve.sem_inc(spread[d], 1)
                            dve.wait_ge(entered[d], 16)
                            scan(d, entry[d][:]).then_inc(scanned[d], 1)
                            dve.wait_ge(scanned[d], 2)
                free()

        def weigh_edges(name, seg_table, heads, source, scale, minus):
            c = D // heads
            with ExitStack() as ctx:
                space = workspace(nc, ctx, name)
                sb, ps, sem, free = space
                stage_keys, turn_keys, compare, total, empty, store, settle, summed = segment_steps(
                    space, dkey, dprev, by_edge(seg_table), D + heads, ident)
                v = [sb(f"v{k}", [P, G, D]) for k in range(2)]
                top_t = [sb(f"top_t{k}", [G * heads, P]) for k in range(2)]
                diff, ex = ([sb(f"{n}{k}", [P, G * heads]) for k in range(2)] for n in ("diff", "ex"))
                msg = [sb(f"msg{k}", [P, G, D + heads]) for k in range(2)]
                peak = [ps(f"peak{k}", [P, 512]) for k in range(2)]
                v_in, top_in = [sem("v_in0"), sem("v_in1")], [sem("top_in0"), sem("top_in1")]
                peaked, differed, risen, weighed, pe_turn = (
                    sem(n) for n in ("peaked", "differed", "risen", "weighed", "pe_turn"))
                rows = max_t.rearrange("(g j) h e -> g (j h) e", j=G)
                with nc.Block() as block:
                    @block.sync
                    def _(sp):
                        def load_peaks(i, k):
                            n = group(i, k)
                            if reuses(i):
                                sp.wait_ge(peaked, n - 1)
                            sp.dma_start(top_t[k][:], rows[bass.ds(n, 1)].squeeze(0)).then_inc(top_in[k], 16)

                        def load(i, k):
                            n = group(i, k)
                            if reuses(i):
                                sp.wait_ge(weighed, n * 2 - 2)
                            sp.dma_start(v[k][:].rearrange("p j d -> p (j d)"), source[bass.ds(n, 1)].squeeze(0)).then_inc(v_in[k], 16)
                        stages = [(4, lambda i, k: store(sp, i, k)), (1, load)]
                        if minus is None:
                            stages.insert(0, (0, load_peaks))
                        pipeline(sp, pairs, *stages)
                        settle(sp, pairs)

                    @block.tensor
                    def _(pe):
                        def turn_peaks(i, k):
                            n = group(i, k)
                            pe.wait_ge(top_in[k], i * 16 + 16)
                            pe.sem_inc(pe_turn, 1)
                            if reuses(i):
                                pe.wait_ge(differed, n - 1)
                                pe.sem_inc(pe_turn, 1)
                            pe.transpose(peak[k][:, 0:G * heads], top_t[k][:], ident[0:G * heads, 0:G * heads]).then_inc(peaked, 1)

                        def total_messages(i, k):
                            pe.wait_ge(weighed, group(i, k) * 2 + 2)
                            total(pe, i, k, msg[k])
                        stages = [(0, lambda i, k: turn_keys(pe, i, k)), (2, total_messages)]
                        if minus is None:
                            stages.insert(0, (0, turn_peaks))
                        pipeline(pe, pairs, *stages)

                    @block.vector
                    def _(dve):
                        def differ(i, k):
                            n = group(i, k)
                            dve.wait_ge(peaked, n + 1)
                            if reuses(i):
                                dve.wait_ge(risen, n - 1)
                            dve.tensor_tensor(diff[k][:], scores[:, bass.ds(n * G * heads, G * heads)],
                                              peak[k][:, 0:G * heads], ALU.subtract).then_inc(differed, 1)

                        def weigh(i, k):
                            n = group(i, k)
                            dve.wait_ge(risen, n + 1)
                            dve.wait_ge(v_in[k], i * 16 + 16)
                            if reuses(i):
                                dve.wait_ge(summed, n * G - G)
                            for_heads = ex[k][:].rearrange("p (j h) -> p j h", h=heads)
                            dve.tensor_tensor(msg[k][:, :, 0:D].rearrange("p j (h c) -> p j h c", c=c),
                                              v[k][:].rearrange("p j (h c) -> p j h c", c=c),
                                              for_heads.unsqueeze(3).to_broadcast([P, G, heads, c]),
                                              ALU.mult).then_inc(weighed, 1)
                            dve.tensor_copy(msg[k][:, :, D:D + heads], for_heads).then_inc(weighed, 1)
                        stages = [(0, lambda i, k: stage_keys(dve, i, k)), (1, lambda i, k: compare(dve, i, k)),
                                  (1, weigh)]
                        if minus is None:
                            stages.insert(1, (0, differ))
                        pipeline(dve, pairs, *stages)

                    @block.scalar
                    def _(act):
                        def rise(i, k):
                            n = group(i, k)
                            if reuses(i):
                                act.wait_ge(weighed, n * 2 - 2)
                            if minus is None:
                                act.wait_ge(differed, n + 1)
                                act.activation(ex[k][:], diff[k][:], ACT.Exp, scale=scale).then_inc(risen, 1)
                            else:
                                act.activation(ex[k][:], scores[:, bass.ds(n * G * heads, G * heads)], ACT.Exp,
                                               bias=minus[:], scale=scale).then_inc(risen, 1)
                        pipeline(act, pairs, (0, rise), (2, lambda i, k: empty(act, i, k)))

                free()

        def nodes_2():
            with ExitStack() as ctx:
                space = workspace(nc, ctx, "l2_nodes")
                sb, ps, sem, free = space
                measure_a, root_a, balance_a, norm_a, a_normed = norm_steps(space, "na", half=half)
                measure_b, root_b, balance_b, norm_b, b_normed = norm_steps(space, "nb", half=half)
                measure_x, root_x, balance_x, norm_x, x_normed = norm_steps(space, "nx", half=half)
                ag, stage_rows, fetch, arrived = sum_fetcher(space, agg2, D + H2)
                den, per = ([sb(f"{n}{k}", [P, G, H2]) for k in range(RING)] for n in ("den", "per"))
                skip, x2g, ua, h_t_s, ub, ux, x3s = (
                    [sb(f"{n}{k}", [P, G, D]) for k in range(RING)] for n in (
                        "skip", "x2g", "ua", "h_t_s", "ub", "ux", "x3s"))
                normed_a, normed_b, x3_t = (
                    [sb(f"{n}{m}", [P, G, D]) for m in range(2)] for n in ("normed_a", "normed_b", "x3_t"))
                x3_s, biased = [sb(f"x3_s{m}", [P, G, D]) for m in range(2)], sem("biased")
                first_s = [sb(f"first_s{k}", [P, G], I32) for k in range(RING)]
                act_t = [sb(f"act_t{m}", [P, 4, GE]) for m in range(2)]
                ext = [sb(f"ext{m}", [P, G, D + 2 * H3]) for m in range(2)]
                ub_t = [sb(f"ub_t{m}", [P, G, P]) for m in range(2)]
                turn_h, y, turn_b = ps("turn_h", [P, G, P]), ps("y", [P, GE]), ps("turn_b", [P, G, P])
                f = [ps(f"f{m}", [P, GE]) for m in range(2)]
                pe_ext = [ps(f"pe_ext{m}", [P, 512]) for m in range(2)]
                skip_in, x2_in, ext_out, x3_out = (
                    [sem(f"{n}{k}") for k in range(RING)] for n in ("skip_in", "x2_in", "ext_out", "x3_out"))
                tgt_out = [[sem(f"tgt_out{k}{j}") for j in range(G)] for k in range(RING)]
                first_staged, pool_turn = sem("first_staged"), sem("pool_turn")
                floored, inverted, conv_done, ua_done, h_turned, h_copied = (
                    sem(n) for n in ("floored", "inverted", "conv_done", "ua_done", "h_turned", "h_copied"))
                b_turned, ub_done = sem("b_turned"), sem("ub_done")
                f_done, gelu_done, y_done, ub_t_done, scaled_b, ux_done = (
                    sem(n) for n in ("f_done", "gelu_done", "y_done", "ub_t_done", "scaled_b", "ux_done"))
                x_turned, x_copied, ext_done, ext_copied = (
                    sem(n) for n in ("x_turned", "x_copied", "ext_done", "ext_copied"))

                APART = 11

                def two_back(i, k):
                    return (i, k - 2) if k >= 2 else (i - 1, k + 2)
                with nc.Block() as block:
                    @block.sync
                    def _(sp):
                        def load(i, k):
                            n = place(i, k)
                            if reuses(i):
                                sp.wait_ge(ua_done, n - RING + 1)
                            sp.dma_start(skip[k][:], by_group(skip_tab, D)[bass.ds(n, 1)].squeeze(0)).then_inc(skip_in[k], 16)

                        def load_x2(i, k):
                            n = place(i, k)
                            if reuses(i):
                                sp.wait_ge(ux_done, n - RING + 1)
                            sp.dma_start(x2g[k][:], by_group(x2b, D)[bass.ds(n, 1)].squeeze(0)).then_inc(x2_in[k], 16)

                        def store_x3(i, k):
                            n = place(i, k)
                            sp.wait_ge(biased, n + 1)
                            sp.dma_start(by_group(x3, D)[bass.ds(n, 1)].squeeze(0), x3_s[k % 2][:]).then_inc(x3_out[k], 16)

                        def store(i, k):
                            n = place(i, k)
                            sp.wait_ge(ext_copied, n * 2 + 2)
                            sp.dma_start(by_group(proj_tab, D + H3)[bass.ds(n, 1)].squeeze(0), ext[k % 2][:, :, 0:D + H3]).then_inc(ext_out[k], 16)
                        rotation(sp, groups, (1, load), (11, load_x2), (18, store_x3), (20, store))
                        all_out(sp, x3_out, ext_out)

                    @block.vector
                    def _(dve):
                        def stage(i, k):
                            if reuses(i):
                                dve.wait_ge(conv_done, place(i, k) - RING + 1)
                            stage_rows(dve.tensor_copy, i, k)

                        def add_bias(i, k):
                            n = place(i, k)
                            dve.wait_ge(x_normed, n * G + G)
                            if follows(i, k, 2):
                                pi, pk = two_back(i, k)
                                dve.wait_ge(x3_out[pk], pi * 16 + 16)
                            dve.tensor_tensor(x3_s[k % 2][:], x3s[k][:], b_3[:].unsqueeze(1).to_broadcast([P, G, D]),
                                              ALU.add).then_inc(biased, 1)

                        def stage_first(i, k):
                            if reuses(i):
                                for s in tgt_out[k]:
                                    dve.wait_ge(s, i * 16)
                            dve.tensor_copy(first_s[k][:], first_row[:, bass.ds(place(i, k) * G, G)]).then_inc(first_staged, 1)

                        def conv(i, k):
                            n = place(i, k)
                            arrived(dve, i, k)
                            dve.tensor_scalar(den[k][:], ag[k][:, :, D:D + H2], 1e-30, None, ALU.max).then_inc(floored, 1)
                            dve.wait_ge(floored, n + 1)
                            dve.reciprocal(per[k][:], den[k][:]).then_inc(inverted, 1)
                            dve.wait_ge(inverted, n + 1)
                            if reuses(i):
                                dve.wait_ge(a_normed, (n - RING + 1) * G)
                            dve.tensor_tensor(ua[k][:].rearrange("p j (h c) -> p j h c", c=C2),
                                              ag[k][:, :, 0:D].rearrange("p j (h c) -> p j h c", c=C2),
                                              per[k][:].unsqueeze(3).to_broadcast([P, G, H2, C2]), ALU.mult).then_inc(conv_done, 1)
                            dve.wait_ge(conv_done, n + 1)
                            dve.wait_ge(skip_in[k], i * 16 + 16)
                            dve.tensor_tensor(ua[k][:], ua[k][:], skip[k][:], ALU.add).then_inc(ua_done, 1)
                            dve.wait_ge(ua_done, n + 1)
                            measure_a(dve, i, k, ua[k])

                        def after_ffn(i, k):
                            n = place(i, k)
                            dve.wait_ge(y_done, n + 1)
                            if follows(i, k, 2):
                                dve.wait_ge(b_turned, n - 1)
                            dve.scalar_tensor_tensor(ub_t[k % 2][:].rearrange("p j e -> p (j e)"), y[:], b_f2[:],
                                                     h_t_s[k][:].rearrange("p j e -> p (j e)"), ALU.add, ALU.add).then_inc(ub_t_done, 1)

                        def moments_b(i, k):
                            n = place(i, k)
                            dve.wait_ge(b_turned, n + 1)
                            if reuses(i):
                                dve.wait_ge(b_normed, (n - RING + 1) * G)
                            dve.tensor_copy(ub[k][:], turn_b[:]).then_inc(ub_done, 1)
                            dve.wait_ge(ub_done, n + 1)
                            measure_b(dve, i, k, ub[k])

                        def residual(i, k):
                            n = place(i, k)
                            dve.wait_ge(b_normed, n * G + G)
                            if reuses(i):
                                dve.wait_ge(x_normed, (n - RING + 1) * G)
                            dve.tensor_tensor(ux[k][:], normed_b[k % 2][:], g_2[:].unsqueeze(1).to_broadcast([P, G, D]), ALU.mult).then_inc(scaled_b, 1)
                            dve.wait_ge(scaled_b, n + 1)
                            dve.wait_ge(x2_in[k], i * 16 + 16)
                            dve.tensor_tensor(ux[k][:], ux[k][:], x2g[k][:], ALU.add).then_inc(ux_done, 1)
                            dve.wait_ge(ux_done, n + 1)
                            measure_x(dve, i, k, ux[k])
                        rotation(dve, groups, (0, stage), (2, conv), (9, moments_b), (13, residual), (17, stage_first), (17, add_bias),
                                 (4, lambda i, k: balance_a(dve, i, k)), (11, lambda i, k: balance_b(dve, i, k)),
                                 (15, lambda i, k: balance_x(dve, i, k)), (8, after_ffn))

                    @block.gpsimd
                    def _(pool):
                        def scatter_tgt(i, k):
                            n = place(i, k)
                            pool.wait_ge(first_staged, n + 1)
                            pool.sem_inc(pool_turn, 1)
                            pool.wait_ge(ext_copied, n * 2 + 2)
                            pool.sem_inc(pool_turn, 1)
                            for j in range(G):
                                pool.indirect_dma_start(
                                    tgt_first, bass.IndirectOffsetOnAxis(first_s[k][:, j:j + 1].bitcast(U32), 0),
                                    ext[k % 2][:, j, D + H3:D + 2 * H3], None, bounds_check=edges - 1, oob_is_err=False,
                                ).then_inc(tgt_out[k][j], 16)
                        rotation(pool, groups, (3, lambda i, k: root_a(pool, i, k)), (10, lambda i, k: root_b(pool, i, k)),
                                 (14, lambda i, k: root_x(pool, i, k)), (0, lambda i, k: fetch(pool, i, k)), (19, scatter_tgt))
                        for j in range(G):
                            all_out(pool, [tgt_out[k][j] for k in range(RING)])

                    @block.scalar
                    def _(act):
                        def apply_a(i, k):
                            if follows(i, k, 2):
                                act.wait_ge(h_turned, place(i, k) - 1)
                            norm_a(act, i, k, normed_a[k % 2], ua[k], range(0, G // 2))

                        def apply_a_rest(i, k):
                            norm_a(act, i, k, normed_a[k % 2], ua[k], range(G // 2, G))

                        def copy_h(i, k):
                            n = place(i, k)
                            act.wait_ge(h_turned, n + 1)
                            if reuses(i):
                                act.wait_ge(ub_t_done, n - RING + 1)
                            act.activation(h_t_s[k][:], turn_h[:], ACT.Identity, bias=b_1[:], scale=g_1[:]).then_inc(h_copied, 1)

                        def gelu(i, k):
                            if follows(i, k, 2):
                                act.wait_ge(y_done, place(i, k) - 1)
                            gelu_some(i, k, range(0, 2))

                        def gelu_some(i, k, some=range(2, 4)):
                            n = place(i, k)
                            for m in some:
                                act.wait_ge(f_done, n * 4 + m + 1)
                                act.activation(act_t[k % 2][:, m, :], f[m % 2][:], ACT.Gelu, bias=b_f1[:, m:m + 1]).then_inc(gelu_done, 1)

                        def apply_b(i, k):
                            if follows(i, k, 2):
                                act.wait_ge(scaled_b, place(i, k) - 1)
                            norm_b(act, i, k, normed_b[k % 2], ub[k])

                        def apply_x(i, k):
                            n = place(i, k)
                            if reuses(i):
                                act.wait_ge(x_turned, n - RING + 1)
                                act.wait_ge(biased, n - RING + 1)
                            norm_x(act, i, k, x3s[k], ux[k])

                        def copy_x(i, k):
                            n = place(i, k)
                            act.wait_ge(x_turned, n + 1)
                            if follows(i, k, 2):
                                act.wait_ge(ext_done, n * 2 - 2)
                            act.copy(x3_t[k % 2][:], turn_h[:]).then_inc(x_copied, 1)

                        def copy_ext(i, k):
                            n = place(i, k)
                            if follows(i, k, 2):
                                pi, pk = two_back(i, k)
                                act.wait_ge(ext_out[pk], pi * 16 + 16)
                                for s in tgt_out[pk]:
                                    act.wait_ge(s, pi * 16 + 16)
                            for m in range(2):
                                act.wait_ge(ext_done, n * 2 + m + 1)
                                act.copy(ext[k % 2][:, 2 * m:2 * m + 2, :], pe_ext[m][:, 0:2 * (D + 2 * H3)].rearrange(
                                    "p (j d) -> p j d", j=2)).then_inc(ext_copied, 1)
                        rotation(act, groups, (6, copy_h), (7, gelu), (5, apply_a), (7, gelu_some), (5, apply_a_rest), (12, apply_b),
                                 (17, copy_x), (16, apply_x),
                                 (18, copy_ext))

                    @block.tensor
                    def _(pe):
                        def turn(i, k):
                            n = place(i, k)
                            pe.wait_ge(a_normed, n * G + G)
                            if follows(i, k, 1):
                                pe.wait_ge(h_copied, n)
                            if follows(i, k, APART + 1):
                                pe.wait_ge(x_copied, n - APART)
                            for j in range(G):
                                last = pe.transpose(turn_h[:, j, :], normed_a[k % 2][:, j, :], ident[:])
                            last.then_inc(h_turned, 1)

                        def widen(i, k):
                            n = place(i, k)
                            pe.wait_ge(h_copied, n + 1)
                            for m in range(4):
                                if m >= 2 or follows(i, k, 1):
                                    pe.wait_ge(gelu_done, n * 4 + m - 1)
                                pe.matmul(f[m % 2][:], w_f1[:, m * P:(m + 1) * P], h_t_s[k][:], start=True, stop=True).then_inc(f_done, 1)

                        def narrow(i, k):
                            n = place(i, k)
                            if follows(i, k, 1):
                                pe.wait_ge(ub_t_done, n)
                            pe.wait_ge(gelu_done, n * 4 + 4)
                            for m in range(4):
                                last = pe.matmul(y[:], w_f2[:, m, :], act_t[k % 2][:, m, :], start=(m == 0), stop=(m == 3))
                            last.then_inc(y_done, 1)

                        def turn_back(i, k):
                            n = place(i, k)
                            pe.wait_ge(ub_t_done, n + 1)
                            if follows(i, k, 1):
                                pe.wait_ge(ub_done, n)
                            for j in range(G):
                                last = pe.transpose(turn_b[:, j, :], ub_t[k % 2][:, j, :], ident[:])
                            last.then_inc(b_turned, 1)

                        def turn_x3(i, k):
                            n = place(i, k)
                            pe.wait_ge(x_normed, n * G + G)
                            if follows(i, k, 1):
                                pe.wait_ge(x_copied, n)
                            pe.wait_ge(h_copied, min(n + APART + 1, groups) if isinstance(n, int) else n + APART + 1)
                            for j in range(G):
                                last = pe.transpose(turn_h[:, j, :], x3s[k][:, j, :], ident[:])
                            last.then_inc(x_turned, 1)

                        def project(i, k):
                            n = place(i, k)
                            pe.wait_ge(x_copied, n + 1)
                            for m in range(2):
                                if follows(i, k, 1):
                                    pe.wait_ge(ext_copied, n * 2 - 1 + m)
                                for j in range(2):
                                    at = j * (D + 2 * H3)
                                    last = pe.matmul(pe_ext[m][:, at:at + D + 2 * H3], x3_t[k % 2][:, 2 * m + j, :], w_proj[:],
                                                     start=True, stop=True)
                                last.then_inc(ext_done, 1)
                        rotation(pe, groups, (6, turn), (7, widen), (9, turn_back), (6 + APART, turn_x3), (8, narrow), (18, project))
                free()

        def edges_3a():
            with ExitStack() as ctx:
                space = workspace(nc, ctx, "l3_edges_a")
                sb, ps, sem, free = space
                src_s = [sb(f"src_s{k}", [P, G], I32) for k in range(2)]
                proj = [sb(f"proj{k}", [P, G, D + H3]) for k in range(2)]
                proj_s = [sb(f"proj_s{k}", [P, G, D + H3]) for k in range(2)]
                moved = sem("moved")
                tgt, both = sb("tgt", [P, groups, G, H3]), [sb(f"both{k}", [P, G, H3]) for k in range(2)]
                padded, masked = sb("padded", [P, tiles]), sb("masked", [P, tiles, H3])
                own, whole = sb("own", [P, 1]), sb("whole", [P, 1])
                index_staged, both_done, scored, pool_turn, final = (
                    sem(n) for n in ("index_staged", "both_done", "scored", "pool_turn", "final"))
                proj_in = [[sem(f"proj_in{k}{j}") for j in range(G)] for k in range(2)]
                tgt_in = sem("tgt_in")
                stage_keys, turn_keys, compare, total, empty, tgt_rows, summed, evacuated = segment_steps(
                    space, dkey, dprev, None, H3, ident, lambda eng, n: eng.wait_ge(both_done, n - 1))
                p_out = [sem("p_out0"), sem("p_out1")]
                with nc.Block() as block:
                    @block.vector
                    def _(dve):
                        def stage(i, k):
                            n = group(i, k)
                            if reuses(i):
                                dve.wait_ge(moved, n - 1)
                            dve.tensor_copy(src_s[k][:], src_i[:, bass.ds(n * G, G)]).then_inc(index_staged, 1)
                            stage_keys(dve, i, k)

                        def move(i, k):
                            n = group(i, k)
                            for j in range(G):
                                dve.wait_ge(proj_in[k][j], i * 16 + 16)
                            if reuses(i):
                                dve.wait_ge(p_out[k], i * 16)
                                dve.wait_ge(both_done, n - 1)
                            dve.tensor_copy(proj_s[k][:], proj[k][:]).then_inc(moved, 1)

                        def score(i, k):
                            n = group(i, k)
                            dve.wait_ge(moved, n + 1)
                            dve.wait_ge(evacuated, n * G + G)
                            if reuses(i):
                                dve.wait_ge(scored, n - 1)
                            dve.tensor_tensor(both[k][:], proj_s[k][:, :, D:D + H3], tgt_rows[k][:], ALU.add).then_inc(both_done, 1)
                            dve.wait_ge(both_done, n + 1)
                            dve.scalar_tensor_tensor(scores[:, bass.ds(n * G * H3, G * H3)], both[k][:].rearrange("p j h -> p (j h)"),
                                                     0.2, both[k][:].rearrange("p j h -> p (j h)"), ALU.mult, ALU.max).then_inc(scored, 1)
                        pipeline(dve, pairs, (2, move), (0, stage), (1, lambda i, k: compare(dve, i, k)), (2, score))
                        dve.wait_ge(scored, groups)
                        dve.tensor_scalar(padded[:], dkey[:], float(pad_node), LOW, ALU.is_equal, ALU.mult).then_inc(final, 1)
                        dve.wait_ge(final, 1)
                        dve.tensor_tensor(masked[:], scores[:, 0:tiles * H3].rearrange("p (t h) -> p t h", h=H3),
                                          padded[:].unsqueeze(2).to_broadcast([P, tiles, H3]), ALU.add).then_inc(final, 1)
                        dve.wait_ge(final, 2)
                        dve.tensor_reduce(own[:], masked[:].rearrange("p t h -> p (t h)"), AX.X, ALU.max).then_inc(final, 1)
                        dve.wait_ge(final, 4)
                        dve.tensor_scalar(gmax[:], whole[:], -1.0, None, ALU.mult).then_inc(final, 1)
                        dve.wait_ge(final, 5)

                    @block.gpsimd
                    def _(pool):
                        def fetch(i, k):
                            pool.wait_ge(index_staged, group(i, k) + 1)
                            pool.sem_inc(pool_turn, 1)
                            for j in range(G):
                                pool.indirect_dma_start(
                                    proj[k][:, j, :], None, proj_tab,
                                    bass.IndirectOffsetOnAxis(src_s[k][:, j:j + 1].bitcast(U32), 0),
                                ).then_inc(proj_in[k][j], 16)
                        pipeline(pool, pairs, (0, fetch))
                        pool.wait_ge(final, 3)
                        pool.partition_all_reduce(whole[:], own[:], P, bass.bass_isa.ReduceOp.max).then_inc(final, 1)

                    @block.tensor
                    def _(pe):
                        def spread_tgt(i, k):
                            total(pe, i, k, tgt[:, bass.ds(group(i, k), 1)].squeeze(1))
                        pe.wait_ge(tgt_in, 16)
                        pipeline(pe, pairs, (0, lambda i, k: turn_keys(pe, i, k)), (1, spread_tgt))

                    @block.scalar
                    def _(act):
                        act.dma_start(tgt[:], by_edge(tgt_first).rearrange("g p j h -> p g j h")).then_inc(tgt_in, 16)
                        pipeline(act, pairs, (0, lambda i, k: empty(act, i, k)))

                    @block.sync
                    def _(sp):
                        def store(i, k):
                            n = group(i, k)
                            sp.wait_ge(moved, n + 1)
                            sp.dma_start(p_edge[bass.ds(n, 1)].squeeze(0).rearrange("p (j d) -> p j d", j=G), proj_s[k][:, :, 0:D]).then_inc(p_out[k], 16)
                        pipeline(sp, pairs, (0, store))
                        for s in p_out:
                            sp.wait_ge(s, 16 * pairs)
                free()

        def nodes_3():
            with ExitStack() as ctx:
                space = workspace(nc, ctx, "l3_nodes")
                sb, _, sem, free = space
                measure, root, balance, apply_norm, normed = norm_steps(space, "ln", eps=eps)
                ag, stage_rows, fetch, arrived = sum_fetcher(space, agg3, D + H3)
                den, per = ([sb(f"{n}{k}", [P, G, H3]) for k in range(RING)] for n in ("den", "per"))
                xg, u, last_x = ([sb(f"{n}{k}", [P, G, D]) for k in range(RING)] for n in ("xg", "u", "last_x"))
                x_in, x_out = ([sem(f"{n}{k}") for k in range(RING)] for n in ("x_in", "x_out"))
                raised, inverted, scaled, mixed = (sem(n) for n in ("raised", "inverted", "scaled", "mixed"))
                with nc.Block() as block:
                    @block.sync
                    def _(sp):
                        def load(i, k):
                            n = place(i, k)
                            if reuses(i):
                                sp.wait_ge(mixed, n - RING + 1)
                            sp.dma_start(xg[k][:], by_group(x3, D)[bass.ds(n, 1)].squeeze(0)).then_inc(x_in[k], 16)

                        def store(i, k):
                            n = place(i, k)
                            sp.wait_ge(normed, n * G + G)
                            sp.dma_start(by_group(out, D)[bass.ds(n, 1)].squeeze(0), last_x[k][:]).then_inc(x_out[k], 16)
                        rotation(sp, groups, (1, load), (6, store))
                        all_out(sp, x_out)

                    @block.vector
                    def _(dve):
                        def mix(i, k):
                            n = place(i, k)
                            arrived(dve, i, k)
                            dve.tensor_scalar(den[k][:], ag[k][:, :, D:D + H3], 1e-16, None, ALU.add).then_inc(raised, 1)
                            dve.wait_ge(raised, n + 1)
                            dve.reciprocal(per[k][:], den[k][:]).then_inc(inverted, 1)
                            dve.wait_ge(inverted, n + 1)
                            if reuses(i):
                                dve.wait_ge(normed, (n - RING + 1) * G)
                            dve.tensor_tensor(u[k][:].rearrange("p j (h c) -> p j h c", c=C3),
                                              ag[k][:, :, 0:D].rearrange("p j (h c) -> p j h c", c=C3),
                                              per[k][:].unsqueeze(3).to_broadcast([P, G, H3, C3]), ALU.mult).then_inc(scaled, 1)
                            dve.wait_ge(scaled, n + 1)
                            dve.wait_ge(x_in[k], i * 16 + 16)
                            dve.tensor_tensor(u[k][:], u[k][:], xg[k][:], ALU.add).then_inc(mixed, 1)
                            dve.wait_ge(mixed, n + 1)
                            measure(dve, i, k, u[k])
                        rotation(dve, groups, (4, lambda i, k: balance(dve, i, k)), (2, mix))

                    @block.gpsimd
                    def _(pool):
                        rotation(pool, groups, (0, lambda i, k: fetch(pool, i, k)))

                    @block.scalar
                    def _(act):
                        def stage(i, k):
                            if reuses(i):
                                act.wait_ge(scaled, place(i, k) - RING + 1)
                            stage_rows(act.copy, i, k)

                        def apply(i, k):
                            if reuses(i):
                                act.wait_ge(x_out[k], i * 16)
                            apply_norm(act, i, k, last_x[k], u[k])
                        rotation(act, groups, (0, stage), (3, lambda i, k: root(act, i, k)), (5, apply))
                free()

        load_consts()
        order_consts()
        load_weights()
        with nc.psum_tensor("count", [P, 512], F32) as count:
            gather_sum_edges(count)
            locate_sums(count)
        nodes_0()
        edges_1a()
        edges_1b()
        nodes_1()
        edges_2a()
        segment_max()
        weigh_edges("l2_edges_b", agg2, H2, v_edge, C2 ** -0.5, None)
        nodes_2()
        edges_3a()
        weigh_edges("l3_edges_b", agg3, H3, p_edge, 1.0, gmax)
        nodes_3()


_WEIGHTS = ["L0_gnn_W", "L0_gnn_b", "L1_gnn_W1", "L1_gnn_b1", "L1_gnn_gamma", "L1_gnn_beta", "L1_gnn_W2", "L1_gnn_b2",
            "L2_gnn_Wq", "L2_gnn_bq", "L2_gnn_Wk", "L2_gnn_bk", "L2_gnn_Wv", "L2_gnn_bv", "L2_gnn_We", "L2_gnn_Wskip",
            "L2_gnn_bskip", "L2_gnn_g1", "L2_gnn_b1", "L2_gnn_g2", "L2_gnn_b2", "L2_gnn_Wf1", "L2_gnn_bf1",
            "L2_gnn_Wf2", "L2_gnn_bf2", "L3_gnn_W_proj", "L3_gnn_a_src", "L3_gnn_a_tgt", "L3_gnn_bias"]


def kernel(x, src, dst, edge_attr_2, edge_attr_64, **weights):
    import numpy as np
    import concourse.bacc as bacc
    from concourse.bass_utils import run_bass_kernel_spmd

    n_nodes, n_edges = np.shape(x)[0], np.shape(src)[0]
    pairs = -(-(max(n_nodes, n_edges) + 1) // (2 * GE))
    rows = 2 * GE * pairs
    tiles = rows // P

    def padded(a, fill):
        a = np.asarray(a)
        more = np.full((rows - a.shape[0],) + a.shape[1:], fill, a.dtype)
        return np.concatenate([a, more])

    def by_edge(a):
        return np.ascontiguousarray(np.swapaxes(a.reshape((tiles, P) + a.shape[1:]), 0, 1))

    src_p, dst_p = padded(src, rows - 1), padded(dst, rows - 1)
    edge = np.full((1,), -1, dst_p.dtype)
    arrays = {
        "in_x": padded(x, 0),
        "in_src": by_edge(src_p),
        "in_dst": by_edge(dst_p),
        "in_dst_line": np.concatenate([edge, dst_p, edge])[None],
        "in_ea2": np.ascontiguousarray(np.swapaxes(padded(edge_attr_2, 0).reshape(rows // GE, GE, 2), 1, 2)),
        "in_ea64": np.ascontiguousarray(np.swapaxes(padded(edge_attr_64, 0).reshape(rows // GE, GE, ED), 1, 2)),
    }
    for name in _WEIGHTS:
        arrays[f"in_{name}"] = np.ascontiguousarray(np.asarray(weights[name]))
    nc = bacc.Bacc("TRN2", target_bir_lowering=False, num_devices=1)
    aps = {name: nc.dram_tensor(name, a.shape, mybir.dt.from_np(a.dtype), kind="ExternalInput").ap()
           for name, a in arrays.items()}
    out = nc.dram_tensor("out_rows", (rows, D), F32, kind="ExternalOutput").ap()
    gnn(nc, *(aps[f"in_{n}"] for n in ("x", "src", "dst", "dst_line", "ea2", "ea64")),
        {n: aps[f"in_{n}"] for n in _WEIGHTS}, out, n_edges)
    result = run_bass_kernel_spmd(nc, [arrays], core_ids=[0])
    return result.results[0]["out_rows"][:n_nodes]
```
